# Optimizing a Trainium2 kernel written in Bass

```python
import numpy as np
import jax
import jax.numpy as jnp

def _softmax(x, axis=-1):
    return jax.nn.softmax(x, axis=axis)
def _gelu(x):
    return jax.nn.gelu(x, approximate=True)
def _silu(x):
    return jax.nn.silu(x)
def _sigmoid(x):
    return jax.nn.sigmoid(x)
def _layernorm(x, axis=-1, eps=1e-5):
    m = jnp.mean(x, axis=axis, keepdims=True)
    v = jnp.var(x, axis=axis, keepdims=True)
    return (x - m) / jnp.sqrt(v + eps)
def _scatter_add(tgt, idx, src, axis=0):
    return tgt.at[idx].add(src)
def _segment_sum(src, seg, n):
    return jax.ops.segment_sum(src, seg, n)

kernel_name = 'mk_metaformer_d2_conv_nhwc128_3f5a04'

def setup_inputs(seed: int = 0):
    np.random.seed(seed)
    _w = jnp.asarray
    def _rec_inputs():
        import jax
        import jax.numpy as jnp
        _gk = jax.random.key(seed)
        x = -0.0003957 + 1 * jax.random.normal(jax.random.fold_in(_gk, 1), (32, 56, 56, 128), jnp.float32)
        return x
    x = _rec_inputs()
    def _L0_conv_setup():
        import jax, jax.numpy as jnp
        import numpy as np
        WS = 7
        SS = 3
        NH = 4

        def build_rel_index(ws):
            coords = np.stack(np.meshgrid(np.arange(ws), np.arange(ws), indexing='ij'))
            flat = coords.reshape(2, -1)
            rel = flat[:, :, None] - flat[:, None, :]
            rel = rel.transpose(1, 2, 0).copy()
            rel[:, :, 0] += ws - 1
            rel[:, :, 1] += ws - 1
            rel[:, :, 0] *= 2 * ws - 1
            return rel.sum(-1)

        def build_shift_mask(Hp, Wp, ws, ss):
            img = np.zeros((Hp, Wp))
            cnt = 0
            for hs in (slice(0, -ws), slice(-ws, -ss), slice(-ss, None)):
                for wsl in (slice(0, -ws), slice(-ws, -ss), slice(-ss, None)):
                    img[hs, wsl] = cnt
                    cnt += 1
            mw = img.reshape(Hp // ws, ws, Wp // ws, ws).transpose(0, 2, 1, 3).reshape(-1, ws * ws)
            diff = mw[:, None, :] - mw[:, :, None]
            return jnp.asarray(np.where(diff != 0, -100.0, 0.0).astype(np.float32))
        key = jax.random.key(seed)
        k1, k2, k3, k4 = jax.random.split(key, 4)
        B, H, W, C = (32, 56, 56, 128)
        x = jax.random.normal(k1, (B, H, W, C), dtype=jnp.float32)
        rpb_table = jax.random.normal(k2, ((2 * WS - 1) * (2 * WS - 1), NH), dtype=jnp.float32) * 0.02
        w_qkv = jax.random.normal(k3, (3 * C, C), dtype=jnp.float32) * 0.02
        w_proj = jax.random.normal(k4, (C, C), dtype=jnp.float32) * 0.02
        b_proj = jnp.zeros((C,), dtype=jnp.float32)
        return {'x': x, 'rpb_table': rpb_table, 'w_qkv': w_qkv, 'w_proj': w_proj, 'b_proj': b_proj}
    _L0_conv_all = _L0_conv_setup()
    _L0_conv_in = {k: v for k, v in _L0_conv_all.items() if k in ('rpb_table', 'w_qkv', 'w_proj', 'b_proj', )}
    del _L0_conv_all

    def _L0_ffn_setup():
        import jax, jax.numpy as jnp
        import numpy as np
        B, N, D, C, E, K = (8, 8192, 128, 128, 8, 2)
        key = jax.random.key(seed)
        k0, k1, k2 = jax.random.split(key, 3)
        x = jax.random.normal(k0, (B, N, D), dtype=jnp.float32)
        router_w = jax.random.normal(k1, (D, E), dtype=jnp.float32) * 0.05
        router_b = jnp.zeros((E,), dtype=jnp.float32)
        expert_w = jax.random.normal(k2, (E, D, C), dtype=jnp.float32) * (1.0 / np.sqrt(D))
        expert_b = jnp.zeros((E, C), dtype=jnp.float32)
        return {'x': x, 'router_w': router_w, 'router_b': router_b, 'expert_w': expert_w, 'expert_b': expert_b}
    _L0_ffn_all = _L0_ffn_setup()
    _L0_ffn_in = {k: v for k, v in _L0_ffn_all.items() if k in ('router_w', 'router_b', 'expert_w', 'expert_b', )}
    del _L0_ffn_all

    def _L1_conv_setup():
        import jax, jax.numpy as jnp
        import numpy as np
        B, H, W, C = (16, 96, 96, 128)
        FOCAL_LEVEL = 3
        FOCAL_WINDOW = 3
        FOCAL_FACTOR = 2
        LN_EPS = 0.001

        def dwconv_same(x, k):
            return jax.lax.conv_general_dilated(x, k, window_strides=(1, 1), padding='SAME', dimension_numbers=('NHWC', 'HWIO', 'NHWC'), feature_group_count=x.shape[-1])
        key = jax.random.key(seed)
        ks = jax.random.split(key, 12)
        s = 0.02
        out_f = 2 * C + (FOCAL_LEVEL + 1)
        inp = {'x': jax.random.normal(ks[0], (B, H, W, C), dtype=jnp.float32), 'Wf': jax.random.normal(ks[1], (C, out_f), dtype=jnp.float32) * s, 'bf': jnp.zeros((out_f,), dtype=jnp.float32), 'Wh': jax.random.normal(ks[2], (C, C), dtype=jnp.float32) * s, 'bh': jnp.zeros((C,), dtype=jnp.float32), 'gamma': jnp.ones((C,), dtype=jnp.float32), 'beta': jnp.zeros((C,), dtype=jnp.float32), 'Wp': jax.random.normal(ks[3], (C, C), dtype=jnp.float32) * s, 'bp': jnp.zeros((C,), dtype=jnp.float32)}
        for l in range(FOCAL_LEVEL):
            kk = FOCAL_FACTOR * l + FOCAL_WINDOW
            inp[f'k{l}'] = jax.random.normal(ks[4 + l], (kk, kk, 1, C), dtype=jnp.float32) * s
        return inp
    _L1_conv_all = _L1_conv_setup()
    _L1_conv_in = {k: v for k, v in _L1_conv_all.items() if k in ('Wf', 'bf', 'k0', 'k1', 'k2', 'Wh', 'bh', 'gamma', 'beta', 'Wp', 'bp', )}
    del _L1_conv_all

    def _L1_ffn_setup():
        import jax, jax.numpy as jnp
        import numpy as np
        BN_EPS = 1e-05
        key = jax.random.key(seed)
        k1, k2, k3 = jax.random.split(key, 3)
        B, T, I, H = (64, 2048, 128, 128)
        x = jax.random.normal(k1, (B, T, I), dtype=jnp.float32)
        W = jax.random.normal(k2, (H, I), dtype=jnp.float32) * (1.0 / np.sqrt(I))
        V = jnp.linalg.qr(jax.random.normal(k3, (H, H), dtype=jnp.float32))[0]
        gamma = jnp.ones((H,), dtype=jnp.float32)
        beta = jnp.zeros((H,), dtype=jnp.float32)
        return {'x': x, 'W': W, 'V': V, 'gamma': gamma, 'beta': beta}
    _L1_ffn_all = _L1_ffn_setup()
    _L1_ffn_in = {k: v for k, v in _L1_ffn_all.items() if k in ('W', 'V', 'gamma', 'beta', )}
    del _L1_ffn_all

    return {
        "x": x,
        "L0_conv_rpb_table": _L0_conv_in["rpb_table"],
        "L0_conv_w_qkv": _L0_conv_in["w_qkv"],
        "L0_conv_w_proj": _L0_conv_in["w_proj"],
        "L0_conv_b_proj": _L0_conv_in["b_proj"],
        "L0_ffn_router_w": _L0_ffn_in["router_w"],
        "L0_ffn_router_b": _L0_ffn_in["router_b"],
        "L0_ffn_expert_w": _L0_ffn_in["expert_w"],
        "L0_ffn_expert_b": _L0_ffn_in["expert_b"],
        "L1_conv_Wf": _L1_conv_in["Wf"],
        "L1_conv_bf": _L1_conv_in["bf"],
        "L1_conv_k0": _L1_conv_in["k0"],
        "L1_conv_k1": _L1_conv_in["k1"],
        "L1_conv_k2": _L1_conv_in["k2"],
        "L1_conv_Wh": _L1_conv_in["Wh"],
        "L1_conv_bh": _L1_conv_in["bh"],
        "L1_conv_gamma": _L1_conv_in["gamma"],
        "L1_conv_beta": _L1_conv_in["beta"],
        "L1_conv_Wp": _L1_conv_in["Wp"],
        "L1_conv_bp": _L1_conv_in["bp"],
        "L1_ffn_W": _L1_ffn_in["W"],
        "L1_ffn_V": _L1_ffn_in["V"],
        "L1_ffn_gamma": _L1_ffn_in["gamma"],
        "L1_ffn_beta": _L1_ffn_in["beta"],
    }

def reference(x, L0_conv_rpb_table, L0_conv_w_qkv, L0_conv_w_proj, L0_conv_b_proj, L0_ffn_router_w, L0_ffn_router_b, L0_ffn_expert_w, L0_ffn_expert_b, L1_conv_Wf, L1_conv_bf, L1_conv_k0, L1_conv_k1, L1_conv_k2, L1_conv_Wh, L1_conv_bh, L1_conv_gamma, L1_conv_beta, L1_conv_Wp, L1_conv_bp, L1_ffn_W, L1_ffn_V, L1_ffn_gamma, L1_ffn_beta):
    import jax
    import jax.numpy as jnp
    def _L0_conv_ref(x, rpb_table, w_qkv, w_proj, b_proj):
        import jax, jax.numpy as jnp
        import numpy as np
        WS = 7
        SS = 3
        NH = 4

        def build_rel_index(ws):
            coords = np.stack(np.meshgrid(np.arange(ws), np.arange(ws), indexing='ij'))
            flat = coords.reshape(2, -1)
            rel = flat[:, :, None] - flat[:, None, :]
            rel = rel.transpose(1, 2, 0).copy()
            rel[:, :, 0] += ws - 1
            rel[:, :, 1] += ws - 1
            rel[:, :, 0] *= 2 * ws - 1
            return rel.sum(-1)

        def build_shift_mask(Hp, Wp, ws, ss):
            img = np.zeros((Hp, Wp))
            cnt = 0
            for hs in (slice(0, -ws), slice(-ws, -ss), slice(-ss, None)):
                for wsl in (slice(0, -ws), slice(-ws, -ss), slice(-ss, None)):
                    img[hs, wsl] = cnt
                    cnt += 1
            mw = img.reshape(Hp // ws, ws, Wp // ws, ws).transpose(0, 2, 1, 3).reshape(-1, ws * ws)
            diff = mw[:, None, :] - mw[:, :, None]
            return jnp.asarray(np.where(diff != 0, -100.0, 0.0).astype(np.float32))
        B, H, W, C = x.shape
        hd = C // NH
        scale = hd ** (-0.5)
        pad_b = -H % WS
        pad_r = -W % WS
        x = jnp.pad(x, ((0, 0), (0, pad_b), (0, pad_r), (0, 0)))
        Hp, Wp = (H + pad_b, W + pad_r)
        xs = jnp.roll(x, (-SS, -SS), axis=(1, 2))
        nWh, nWw = (Hp // WS, Wp // WS)
        N = WS * WS
        nW = nWh * nWw
        win = xs.reshape(B, nWh, WS, nWw, WS, C).transpose(0, 1, 3, 2, 4, 5).reshape(-1, N, C)
        qkv = (win @ w_qkv.T).reshape(-1, N, 3, NH, hd)
        q = qkv[:, :, 0].transpose(0, 2, 1, 3) * scale
        k = qkv[:, :, 1].transpose(0, 2, 1, 3)
        v = qkv[:, :, 2].transpose(0, 2, 1, 3)
        attn = jnp.einsum('bhid,bhjd->bhij', q, k)
        rel_idx = build_rel_index(WS)
        bias = rpb_table[rel_idx.reshape(-1)].reshape(N, N, NH).transpose(2, 0, 1)
        attn = attn + bias[None]
        mask = build_shift_mask(Hp, Wp, WS, SS)
        attn = attn.reshape(B, nW, NH, N, N) + mask[None, :, None]
        attn = jax.nn.softmax(attn.reshape(-1, NH, N, N), axis=-1)
        out = jnp.einsum('bhij,bhjd->bihd', attn, v).reshape(-1, N, C)
        out = out @ w_proj.T + b_proj
        out = out.reshape(B, nWh, nWw, WS, WS, C).transpose(0, 1, 3, 2, 4, 5).reshape(B, Hp, Wp, C)
        out = jnp.roll(out, (SS, SS), axis=(1, 2))
        return out[:, :H, :W, :]

    def _L0_ffn_ref(x, router_w, router_b, expert_w, expert_b):
        import jax, jax.numpy as jnp
        import numpy as np
        B, N, D, C, E, K = (8, 8192, 128, 128, 8, 2)
        router_probs = jax.nn.softmax(x @ router_w + router_b, axis=-1)
        top_p, top_i = jax.lax.top_k(router_probs, K)
        top_p = top_p / jnp.sum(top_p, axis=-1, keepdims=True)
        expert_out = jnp.einsum('bnd,edc->bnec', x, expert_w) + expert_b
        gathered = jnp.take_along_axis(expert_out, top_i[..., None], axis=2)
        return jnp.einsum('bnk,bnkc->bnc', top_p, gathered)

    def _L1_conv_ref(x, Wf, bf, k0, k1, k2, Wh, bh, gamma, beta, Wp, bp):
        import jax, jax.numpy as jnp
        import numpy as np
        B, H, W, C = (16, 96, 96, 128)
        FOCAL_LEVEL = 3
        FOCAL_WINDOW = 3
        FOCAL_FACTOR = 2
        LN_EPS = 0.001

        def dwconv_same(x, k):
            return jax.lax.conv_general_dilated(x, k, window_strides=(1, 1), padding='SAME', dimension_numbers=('NHWC', 'HWIO', 'NHWC'), feature_group_count=x.shape[-1])
        gelu = lambda t: jax.nn.gelu(t, approximate=False)
        y = jnp.einsum('bhwc,cd->bhwd', x, Wf) + bf
        q = y[..., :C]
        ctx = y[..., C:2 * C]
        gates = y[..., 2 * C:]
        ctx_all = jnp.zeros_like(ctx)
        for l, k in enumerate((k0, k1, k2)):
            ctx = gelu(dwconv_same(ctx, k))
            ctx_all = ctx_all + ctx * gates[..., l:l + 1]
        ctx_global = gelu(jnp.mean(ctx, axis=(1, 2), keepdims=True))
        ctx_all = ctx_all + ctx_global * gates[..., FOCAL_LEVEL:]
        modulator = jnp.einsum('bhwc,cd->bhwd', ctx_all, Wh) + bh
        x_out = q * modulator
        mu = jnp.mean(x_out, axis=-1, keepdims=True)
        var = jnp.mean(jnp.square(x_out - mu), axis=-1, keepdims=True)
        x_out = (x_out - mu) * jax.lax.rsqrt(var + LN_EPS) * gamma + beta
        x_out = jnp.einsum('bhwc,cd->bhwd', x_out, Wp) + bp
        return x_out

    def _L1_ffn_ref(x, W, V, gamma, beta):
        import jax, jax.numpy as jnp
        import numpy as np
        BN_EPS = 1e-05
        B, T, H = (x.shape[0], x.shape[1], W.shape[0])
        Wx = jnp.einsum('bti,hi->bth', x, W)
        flat = Wx.reshape(B * T, H)
        mean = jnp.mean(flat, axis=0)
        var = jnp.var(flat, axis=0)
        Wx = ((flat - mean) * jax.lax.rsqrt(var + BN_EPS) * gamma + beta).reshape(B, T, H)
        Vt = V.T

        def step(yt, wx_t):
            yt = jax.nn.sigmoid(wx_t + yt @ Vt)
            return (yt, yt)
        y0 = jnp.zeros((B, H), dtype=Wx.dtype)
        _, ys = jax.lax.scan(step, y0, jnp.swapaxes(Wx, 0, 1))
        return jnp.swapaxes(ys, 0, 1)

    def _gn(v, G=32, eps=1e-5):
        B_, H_, W_, C_ = v.shape
        g = v.reshape(B_, H_, W_, G, C_ // G)
        m = jnp.mean(g, axis=(1, 2, 4), keepdims=True)
        s = jnp.var(g, axis=(1, 2, 4), keepdims=True)
        return ((g - m) / jnp.sqrt(s + eps)).reshape(v.shape)

    def _ln_c(v, eps=1e-6):
        m = jnp.mean(v, axis=-1, keepdims=True)
        s = jnp.var(v, axis=-1, keepdims=True)
        return (v - m) / jnp.sqrt(s + eps)

    def _ln_t(v, eps=1e-5):
        m = jnp.mean(v, axis=-1, keepdims=True)
        s = jnp.var(v, axis=-1, keepdims=True)
        return (v - m) / jnp.sqrt(s + eps)

    def _to_tokens(v):
        B_, H_, W_, C_ = v.shape
        return v.reshape(B_, H_ * W_, C_)
    def _from_tokens(t, like):
        return t.reshape(like.shape)

    x = x + _L0_conv_ref(_ln_c(x), L0_conv_rpb_table, L0_conv_w_qkv, L0_conv_w_proj, L0_conv_b_proj)
    t = _to_tokens(x)
    t = t + _L0_ffn_ref(_ln_t(t), L0_ffn_router_w, L0_ffn_router_b, L0_ffn_expert_w, L0_ffn_expert_b)
    x = _from_tokens(t, x)
    x = x + _L1_conv_ref(_ln_c(x), L1_conv_Wf, L1_conv_bf, L1_conv_k0, L1_conv_k1, L1_conv_k2, L1_conv_Wh, L1_conv_bh, L1_conv_gamma, L1_conv_beta, L1_conv_Wp, L1_conv_bp)
    t = _to_tokens(x)
    t = t + _L1_ffn_ref(_ln_t(t), L1_ffn_W, L1_ffn_V, L1_ffn_gamma, L1_ffn_beta)
    x = _from_tokens(t, x)
    return x


_drawn_inputs = setup_inputs


def setup_inputs(seed=0):
    import zlib

    import numpy as np

    out = dict(_drawn_inputs(seed))
    spreads = {'L0_conv_b_proj': (0.0, 0.1),
     'L0_ffn_router_b': (0.0, 0.1),
     'L0_ffn_expert_b': (0.0, 0.1),
     'L1_conv_bf': (0.0, 0.1),
     'L1_conv_bh': (0.0, 0.1),
     'L1_conv_gamma': (1.0, 0.6),
     'L1_conv_beta': (0.0, 0.476),
     'L1_conv_bp': (0.0, 0.1),
     'L1_ffn_gamma': (1.0, 0.6),
     'L1_ffn_beta': (0.0, 0.537)}
    factors = {'L0_conv_rpb_table': 29.241,
     'L1_conv_k0': 8.0,
     'L1_conv_k1': 30.666,
     'L1_conv_k2': 64.0,
     'L1_conv_Wh': 8.0}
    for name, (base, spread) in spreads.items():
        noise = np.random.default_rng([zlib.crc32(name.encode()), seed]).standard_normal(out[name].shape)
        drawn = base * np.exp(spread * noise) if base else spread * noise
        out[name] = jnp.asarray(drawn.astype(out[name].dtype))
    for name, factor in factors.items():
        out[name] = (out[name] * factor).astype(out[name].dtype)
    return out
```

```python
from contextlib import ExitStack

import concourse.bass as bass
from concourse import mybir

F32 = mybir.dt.float32
ALU = mybir.AluOpType
ACT = mybir.ActivationFunctionType
AX = mybir.AxisListType

P = 128
C = 128
IMG = 56
PIX = IMG * IMG
WS = 7
SHIFT = 3
WTOK = WS * WS
HEADS = 4
HD = C // HEADS
EXPERTS = 8
TAPS = (3, 5, 7)
BANK = 512


MANY = 1 << 20


class Step:

    def __init__(self, loop, unroll, off):
        self.loop, self.unroll, self.off = loop, unroll, off
        self.is_static = isinstance(loop, int)

    def __add__(self, k):
        return Step(self.loop, self.unroll, self.off + k)

    def __sub__(self, k):
        return self + -k

    def val(self, scale=1, plus=0):
        return self.loop * (self.unroll * scale) + (self.off * scale + plus)

    def slot(self, n):
        assert self.unroll % n == 0
        return self.off % n

    def turn(self, n, scale=1, plus=0):
        return self.loop * (self.unroll // n * scale) + (self.off // n * scale + plus)


def run_steps(eng, count, unroll, step, ahead=3):
    rounds = (count - 1 - ahead) // unroll
    if rounds < 3:
        for n in range(count):
            step(Step(0, unroll, n), n, n - count)
        return
    for n in range(unroll):
        step(Step(0, unroll, n), n, n - count)
    with eng.Fori(1, rounds) as it:
        for u in range(unroll):
            step(Step(it, unroll, u), MANY, -MANY)
    for n in range(rounds * unroll, count):
        step(Step(0, unroll, n), n, n - count)


def hold(eng, sem, value, ticks):
    eng.wait_ge(sem, value)
    eng.sem_inc(ticks, 1)


class Stage:

    def __init__(self, nc, name):
        self.nc, self.name, self.ctx, self.used = nc, name, ExitStack(), []

    def sb(self, name, shape):
        return self.ctx.enter_context(self.nc.sbuf_tensor(f"{self.name}_{name}", shape, F32))

    def ps(self, name, shape):
        return self.ctx.enter_context(self.nc.psum_tensor(f"{self.name}_{name}", shape, F32))

    def sem(self, name):
        self.used.append(self.ctx.enter_context(self.nc.semaphore(f"{self.name}_{name}")))
        return self.used[-1]

    def sems(self, name, n):
        return [self.sem(f"{name}{i}") for i in range(n)]

    def clear(self):
        with self.nc.Block() as block:
            @block.gpsimd
            def _(pool):
                for sem in self.used:
                    pool.sem_clear(sem)

    def block(self):
        self.ctx.callback(self.clear)
        return self.ctx.enter_context(self.nc.Block())


def dram(ap, offset, dims):
    return bass.AP(ap.tensor, offset, [list(d) for d in dims])


def row_to_all(ap, n, offset=0):
    return dram(ap, offset, [(0, P), (1, n)])


def attention_stage(nc, B, x_win, w_qkv_t, w_proj_t, b_proj, rpb_rev, shift_mask, ident, x1):
    N = B * 8
    PAIRS, W = 4, 8
    SCALE = float(HD) ** -0.5
    EPS = 1e-6
    U = 8
    S = Stage(nc, "att")
    with S.ctx:
        idn = S.sb("idn", [P, P])
        wqkv = S.sb("wqkv", [C, 3 * C])
        wproj = S.sb("wproj", [C, C])
        bproj = S.sb("bproj", [P, C])
        halfneg = S.sb("halfneg", [P, PAIRS])
        mask = S.sb("mask", [P, 2, PAIRS * WTOK])
        bias = S.sb("bias", [P, 2, HEADS, PAIRS * WTOK])
        relb = S.sb("relb", [P, HEADS, WTOK])
        xin = S.sb("xin", [P, 4, PAIRS, C])
        stat = S.sb("stat", [P, 2, PAIRS, 6])
        mv = S.sb("mv", [P, 2, PAIRS, 2])
        rstd = S.sb("rstd", [P, 2, PAIRS])
        xn = S.sb("xn", [P, 2, PAIRS, C])
        xnT = S.sb("xnT", [C, W * WTOK])
        qT = S.sb("qT", [C, W * WTOK])
        kT = S.sb("kT", [C, W * WTOK])
        vv = S.sb("vv", [WTOK, 2, W, C])
        sc = S.sb("sc", [P, HEADS * PAIRS, WTOK])
        pr = S.sb("pr", [P, HEADS * PAIRS, WTOK])
        mx = S.sb("mx", [P, HEADS * PAIRS])
        sm = S.sb("sm", [P, HEADS * PAIRS])
        rs = S.sb("rs", [P, HEADS * PAIRS])
        prT = S.sb("prT", [WTOK, PAIRS, HEADS, P])
        oT = S.sb("oT", [C, W, 64])
        x1s = S.sb("x1s", [P, 2, PAIRS, C])

        rel_dram = nc.dram_tensor("rel_dram", (HEADS, WTOK, WTOK), F32).ap()

        psc = S.ps("psc", [P, HEADS, BANK])
        pf = S.ps("pf", [P, 2, BANK])
        pb = S.ps("pb", [P, 2, BANK])

        const_in = S.sem("const_in")
        ticks = S.sem("ticks")
        rel_in, rel_spread = S.sem("rel_in"), S.sem("rel_spread")
        zeroed_v = S.sem("zeroed_v")
        zeroed_p = S.sem("zeroed_p")
        rel_zero = S.sem("rel_zero")
        bias_built = S.sem("bias_built")
        x_in = S.sems("x_in", 4)
        stats_part = S.sem("stats_part")
        stats = S.sem("stats")
        eps_added = S.sem("eps_added")
        rstd_done = S.sem("rstd_done")
        centred = S.sem("centred")
        normed = S.sem("normed")
        bproj_added = S.sem("bproj_added")
        f0_full, f1_full = S.sem("f0_full"), S.sem("f1_full")
        xT_out, q_out, k_out, v0_out, v1_out = (S.sem(f"{n}_out") for n in ("xT", "q", "k", "v0", "v1"))
        scored = S.sem("scored")
        biased = S.sem("biased")
        maxed = S.sem("maxed")
        shifted = S.sem("shifted")
        exped = S.sem("exped")
        summed = S.sem("summed")
        inverted = S.sem("inverted")
        probs = S.sem("probs")
        turned = S.sems("turned", PAIRS)
        prT_out = S.sems("prT_out", PAIRS)
        attended = S.sem("attended")
        oT_out = S.sem("oT_out")
        projected = S.sem("projected")
        x1_ready = S.sem("x1_ready")
        x1_out = S.sems("x1_out", 2)
        block = S.block()

        @block.sync
        def _(sp):
            for dst, src in ((idn[:], ident), (wqkv[:], w_qkv_t), (wproj[:], w_proj_t),
                             (bproj[:], row_to_all(b_proj, C)), (mask[:], shift_mask)):
                sp.dma_start(dst, src).then_inc(const_in, 16)
            SIDE = 2 * WS - 1
            for h in range(HEADS):
                for r1 in range(WS):
                    off = h * SIDE * SIDE + (WS - 1 - r1) * SIDE + WS - 1
                    sp.dma_start(dram(rel_dram, (h * WTOK + r1 * WS) * WTOK, [(WS, WS), (WTOK, WS), (1, WS)]),
                                 dram(rpb_rev, off, [(SIDE, WS), (-1, WS), (1, WS)])).then_inc(rel_spread, 16)
            sp.wait_ge(rel_spread, 16 * HEADS * WS)
            sp.wait_ge(rel_zero, 1)
            for base in (0, 64):
                sp.dma_start(relb[base:base + WTOK, :, :],
                             dram(rel_dram, 0, [(WTOK, WTOK), (WTOK * WTOK, HEADS), (1, WTOK)])).then_inc(rel_in, 16)

            def load(n):
                s = n.slot(4)
                for odd in range(2):
                    src = dram(x_win, n.val(W * WTOK * C, odd * WTOK * C),
                               [(C, WTOK), (2 * WTOK * C, PAIRS), (1, C)])
                    sp.dma_start(xin[odd * 64:odd * 64 + WTOK, s, :, :], src).then_inc(x_in[s], 16)

            def step(n, first, last):
                if first == 0:
                    for k in range(3):
                        if k < N:
                            load(n + k)
                if last < -3:
                    if first >= 1:
                        hold(sp, x1_ready, n.val(), ticks)
                    load(n + 3)
                hold(sp, x1_ready, n.val(1, 1), ticks)
                for pair in range(PAIRS):
                    for odd in range(2):
                        off = n.val(WS * IMG * C, (2 * pair + odd) * WS * C)
                        sp.dma_start(dram(x1, off, [(IMG * C, WS), (C, WS), (1, C)]),
                                     x1s[odd * 64:odd * 64 + WTOK, n.slot(2), pair, :]).then_inc(x1_out[n.slot(2)], 16)

            sp.wait_ge(zeroed_p, 4)
            run_steps(sp, N, U, step)
            for s in range(2):
                sp.wait_ge(x1_out[s], 16 * W * ((N + 1 - s) // 2))

        @block.gpsimd
        def _(pool):
            for s in range(4):
                pool.memset(xin[:, s, :, :], 0.0).then_inc(zeroed_p, 1)
            pool.memset(halfneg[:], -0.5).then_inc(zeroed_p, 1)
            pool.memset(oT[:], 0.0).then_inc(zeroed_p, 1)
            pool.wait_ge(zeroed_p, 6)
            pool.wait_ge(const_in, 80)

            def norm(n):
                a, s = n.slot(2), n.slot(4)
                hold(pool, stats, n.val(1, 1), ticks)
                pool.tensor_scalar(rstd[:, a, :], mv[:, a, :, 1], EPS, None, ALU.add).then_inc(eps_added, 1)
                pool.wait_ge(eps_added, n.val(1, 1))
                pool.tensor_tensor(rstd[:, a, :], rstd[:, a, :], halfneg[:], ALU.pow).then_inc(rstd_done, 1)
                pool.wait_ge(rstd_done, n.val(1, 1))
                pool.sem_inc(ticks, 1)
                for t in range(PAIRS):
                    ins = pool.tensor_scalar(xn[:, a, t, :], xin[:, s, t, :], mv[:, a, t, 0:1],
                                             rstd[:, a, t:t + 1], ALU.subtract, ALU.mult)
                ins.then_inc(normed, 1)
                pool.wait_ge(normed, n.val(1, 1))
                pool.tensor_tensor(xin[:, s, :, :], xin[:, s, :, :],
                                   bproj[:].unsqueeze(1).to_broadcast([P, PAIRS, C]), ALU.add).then_inc(bproj_added, 1)

            def step(n, first, last):
                if first == 0:
                    norm(n)
                    if N > 1:
                        norm(n + 1)
                if last < -2:
                    pool.wait_ge(xT_out, n.val(1, 1))
                    norm(n + 2)

            run_steps(pool, N, U, step)

        @block.scalar
        def _(act):
            def copy(out, in_):
                return act.activation(out, in_, ACT.Copy)

            def front(n):
                act.wait_ge(f0_full, n.val(3, 1))
                copy(xnT[:].rearrange("c (w t) -> c w t", t=WTOK),
                     pf[:, 0, :].rearrange("c (w t) -> c w t", t=64)[:, :, 0:WTOK]).then_inc(xT_out, 1)
                act.wait_ge(f1_full, n.val(2, 1))
                act.activation(qT[:], pf[:, 1, 0:W * WTOK], ACT.Copy, scale=SCALE).then_inc(q_out, 1)
                act.wait_ge(f0_full, n.val(3, 2))
                copy(kT[:], pf[:, 0, 0:W * WTOK]).then_inc(k_out, 1)
                v = vv[:, n.slot(2), :, :].rearrange("t w c -> t (w c)")
                act.wait_ge(f1_full, n.val(2, 2))
                copy(v[:, 0:BANK], pf[0:WTOK, 1, :]).then_inc(v0_out, 1)
                act.wait_ge(f0_full, n.val(3, 3))
                copy(v[:, BANK:2 * BANK], pf[0:WTOK, 0, :]).then_inc(v1_out, 1)

            def exp(n):
                act.wait_ge(shifted, n.val(1, 1))
                act.activation(pr[:], sc[:], ACT.Exp).then_inc(exped, 1)

            def back(n):
                for pair in (0, 2):
                    act.wait_ge(turned[pair], n.val(1, 1))
                    copy(prT[:, pair, :, :].rearrange("t h i -> t (h i)"), pb[0:WTOK, 0, :]).then_inc(prT_out[pair], 1)
                act.wait_ge(attended, n.val(1, 1))
                copy(oT[:, :, 0:WTOK], pb[:, 0, 0:W * WTOK].rearrange("c (w t) -> c w t", t=WTOK)).then_inc(oT_out, 1)

            act.wait_ge(zeroed_p, 6)

            def step(n, first, last):
                if first == 0:
                    front(n)
                    exp(n)
                if last < -1:
                    front(n + 1)
                back(n)
                if last < -1:
                    exp(n + 1)

            run_steps(act, N, U, step)

        @block.vector
        def _(dve):
            dve.memset(relb[:], 0.0).then_inc(rel_zero, 1)
            dve.memset(psc[:], 0.0).then_inc(zeroed_v, 1)
            dve.wait_ge(zeroed_p, 6)
            dve.wait_ge(const_in, 80)
            dve.wait_ge(rel_in, 32)
            for kind in range(2):
                for h in range(HEADS):
                    dve.tensor_tensor(bias[:, kind, h, :].rearrange("p (q j) -> p q j", j=WTOK),
                                      mask[:, kind, :].rearrange("p (q j) -> p q j", j=WTOK),
                                      relb[:, h, :].unsqueeze(1).to_broadcast([P, PAIRS, WTOK]),
                                      ALU.add).then_inc(bias_built, 1)

            def layer_stats(n):
                a, s = n.slot(2), n.slot(4)
                dve.wait_ge(x_in[s], n.turn(4, 32, 32))
                for t in range(PAIRS):
                    dve.bn_stats(stat[:, a, t, :], xin[:, s, t, :]).then_inc(stats_part, 1)
                hold(dve, stats_part, n.val(PAIRS, PAIRS), ticks)
                for t in range(PAIRS):
                    ins = dve.bn_aggr(mv[:, a, t, :], stat[:, a, t, :])
                ins.then_inc(stats, 1)

            def softmax_front(n, kind):
                dve.wait_ge(scored, n.val(1, 1))
                dve.tensor_tensor(sc[:].rearrange("p (h q) j -> p h (q j)", h=HEADS),
                                  psc[:, :, 0:PAIRS * WTOK], bias[:, kind, :, :], ALU.add).then_inc(biased, 1)
                dve.wait_ge(biased, n.val(1, 1))
                dve.tensor_reduce(mx[:], sc[:], AX.X, ALU.max).then_inc(maxed, 1)
                dve.wait_ge(maxed, n.val(1, 1))
                dve.tensor_tensor(sc[:], sc[:], mx[:].unsqueeze(2).to_broadcast([P, HEADS * PAIRS, WTOK]),
                                  ALU.subtract).then_inc(shifted, 1)

            def softmax_back(n):
                dve.wait_ge(exped, n.val(1, 1))
                dve.tensor_reduce(sm[:], pr[:], AX.X, ALU.add).then_inc(summed, 1)
                dve.wait_ge(summed, n.val(1, 1))
                dve.reciprocal(rs[:], sm[:]).then_inc(inverted, 1)
                dve.wait_ge(inverted, n.val(1, 1))
                dve.tensor_tensor(pr[:], pr[:], rs[:].unsqueeze(2).to_broadcast([P, HEADS * PAIRS, WTOK]),
                                  ALU.mult).then_inc(probs, 1)

            def back(n):
                for pair in (1, 3):
                    dve.wait_ge(turned[pair], n.val(1, 1))
                    dve.tensor_copy(prT[:, pair, :, :].rearrange("t h i -> t (h i)"),
                                    pb[0:WTOK, 1, :]).then_inc(prT_out[pair], 1)

            def residual(n, first):
                dve.wait_ge(projected, n.val(1, 1))
                dve.wait_ge(bproj_added, n.val(1, 1))
                if first >= 2:
                    dve.wait_ge(x1_out[n.slot(2)], n.turn(2, 16 * W))
                dve.tensor_tensor(x1s[:, n.slot(2), :, :].rearrange("p q c -> p (q c)"), pb[:, 1, :],
                                  xin[:, n.slot(4), :, :].rearrange("p q c -> p (q c)"), ALU.add).then_inc(x1_ready, 1)

            dve.wait_ge(bias_built, 2 * HEADS)

            def step(n, first, last):
                kind = (n + 1).slot(8) == 7
                if first == 0:
                    layer_stats(n)
                    if N > 1:
                        layer_stats(n + 1)
                    softmax_front(n, 0)
                    softmax_back(n)
                if last < -2:
                    dve.wait_ge(normed, n.val(1, 1))
                    layer_stats(n + 2)
                back(n)
                if last < -1:
                    softmax_front(n + 1, int(kind))
                    softmax_back(n + 1)
                residual(n, first)

            run_steps(dve, N, U, step)

        @block.tensor
        def _(pe):
            pe.wait_ge(const_in, 80)
            pe.wait_ge(zeroed_v, 1)
            pe.wait_ge(zeroed_p, 6)

            def front(n, first):
                a = n.slot(2)
                pe.wait_ge(normed, n.val(1, 1))
                if first >= 1:
                    pe.wait_ge(v1_out, n.val())
                for t in range(PAIRS):
                    ins = pe.transpose(pf[:, 0, t * P:(t + 1) * P], xn[:, a, t, :], idn[:])
                ins.then_inc(f0_full, 1)
                pe.wait_ge(xT_out, n.val(1, 1))
                if first >= 1:
                    pe.wait_ge(v0_out, n.val())
                pe.matmul(pf[:, 1, 0:W * WTOK], wqkv[:, 0:C], xnT[:], start=True, stop=True).then_inc(f1_full, 1)
                pe.matmul(pf[:, 0, 0:W * WTOK], wqkv[:, C:2 * C], xnT[:], start=True, stop=True).then_inc(f0_full, 1)
                pe.wait_ge(q_out, n.val(1, 1))
                for half in range(2):
                    if half == 1:
                        pe.wait_ge(k_out, n.val(1, 1))
                    for w in range(PAIRS):
                        win = half * PAIRS + w
                        ins = pe.matmul(pf[0:WTOK, 1 - half, w * C:(w + 1) * C], xnT[:, win * WTOK:(win + 1) * WTOK],
                                        wqkv[:, 2 * C:3 * C], start=True, stop=True)
                    ins.then_inc(f0_full if half else f1_full, 1)
                if first >= 1:
                    pe.wait_ge(biased, n.val())
                for w in range(W):
                    p0, pair = (w % 2) * 64, w // 2
                    for h in range(HEADS):
                        ins = pe.matmul(psc[p0:p0 + WTOK, h, pair * WTOK:(pair + 1) * WTOK],
                                        qT[h * HD:(h + 1) * HD, w * WTOK:(w + 1) * WTOK],
                                        kT[h * HD:(h + 1) * HD, w * WTOK:(w + 1) * WTOK], start=True, stop=True)
                ins.then_inc(scored, 1)

            def back(n, first):
                hold(pe, probs, n.val(1, 1), ticks)
                for pair in range(PAIRS):
                    if pair == 1 and first >= 1:
                        hold(pe, x1_ready, n.val(), ticks)
                    if pair >= 2:
                        hold(pe, prT_out[pair - 2], n.val(1, 1), ticks)
                    for h in range(HEADS):
                        ins = pe.transpose(pb[0:WTOK, pair % 2, h * P:(h + 1) * P], pr[:, h * PAIRS + pair, :], idn[:])
                    ins.then_inc(turned[pair], 1)
                pe.wait_ge(v1_out, n.val(1, 1))
                for pair in range(PAIRS):
                    hold(pe, prT_out[(2, 3, 0, 1)[pair]], n.val(1, 1), ticks)
                for w in range(W):
                    pair, i0 = w // 2, (w % 2) * 64
                    for h in range(HEADS):
                        ins = pe.matmul(pb[h * HD:(h + 1) * HD, 0, w * WTOK:(w + 1) * WTOK],
                                        vv[:, n.slot(2), w, h * HD:(h + 1) * HD],
                                        prT[:, pair, h, i0:i0 + WTOK], start=True, stop=True)
                ins.then_inc(attended, 1)
                pe.wait_ge(oT_out, n.val(1, 1))
                for pair in range(PAIRS):
                    ins = pe.matmul(pb[:, 1, pair * C:(pair + 1) * C],
                                    oT[:, 2 * pair:2 * pair + 2, :].rearrange("c w t -> c (w t)"), wproj[:],
                                    start=True, stop=True)
                ins.then_inc(projected, 1)

            def step(n, first, last):
                if first == 0:
                    front(n, 0)
                if last < -1:
                    front(n + 1, 1)
                back(n, first)

            run_steps(pe, N, U, step)


def expert_stage(nc, B, x1, router_w, router_b, expert_w, expert_b, erank, ident, x2):
    T = 7
    GROUP = T * P
    N = B * PIX // GROUP
    EPS = 1e-5
    E = EXPERTS
    NOT_CHOSEN = -1e38
    U = 6
    S = Stage(nc, "moe")
    with S.ctx:
        idn = S.sb("idn", [P, P])
        wr = S.sb("wr", [C, E])
        br = S.sb("br", [P, E])
        we = S.sb("we", [C, E, C])
        be = S.sb("be", [E, C])
        rank = S.sb("rank", [P, E])
        halfneg = S.sb("halfneg", [P, T])
        xin = S.sb("xin", [P, 3, T, C])
        stat = S.sb("stat", [P, 2, T, 6])
        mv = S.sb("mv", [P, 2, T, 2])
        rstd = S.sb("rstd", [P, 2, T])
        xn = S.sb("xn", [P, 2, T, C])
        xnT = S.sb("xnT", [C, 2, T, P])
        logit = S.sb("logit", [P, T, E])
        rest = S.sb("rest", [P, T, E])
        hit = S.sb("hit", [P, 2, T, E])
        ranked = S.sb("ranked", [P, 2, T, E])
        one = S.sb("one", [P, 2, T, E])
        best = S.sb("best", [P, 2, T])
        top = S.sb("top", [P, 2, T])
        gap = S.sb("gap", [P, T])
        second = S.sb("second", [P, T])
        total = S.sb("total", [P, T])
        share = S.sb("share", [P, 2, T])
        part = S.sb("part", [P, 2, T, E])
        gate = S.sb("gate", [P, 2, T, E])
        gateT = S.sb("gateT", [E, T, P])
        acc = S.sb("acc", [P, 3, T, C])
        odd = S.sb("odd", [P, 2, C])

        px = S.ps("px", [P, 2, BANK])
        pr = S.ps("pr", [P, BANK])
        pe_out = S.ps("pe_out", [P, 2, 2, BANK])

        ticks = S.sem("ticks")
        const_in = S.sem("const_in")
        filled = S.sem("filled")
        x_in = S.sems("x_in", 3)
        stats_part, stats = S.sem("stats_part"), S.sem("stats")
        eps_added, rstd_done, normed = S.sem("eps_added"), S.sem("rstd_done"), S.sem("normed")
        turned, xT_out = S.sems("turned", 2), S.sems("xT_out", 2)
        logits_made = S.sem("logits_made")
        routing = S.sem("routing")
        gap_ready, second_ready = S.sem("gap_ready"), S.sem("second_ready")
        gates_ready = S.sem("gates_ready")
        gates_turned, gT_out = S.sems("gates_turned", 2), S.sems("gT_out", 2)
        bias_made, acc_begun = S.sems("bias_made", 2), S.sems("acc_begun", 2)
        expert_done = S.sem("expert_done")
        mixing, mixed = S.sem("mixing"), S.sem("mixed")
        x2_out = S.sems("x2_out", 3)
        block = S.block()
        HALVES = ((0, 4), (4, T))
        CONSTS = 16 * 6

        @block.sync
        def _(sp):
            for dst, src in ((idn[:], ident), (wr[:], router_w), (br[:], row_to_all(router_b, E)),
                             (we[:], dram(expert_w, 0, [(C, C), (C * C, E), (1, C)])),
                             (be[:], expert_b), (rank[:], erank)):
                sp.dma_start(dst, src).then_inc(const_in, 16)

            def load(n):
                sp.dma_start(xin[:, n.slot(3), :, :], dram(x1, n.val(GROUP * C), [(T * C, P), (1, T * C)]))\
                  .then_inc(x_in[n.slot(3)], 16)

            def step(n, first, last):
                if first == 0:
                    for k in range(min(3, N)):
                        load(n + k)
                elif last < -2:
                    hold(sp, acc_begun[1], n.val(), ticks)
                    load(n + 2)
                hold(sp, mixed, n.val(T, T), ticks)
                sp.dma_start(dram(x2, n.val(GROUP * C), [(T * C, P), (1, T * C)]), acc[:, n.slot(3), :, :])\
                  .then_inc(x2_out[n.slot(3)], 16)

            run_steps(sp, N, U, step)
            for s in range(3):
                sp.wait_ge(x2_out[s], 16 * ((N + 2 - s) // 3))

        @block.gpsimd
        def _(pool):
            pool.memset(halfneg[:], -0.5).then_inc(filled, 1)
            pool.wait_ge(filled, 1)

            def norm(n):
                a = n.slot(2)
                hold(pool, stats, n.val(1, 1), ticks)
                pool.tensor_scalar(rstd[:, a, :], mv[:, a, :, 1], EPS, None, ALU.add).then_inc(eps_added, 1)
                pool.wait_ge(eps_added, n.val(1, 1))
                pool.tensor_tensor(rstd[:, a, :], rstd[:, a, :], halfneg[:], ALU.pow).then_inc(rstd_done, 1)
                hold(pool, rstd_done, n.val(1, 1), ticks)
                for t in range(T):
                    ins = pool.tensor_scalar(xn[:, a, t, :], xin[:, n.slot(3), t, :], mv[:, a, t, 0:1],
                                             rstd[:, a, t:t + 1], ALU.subtract, ALU.mult)
                ins.then_inc(normed, 1)

            def step(n, first, last):
                if first == 0:
                    norm(n)
                    norm(n + 1)
                if last < -2:
                    pool.wait_ge(turned[1], n.val(1, 1))
                    norm(n + 2)

            run_steps(pool, N, U, step)

        @block.scalar
        def _(act):
            def front(n, first):
                if first >= 1:
                    act.wait_ge(mixed, n.val(T, -T))
                for b, (t0, t1) in enumerate(HALVES):
                    act.wait_ge(turned[b], n.val(1, 1))
                    act.activation(xnT[:, n.slot(2), t0:t1, :], px[:, b, 0:(t1 - t0) * P], ACT.Copy).then_inc(xT_out[b], 1)

            def gates(n):
                act.wait_ge(gap_ready, n.val(1, 1))
                act.activation(second[:], gap[:], ACT.Exp).then_inc(second_ready, 1)
                for b, (t0, t1) in enumerate(HALVES):
                    act.wait_ge(gates_turned[b], n.val(1, 1))
                    act.activation(gateT[:, t0:t1, :], px[0:E, b, 0:(t1 - t0) * P], ACT.Copy).then_inc(gT_out[b], 1)

            def step(n, first, last):
                if first == 0:
                    front(n, 0)
                    gates(n)
                if last < -1:
                    front(n + 1, first)
                    gates(n + 1)

            run_steps(act, N, U, step)

        @block.vector
        def _(dve):
            dve.wait_ge(const_in, CONSTS)

            def layer_stats(n):
                a, s = n.slot(2), n.slot(3)
                dve.wait_ge(x_in[s], n.turn(3, 16, 16))
                for t in range(T):
                    dve.bn_stats(stat[:, a, t, :], xin[:, s, t, :]).then_inc(stats_part, 1)
                hold(dve, stats_part, n.val(T, T), ticks)
                for t in range(T):
                    ins = dve.bn_aggr(mv[:, a, t, :], stat[:, a, t, :])
                ins.then_inc(stats, 1)

            OPS = 19

            def route(n):
                done = [0]

                def then(ins):
                    ins.then_inc(routing, 1)
                    done[0] += 1
                    dve.wait_ge(routing, n.val(OPS, done[0]))

                def wide(x):
                    return x.unsqueeze(2).to_broadcast([P, T, E])

                ranks = rank[:].unsqueeze(1).to_broadcast([P, T, E])
                dve.wait_ge(logits_made, n.val(1, 1))
                then(dve.tensor_tensor(logit[:], pr[:, 0:T * E].rearrange("p (t e) -> p t e", e=E),
                                       br[:].unsqueeze(1).to_broadcast([P, T, E]), ALU.add))
                for k, x in enumerate((logit, rest)):
                    then(dve.tensor_reduce(best[:, k, :], x[:], AX.X, ALU.max))
                    then(dve.tensor_tensor(hit[:, k, :, :], x[:], wide(best[:, k, :]), ALU.is_equal))
                    then(dve.tensor_tensor(ranked[:, k, :, :], hit[:, k, :, :], ranks, ALU.mult))
                    then(dve.tensor_reduce(top[:, k, :], ranked[:, k, :, :], AX.X, ALU.max))
                    then(dve.tensor_tensor(one[:, k, :, :], ranked[:, k, :, :], wide(top[:, k, :]), ALU.is_equal))
                    if k == 0:
                        then(dve.scalar_tensor_tensor(out=rest[:], in0=one[:, 0, :, :], scalar=NOT_CHOSEN,
                                                      in1=logit[:], op0=ALU.mult, op1=ALU.add))
                then(dve.tensor_tensor(gap[:], best[:, 1, :], best[:, 0, :], ALU.subtract))
                dve.sem_inc(gap_ready, 1)
                dve.wait_ge(second_ready, n.val(1, 1))
                then(dve.tensor_scalar(total[:], second[:], 1.0, None, ALU.add))
                then(dve.reciprocal(share[:, 0, :], total[:]))
                then(dve.tensor_tensor(share[:, 1, :], share[:, 0, :], second[:], ALU.mult))
                for k in range(2):
                    then(dve.tensor_tensor(part[:, k, :, :], one[:, k, :, :], wide(share[:, k, :]), ALU.mult))
                then(dve.tensor_tensor(gate[:, n.slot(2), :, :], part[:, 0, :, :], part[:, 1, :, :], ALU.add))
                assert done[0] == OPS, done
                dve.sem_inc(gates_ready, 1)

            def begin(n, first):
                if first >= 2:
                    dve.wait_ge(x2_out[n.slot(3)], n.turn(3, 16))
                for b, (t0, t1) in enumerate(HALVES):
                    dve.wait_ge(bias_made[b], n.val(1, 1))
                    dve.tensor_tensor(acc[:, n.slot(3), t0:t1, :],
                                      px[:, b, 0:(t1 - t0) * C].rearrange("p (t c) -> p t c", c=C),
                                      xin[:, n.slot(3), t0:t1, :], ALU.add).then_inc(acc_begun[b], 1)

            MIX = E

            def mix(n, t):
                e0 = MIX * t
                b = (n.off * T + t) % 2
                a, o, g = acc[:, n.slot(3), t, :], odd[:, b, :], gate[:, n.slot(2), t, :]
                dve.wait_ge(expert_done, n.val(T, t + 1))
                if t == 0:
                    dve.wait_ge(acc_begun[1], n.val(1, 1))
                for e in range(E):
                    src = pe_out[:, b, e // 4, (e % 4) * C:(e % 4 + 1) * C]
                    if e == 1:
                        dve.tensor_scalar(o, src, g[:, e:e + 1], None, ALU.mult).then_inc(mixing, 1)
                        continue
                    if e >= 2:
                        dve.wait_ge(mixing, n.val(T * MIX, e0 + e - 1))
                    into = a if e % 2 == 0 else o
                    ins = dve.scalar_tensor_tensor(out=into, in0=src, scalar=g[:, e:e + 1], in1=into,
                                                   op0=ALU.mult, op1=ALU.add).then_inc(mixing, 1)
                dve.wait_ge(mixing, n.val(T * MIX, e0 + E))
                dve.tensor_tensor(a, a, o, ALU.add).then_inc(mixed, 1)

            def step(n, first, last):
                if first == 0:
                    for k in range(min(2, N)):
                        layer_stats(n + k)
                    route(n)
                    begin(n, 0)
                if last < -2:
                    dve.wait_ge(normed, n.val(1, 1))
                    layer_stats(n + 2)
                for t in range(2):
                    mix(n, t)
                if last < -1:
                    route(n + 1)
                for t in range(2, 6):
                    mix(n, t)
                if last < -1:
                    begin(n + 1, first)
                mix(n, 6)

            run_steps(dve, N, U, step)

        @block.tensor
        def _(pe):
            pe.wait_ge(const_in, CONSTS)

            def turn(n, first):
                pe.wait_ge(normed, n.val(1, 1))
                for b, (t0, t1) in enumerate(HALVES):
                    if first >= 1:
                        pe.wait_ge(acc_begun[b], n.val())
                    for t in range(t0, t1):
                        ins = pe.transpose(px[:, b, (t - t0) * P:(t - t0 + 1) * P], xn[:, n.slot(2), t, :], idn[:])
                    ins.then_inc(turned[b], 1)

            def logits(n, first):
                pe.wait_ge(xT_out[1], n.val(1, 1))
                if first >= 1:
                    pe.wait_ge(gates_ready, n.val())
                for t in range(T):
                    ins = pe.matmul(pr[:, t * E:(t + 1) * E], xnT[:, n.slot(2), t, :], wr[:], start=True, stop=True)
                ins.then_inc(logits_made, 1)

            def turn_gates(n):
                pe.wait_ge(gates_ready, n.val(1, 1))
                for b, (t0, t1) in enumerate(HALVES):
                    for t in range(t0, t1):
                        ins = pe.transpose(px[0:E, b, (t - t0) * P:(t - t0 + 1) * P], gate[:, n.slot(2), t, :], idn[:])
                    ins.then_inc(gates_turned[b], 1)

            def gated_bias(n):
                for b, (t0, t1) in enumerate(HALVES):
                    pe.wait_ge(gT_out[b], n.val(1, 1))
                    for t in range(t0, t1):
                        ins = pe.matmul(px[:, b, (t - t0) * C:(t - t0 + 1) * C], gateT[:, t, :], be[:],
                                        start=True, stop=True)
                    ins.then_inc(bias_made[b], 1)

            def experts(n, t, first):
                b = (n.off * T + t) % 2
                if first >= 1 or t >= 2:
                    pe.wait_ge(mixed, n.val(T, t - 1))
                for half in range(2):
                    ins = pe.matmul(pe_out[:, b, half, :], xnT[:, n.slot(2), t, :],
                                    we[:, half * 4:half * 4 + 4, :].rearrange("d e c -> d (e c)"), start=True, stop=True)
                ins.then_inc(expert_done, 1)

            def step(n, first, last):
                if first == 0:
                    turn(n, 0)
                    logits(n, 0)
                    turn_gates(n)
                    gated_bias(n)
                if last < -1:
                    turn(n + 1, 1)
                for t in range(2):
                    experts(n, t, first)
                if last < -1:
                    logits(n + 1, 1)
                for t in range(2, 5):
                    experts(n, t, first)
                if last < -1:
                    turn_gates(n + 1)
                experts(n, 5, first)
                if last < -1:
                    gated_bias(n + 1)
                experts(n, 6, first)

            run_steps(pe, N, U, step)


ROW = 64
QUAD = 4
GROUPS = C // QUAD
ODD = IMG // 2 + 1
EVEN = IMG // 2
BLOCKS = (2, 3, 5)
FURTHEST = (64, 128, 256)
G_LEN = tuple(P - 1 + P * b for b in BLOCKS)
G_OFF = (0, G_LEN[0], G_LEN[0] + G_LEN[1])
G_ALL = sum(G_LEN)

ODD_ROWS = (((54, 1, 1), (0, 2, 27)), ((53, 0, 2), (1, 2, 26)))
EVEN_ROWS = (((53, 0, 2), (1, 2, 26)), ((54, 0, 1), (0, 1, 27)))
COLS = ((53, 0, 3), (0, 3, 53))
ROLLED = 8


def load_rolled(eng, dst, pitch, src, n, rows, sem):
    for half in range(2):
        for row, tile, tiles in rows[half]:
            for col, w0, ws in COLS:
                p0 = half * pitch + w0
                eng.dma_start(dst[p0:p0 + ws, tile:tile + tiles, :],
                              dram(src, n.val(PIX * C, (row * IMG + col) * C),
                                   [(C, ws), (2 * IMG * C, tiles), (1, C)])).then_inc(sem, 16)


def focal_input_stage(nc, B, x2, Wf, bf, edge_mask, ident, q, c0, gates):
    N = B
    EPS = 1e-6
    OUT = 2 * C + 4
    U = 2
    CHUNKS = [(t, min(4, ODD - t)) for t in range(0, ODD, 4)]
    NCH = len(CHUNKS)
    PAIRS = [(t, min(2, ODD - t)) for t in range(0, ODD, 2)]
    NPR = len(PAIRS)
    S = Stage(nc, "foc")
    with S.ctx:
        idn = S.sb("idn", [P, P])
        wf = S.sb("wf", [C, OUT])
        bias = S.sb("bias", [P, OUT])
        edge = S.sb("edge", [P, 4])
        cbias = S.sb("cbias", [P, 4, C])
        halfneg = S.sb("halfneg", [P, ODD])
        xin = S.sb("xin", [P, 2, ODD, C])
        stat = S.sb("stat", [P, ODD, 6])
        mv = S.sb("mv", [P, ODD, 2])
        rstd = S.sb("rstd", [P, 2, ODD])
        nmean = S.sb("nmean", [P, 2, ODD])
        xn = S.sb("xn", [P, 2, 4, C])
        xnT = S.sb("xnT", [C, 2, 4 * P])
        qs = S.sb("qs", [P, ODD, C])
        cs = S.sb("cs", [P, GROUPS, ODD, QUAD])
        gs = S.sb("gs", [P, 4, ODD])
        px = S.ps("px", [P, 2, BANK])
        py = S.ps("py", [P, 2, 2, BANK])

        ticks = S.sem("ticks")
        const_in = S.sem("const_in")
        zeroed = S.sem("zeroed")
        filled = S.sem("filled")
        cbias_built = S.sem("cbias_built")
        x_in = S.sems("x_in", 2)
        stats_part, stats, eps_added, rstd_done = (S.sem(f"{k}") for k in ("stats_part", "stats", "eps_added", "rstd_done"))
        nmean_done = S.sem("nmean_done")
        normed, turned, xT_out = S.sem("normed"), S.sem("turned"), S.sem("xT_out")
        made, ctx_read, gates_read, q_read = S.sem("made"), S.sem("ctx_read"), S.sem("gates_read"), S.sem("q_read")
        q_biased = S.sem("q_biased")
        q_out, c_out, g_out = S.sem("q_out"), S.sem("c_out"), S.sem("g_out")
        block = S.block()

        @block.sync
        def _(sp):
            for dst, src in ((idn[:], ident), (wf[:], Wf), (bias[:], row_to_all(bf, OUT)), (edge[:], edge_mask)):
                sp.dma_start(dst, src).then_inc(const_in, 16)
            sp.wait_ge(zeroed, 2)

            def step(n, first, last):
                if first == 0:
                    load_rolled(sp, xin[:, n.slot(2), :, :], ROW, x2, n, ODD_ROWS, x_in[n.slot(2)])
                if last < -1:
                    if first >= 1:
                        hold(sp, normed, n.val(NCH), ticks)
                    load_rolled(sp, xin[:, (n + 1).slot(2), :, :], ROW, x2, n + 1, ODD_ROWS, x_in[(n + 1).slot(2)])
                hold(sp, ctx_read, n.val(NPR, NPR), ticks)
                sp.dma_start(dram(c0, n.val(ODD * QUAD), [(B * ODD * QUAD, P), (P * B * ODD * QUAD, GROUPS), (1, ODD * QUAD)]),
                             cs[:].rearrange("p g j c -> p g (j c)")).then_inc(c_out, 16)
                hold(sp, gates_read, n.val(NPR, NPR), ticks)
                for half, j0 in ((0, 0), (1, 1)):
                    sp.dma_start(dram(gates, n.val(EVEN, half * ROW * 4 * B * EVEN), [(4 * B * EVEN, ROW), (B * EVEN, 4), (1, EVEN)]),
                                 gs[(1 - half) * ROW:(2 - half) * ROW, :, j0:j0 + EVEN]).then_inc(g_out, 16)
                hold(sp, q_biased, n.val(1, 1), ticks)
                for half, j0 in ((0, 1), (1, 0)):
                    row = 2 * j0 - 1 + half
                    sp.dma_start(dram(q, n.val(PIX * C, row * IMG * C), [(C, IMG), (2 * IMG * C, EVEN), (1, C)]),
                                 qs[half * ROW:half * ROW + IMG, j0:j0 + EVEN, :]).then_inc(q_out, 16)

            run_steps(sp, N, U, step)
            sp.wait_ge(c_out, 16 * N)
            sp.wait_ge(g_out, 32 * N)
            sp.wait_ge(q_out, 32 * N)

        @block.gpsimd
        def _(pool):
            for s in range(2):
                pool.memset(xin[:, s, :, :], 0.0).then_inc(zeroed, 1)
            pool.memset(halfneg[:], -0.5).then_inc(filled, 1)
            pool.wait_ge(filled, 1)
            pool.wait_ge(const_in, 64)

            def step(n, first, last):
                def scale(n):
                    a = n.slot(2)
                    hold(pool, stats, n.val(1, 1), ticks)
                    pool.tensor_scalar(rstd[:, a, :], mv[:, :, 1], EPS, None, ALU.add).then_inc(eps_added, 1)
                    pool.wait_ge(eps_added, n.val(1, 1))
                    pool.tensor_tensor(rstd[:, a, :], rstd[:, a, :], halfneg[:], ALU.pow).then_inc(rstd_done, 1)

                if first == 0:
                    scale(n)
                if last < -1:
                    scale(n + 1)
                pool.wait_ge(q_read, n.val(NPR, NPR))
                pool.tensor_tensor(qs[:], qs[:], bias[:, 0:C].unsqueeze(1).to_broadcast([P, ODD, C]), ALU.add)\
                    .then_inc(q_biased, 1)

            run_steps(pool, N, U, step)

        @block.scalar
        def _(act):
            act.wait_ge(const_in, 64)

            def normalise(n, c):
                t0, tn = CHUNKS[c]
                b = (n.off * NCH + c) % 2
                if c == 0:
                    act.wait_ge(nmean_done, n.val(1, 1))
                if not (n.is_static and n.off * NCH + c < 2):
                    act.wait_ge(turned, n.val(NCH, c - 1))
                for t in range(tn):
                    ins = act.activation(xn[:, b, t, :], xin[:, n.slot(2), t0 + t, :], ACT.Identity,
                                         bias=nmean[:, n.slot(2), t0 + t:t0 + t + 1],
                                         scale=rstd[:, n.slot(2), t0 + t:t0 + t + 1])
                ins.then_inc(normed, 1)

            def step(n, first, last):
                if first == 0:
                    normalise(n, 0)
                for c, (t0, tn) in enumerate(CHUNKS):
                    b = (n.off * NCH + c) % 2
                    act.wait_ge(turned, n.val(NCH, c + 1))
                    act.activation(xnT[:, b, 0:tn * P], px[:, b, 0:tn * P], ACT.Copy).then_inc(xT_out, 1)
                    if c + 1 < NCH:
                        normalise(n, c + 1)
                    elif last < -1:
                        normalise(n + 1, 0)
                    for k in range(2 * c, min(2 * c + 2, NPR)):
                        p0, pn = PAIRS[k]
                        y = (n.off * NPR + k) % 2
                        if k == 0 and first >= 1:
                            act.wait_ge(q_out, n.val(32))
                            act.sem_inc(ticks, 1)
                        act.wait_ge(gates_read, n.val(NPR, k + 1))
                        act.activation(qs[:, p0:p0 + pn, :], py[:, y, 0:pn, 0:C], ACT.Copy).then_inc(q_read, 1)

            run_steps(act, N, U, step)

        @block.vector
        def _(dve):
            dve.wait_ge(const_in, 64)
            for k in range(4):
                dve.tensor_scalar(cbias[:, k, :], bias[:, C:2 * C], edge[:, k:k + 1], None, ALU.mult).then_inc(cbias_built, 1)
            dve.wait_ge(cbias_built, 4)

            def layer_stats(n):
                s = n.slot(2)
                dve.wait_ge(x_in[s], n.turn(2, 16 * ROLLED, 16 * ROLLED))
                for t in range(ODD):
                    dve.bn_stats(stat[:, t, :], xin[:, s, t, :]).then_inc(stats_part, 1)
                hold(dve, stats_part, n.val(ODD, ODD), ticks)
                for t in range(ODD):
                    ins = dve.bn_aggr(mv[:, t, :], stat[:, t, :])
                ins.then_inc(stats, 1)
                dve.wait_ge(rstd_done, n.val(1, 1))
                dve.sem_inc(ticks, 1)
                dve.wait_ge(stats, n.val(1, 1))
                dve.scalar_tensor_tensor(out=nmean[:, s, :], in0=mv[:, :, 0], scalar=-1.0, in1=rstd[:, s, :],
                                         op0=ALU.mult, op1=ALU.mult).then_inc(nmean_done, 1)

            def step(n, first, last):
                if first == 0:
                    layer_stats(n)
                for k, (p0, pn) in enumerate(PAIRS):
                    y = (n.off * NPR + k) % 2
                    if k == NPR // 2 and last < -1:
                        if first >= 1:
                            dve.wait_ge(normed, n.val(NCH))
                            dve.sem_inc(ticks, 1)
                        dve.wait_ge(nmean_done, n.val(1, 1))
                        layer_stats(n + 1)
                    dve.wait_ge(made, n.val(NPR, k + 1))
                    if k == 0 and first >= 1:
                        dve.sem_inc(ticks, 1)
                        dve.wait_ge(c_out, n.val(16))
                        dve.sem_inc(ticks, 1)
                        dve.wait_ge(g_out, n.val(32))
                    version = 0 if k == 0 else (3 if k == NPR - 1 else 1)
                    dve.tensor_tensor(cs[:, :, p0:p0 + pn, :].rearrange("p g j c -> p j g c"),
                                      py[:, y, 0:pn, C:2 * C].rearrange("p j (g c) -> p j g c", c=QUAD),
                                      cbias[:, version:version + pn, :].rearrange("p j (g c) -> p j g c", c=QUAD),
                                      ALU.add).then_inc(ctx_read, 1)
                    dve.tensor_tensor(gs[:, :, p0:p0 + pn].rearrange("p l j -> p j l"), py[:, y, 0:pn, 2 * C:OUT],
                                      bias[:, 2 * C:OUT].unsqueeze(1).to_broadcast([P, pn, 4]), ALU.add).then_inc(gates_read, 1)

            run_steps(dve, N, U, step)

        @block.tensor
        def _(pe):
            pe.wait_ge(const_in, 64)

            def turn(n, c):
                t0, tn = CHUNKS[c]
                b = (n.off * NCH + c) % 2
                pe.wait_ge(normed, n.val(NCH, c + 1))
                if not (n.is_static and n.off * NCH + c < 2):
                    pe.wait_ge(xT_out, n.val(NCH, c - 1))
                for t in range(tn):
                    ins = pe.transpose(px[:, b, t * P:(t + 1) * P], xn[:, b, t, :], idn[:])
                ins.then_inc(turned, 1)

            def step(n, first, last):
                if first == 0:
                    turn(n, 0)
                for c, (t0, tn) in enumerate(CHUNKS):
                    b = (n.off * NCH + c) % 2
                    if c + 1 < NCH:
                        turn(n, c + 1)
                    elif last < -1:
                        turn(n + 1, 0)
                    pe.wait_ge(xT_out, n.val(NCH, c + 1))
                    for k in range(2 * c, min(2 * c + 2, NPR)):
                        p0, pn = PAIRS[k]
                        y = (n.off * NPR + k) % 2
                        if not (n.is_static and n.off * NPR + k < 2):
                            pe.wait_ge(gates_read, n.val(NPR, k - 1))
                            pe.sem_inc(ticks, 1)
                            pe.wait_ge(q_read, n.val(NPR, k - 1))
                        for j in range(pn):
                            t = p0 + j - t0
                            ins = pe.matmul(py[:, y, j, 0:OUT], xnT[:, b, t * P:(t + 1) * P], wf[:], start=True, stop=True)
                        ins.then_inc(made, 1)

            run_steps(pe, N, U, step)


def convolution_stage(nc, B, c0, gates, kernels, gap_mask, ctx_all):
    N = C
    HALF = B // 2
    U = 8
    PER = QUAD
    AHEAD = 4
    T_ALL = P * sum(BLOCKS)
    T_OFF = (0, P * BLOCKS[0], P * (BLOCKS[0] + BLOCKS[1]))
    S = Stage(nc, "conv")
    with S.ctx:
        gvec = S.sb("gvec", [C, G_ALL])
        ones = S.sb("ones", [P, P])
        gap = S.sb("gap", [P, 1])
        gate = S.sb("gate", [P, 4, B, EVEN])
        toep = S.sb("toep", [P, 2, PER, T_ALL])
        cin = S.sb("cin", [P, 2, B, ODD, PER])
        c1 = S.sb("c1", [P, 4, B, EVEN + 2])
        c2 = S.sb("c2", [P, 2, B, EVEN + 4])
        c3 = S.sb("c3", [P, 2, B, EVEN])
        g1 = S.sb("g1", [P, B, EVEN])
        g2 = S.sb("g2", [P, B, EVEN])
        g3 = S.sb("g3", [P, B, EVEN])
        pooled = S.sb("pooled", [P, B])
        glob = S.sb("glob", [P, B])
        out = S.sb("out", [P, 2, B, PER, EVEN])
        gvec_dram = nc.dram_tensor("gvec_dram", (C, G_ALL), F32).ap()
        group_dram = nc.dram_tensor("group_dram", (2, PER, G_ALL), F32).ap()
        rows_dram = nc.dram_tensor("rows_dram", (2, PER, P, T_ALL), F32).ap()
        pc = [S.ps(f"pc{k}", [P, 2, BANK]) for k in range(3)]
        pm = S.ps("pm", [P, BANK])

        ticks = S.sem("ticks")
        zeroed = S.sem("zeroed")
        taps_in, gvec_out = S.sem("taps_in"), S.sem("gvec_out")
        const_in = S.sem("const_in")
        rows_made = S.sems("rows_made", 2)
        group_in, toep_in, c0_in = S.sems("group_in", 2), S.sems("toep_in", 2), S.sems("c0_in", 2)
        convolved = S.sems("convolved", 3)
        activated = S.sems("activated", 3)
        gated1, gated2, gated3 = S.sem("gated1"), S.sem("gated2"), S.sem("gated3")
        pooled_part, averaged, glob_ready = S.sem("pooled_part"), S.sem("averaged"), S.sem("glob_ready")
        summed, gglob, summed_glob = S.sem("summed"), S.sem("gglob"), S.sem("summed_glob")
        combined = S.sem("combined")
        stored = S.sems("stored", 2)
        block = S.block()
        NG = N // PER

        @block.sync
        def _(sp):
            sp.wait_ge(zeroed, 1)
            for k, size in enumerate(TAPS):
                r = size // 2
                at = G_OFF[k] + P - 1 + FURTHEST[k] - r * ROW - r
                for row in range(size):
                    sp.dma_start(gvec[:, at + row * ROW:at + row * ROW + size],
                                 dram(kernels[k], row * size, [(size * size, C), (1, size)])).then_inc(taps_in, 16)
            sp.dma_start(gate[:], gates).then_inc(const_in, 16)
            sp.dma_start(gap[:], gap_mask).then_inc(const_in, 16)
            sp.wait_ge(taps_in, 16 * sum(TAPS))
            sp.dma_start(gvec_dram, gvec[:]).then_inc(gvec_out, 16)
            sp.wait_ge(gvec_out, 16)

            def load(g, n, extra):
                s = g.slot(2)
                sp.dma_start(cin[:, s, :, :, :].rearrange("p b j c -> p (b j c)"),
                             dram(c0, g.val(P * B * ODD * PER), [(B * ODD * PER, P), (1, B * ODD * PER)]))\
                  .then_inc(c0_in[s], 16)
                sp.dma_start(dram(group_dram, s * PER * G_ALL, [(G_ALL, PER), (1, G_ALL)]),
                             dram(gvec_dram, g.val(PER * G_ALL), [(G_ALL, PER), (1, G_ALL)])).then_inc(group_in[s], 16)
                hold(sp, group_in[s], g.turn(2, 16, 16), ticks)
                for k, blocks in enumerate(BLOCKS):
                    sp.dma_start(dram(rows_dram, s * PER * P * T_ALL + T_OFF[k], [(P * T_ALL, PER), (T_ALL, P), (1, P * blocks)]),
                                 dram(group_dram, s * PER * G_ALL + G_OFF[k] + P - 1,
                                      [(G_ALL, PER), (-1, P), (1, P * blocks)])).then_inc(rows_made[s], 16)
                hold(sp, rows_made[s], g.turn(2, 48, 48), ticks)
                sp.dma_start(toep[:, s, :, :], dram(rows_dram, s * PER * P * T_ALL, [(T_ALL, P), (P * T_ALL, PER), (1, T_ALL)]))\
                  .then_inc(toep_in[s], 16)

            def step(n, first, last):
                if n.off % PER != PER - 1:
                    return
                g = Step(n.loop, U // PER, n.off // PER)
                if first < PER:
                    load(g, n, 0)
                    load(g + 1, n, 1)
                if last + 1 < -2 * PER + 1:
                    hold(sp, convolved[2], n.val(1, 1), ticks)
                    load(g + 2, n, 2)
                hold(sp, combined, n.val(1, 1), ticks)
                sp.dma_start(dram(ctx_all, g.val(P * B * EVEN * PER), [(B * EVEN * PER, P), (1, B * EVEN * PER)]),
                             out[:, g.slot(2), :, :, :].rearrange("p b c i -> p (b c i)")).then_inc(stored[g.slot(2)], 16)

            run_steps(sp, N, U, step, AHEAD + PER)
            for s in range(2):
                sp.wait_ge(stored[s], 16 * (NG // 2))

        @block.gpsimd
        def _(pool):
            pool.memset(gvec[:], 0.0).then_inc(zeroed, 1)
            pool.memset(c1[:], 0.0).then_inc(zeroed, 1)
            pool.memset(c2[:], 0.0).then_inc(zeroed, 1)
            pool.memset(ones[:], 1.0).then_inc(zeroed, 1)
            pool.wait_ge(const_in, 32)

            def step(n, first, last):
                pool.wait_ge(activated[1], n.val(1, 1))
                if first >= 1:
                    pool.sem_inc(ticks, 1)
                    pool.wait_ge(combined, n.val())
                pool.tensor_tensor(g2[:], c2[:, n.slot(2), :, 2:2 + EVEN], gate[:, 1, :, :], ALU.mult).then_inc(gated2, 1)

            run_steps(pool, N, U, step, AHEAD)

        @block.scalar
        def _(act):
            act.wait_ge(zeroed, 4)
            act.wait_ge(const_in, 32)

            def gelu(k, n, first):
                dst, slots = (c1, c2, c3)[k], (4, 2, 2)[k]
                edge = (1, 2, 0)[k]
                act.wait_ge(convolved[k], n.val(1, 1))
                if first >= slots:
                    act.sem_inc(ticks, 1)
                    act.wait_ge((gated1, gated2, gated3)[k], n.val(1, 1 - slots))
                    if k < 2:
                        act.sem_inc(ticks, 1)
                        act.wait_ge(convolved[k + 1], n.val(1, 1 - slots))
                    else:
                        act.sem_inc(ticks, 1)
                        act.wait_ge(pooled_part, n.val(1, -1))
                for half in range(2):
                    ins = act.activation(dst[:, n.slot(slots), half * HALF:(half + 1) * HALF, edge:edge + EVEN],
                                         pc[k][:, half, 0:HALF * EVEN].rearrange("p (b i) -> p b i", i=EVEN),
                                         ACT.Gelu, scale=gap[:])
                ins.then_inc(activated[k], 1)

            def average(n, first):
                act.wait_ge(averaged, n.val(1, 1))
                if first >= 1:
                    act.sem_inc(ticks, 1)
                    act.wait_ge(gglob, n.val())
                act.activation(glob[:], pm[:, 0:B], ACT.Gelu, scale=1.0 / PIX).then_inc(glob_ready, 1)

            def step(n, first, last):
                if first == 0:
                    gelu(0, n, 0)
                    gelu(0, n + 1, 1)
                    gelu(1, n, 0)
                if last < -3:
                    gelu(0, n + 2, first + 2)
                if first >= 1:
                    average(n - 1, first - 1)
                if last < -2:
                    gelu(1, n + 1, first + 1)
                if last < -1:
                    gelu(2, n, first)

            run_steps(act, N + 1, U, step, AHEAD)

        @block.vector
        def _(dve):
            dve.wait_ge(const_in, 32)

            def products(n, first):
                s = n.slot(2)
                dve.wait_ge(activated[2], n.val(1, 1))
                dve.tensor_reduce(pooled[:], c3[:, s, :, :], AX.X, ALU.add).then_inc(pooled_part, 1)
                if first >= 1:
                    dve.wait_ge(combined, n.val())
                dve.tensor_tensor(g3[:], c3[:, s, :, :], gate[:, 2, :, :], ALU.mult).then_inc(gated3, 1)
                dve.wait_ge(gated3, n.val(1, 1))
                dve.sem_inc(ticks, 1)
                dve.wait_ge(gated1, n.val(1, 1))
                dve.tensor_tensor(g3[:], g3[:], g1[:], ALU.add).then_inc(summed, 1)

            def first_gate(n, first):
                dve.wait_ge(activated[0], n.val(1, 1))
                if first >= 1:
                    dve.sem_inc(ticks, 1)
                    dve.wait_ge(summed_glob, n.val())
                dve.tensor_tensor(g1[:], c1[:, n.slot(4), :, 1:1 + EVEN], gate[:, 0, :, :], ALU.mult).then_inc(gated1, 1)

            def combine(n, first):
                g = Step(n.loop, U // PER, n.off // PER)
                s = g.slot(2)
                dve.wait_ge(glob_ready, n.val(1, 1))
                dve.sem_inc(ticks, 1)
                dve.wait_ge(summed, n.val(1, 1))
                dve.tensor_tensor(g1[:], gate[:, 3, :, :], glob[:].unsqueeze(2).to_broadcast([P, B, EVEN]),
                                  ALU.mult).then_inc(gglob, 1)
                dve.wait_ge(gglob, n.val(1, 1))
                dve.tensor_tensor(g3[:], g3[:], g1[:], ALU.add).then_inc(summed_glob, 1)
                dve.wait_ge(summed_glob, n.val(1, 1))
                if first >= 2 * PER and n.off % PER == 0:
                    dve.sem_inc(ticks, 1)
                    dve.wait_ge(stored[s], g.turn(2, 16))
                dve.sem_inc(ticks, 1)
                dve.wait_ge(gated2, n.val(1, 1))
                dve.tensor_tensor(out[:, s, :, n.off % PER, :], g3[:], g2[:], ALU.add).then_inc(combined, 1)

            def step(n, first, last):
                if first >= 1:
                    combine(n - 1, first - 1)
                if last < -1:
                    first_gate(n, first)
                    products(n, first)

            run_steps(dve, N + 1, U, step, AHEAD)

        @block.tensor
        def _(pe):
            pe.wait_ge(zeroed, 4)

            def convolve(k, n, first, group_first):
                g = Step(n.loop, U // PER, n.off // PER)
                ch, s = n.off % PER, g.slot(2)
                if k == 0 and ch == 0:
                    hold(pe, c0_in[s], g.turn(2, 16, 16), ticks)
                    hold(pe, toep_in[s], g.turn(2, 16, 16), ticks)
                if k > 0:
                    hold(pe, activated[k - 1], n.val(1, 1), ticks)
                if first >= 1:
                    pe.wait_ge(activated[k], n.val())
                blocks = BLOCKS[k]
                for blk in range(blocks):
                    w = toep[:, s, ch, T_OFF[k] + blk * P:T_OFF[k] + (blk + 1) * P]
                    below = blocks - 1 - blk
                    for half in range(2):
                        b = slice(half * HALF, (half + 1) * HALF)
                        if k == 0:
                            src = cin[:, s, b, below:below + EVEN, ch]
                        else:
                            src = (c1, c2)[k - 1][:, n.slot((4, 2)[k - 1]), b, below:below + EVEN]
                        ins = pe.matmul(pc[k][:, half, 0:HALF * EVEN], w, src, start=(blk == 0), stop=(blk == blocks - 1))
                ins.then_inc(convolved[k], 1)

            def average(n, first):
                if first >= 1:
                    pe.wait_ge(glob_ready, n.val())
                    pe.sem_inc(ticks, 1)
                pe.wait_ge(pooled_part, n.val(1, 1))
                pe.matmul(pm[:, 0:B], ones[:], pooled[:], start=True, stop=True).then_inc(averaged, 1)

            def step(n, first, last):
                if first == 0:
                    convolve(0, n, 0, 0)
                    convolve(0, n + 1, 1, 0)
                    convolve(1, n, 0, 0)
                if last < -3:
                    convolve(0, n + 2, first + 2, 0)
                if first >= 1:
                    average(n - 1, first - 1)
                if last < -2:
                    convolve(1, n + 1, first + 1, 0)
                if last < -1:
                    convolve(2, n, first, 0)

            run_steps(pe, N + 1, U, step, AHEAD)


def focal_output_stage(nc, B, ctx_all, q, x2, Wh, bh, gamma, beta, Wp, bp, ident, x3, gram):
    N = B
    TOK = 2 * IMG
    CH = 4
    NCH = EVEN // CH
    EPS, EPS_T = 1e-3, 1e-5
    U = 2
    S = Stage(nc, "mod")
    with S.ctx:
        idn = S.sb("idn", [P, P])
        wh = S.sb("wh", [C, C])
        wp = S.sb("wp", [C, C])
        wpg = S.sb("wpg", [C, C])
        bhr = S.sb("bhr", [P, C])
        bpr = S.sb("bpr", [P, C])
        gcol = S.sb("gcol", [C, 1])
        bcol = S.sb("bcol", [C, 1])
        bmat = S.sb("bmat", [C, P])
        brow = S.sb("brow", [P, C])
        halfneg = S.sb("halfneg", [P, CH])
        cin = S.sb("cin", [TOK, 2, C, EVEN])
        qin = S.sb("qin", [TOK, 2, EVEN, C])
        xin = S.sb("xin", [TOK, 2, EVEN, C])
        cT = S.sb("cT", [C, 2, CH * TOK])
        y = S.sb("y", [TOK, 2, CH, C])
        yn = S.sb("yn", [TOK, 2, CH, C])
        yT = S.sb("yT", [C, 2, CH * TOK])
        z = S.sb("z", [TOK, 2, CH, C + 1])
        stat = S.sb("stat", [TOK, 2, CH, 6])
        mv = S.sb("mv", [TOK, 2, 2, CH, 2])
        rstd = S.sb("rstd", [TOK, 2, 2, CH])
        nmean = S.sb("nmean", [TOK, 2, 2, CH])
        gout = S.sb("gout", [C, C + 1])

        pt = S.ps("pt", [P, BANK])
        pm = S.ps("pm", [P, 2, BANK])
        pu = S.ps("pu", [P, BANK])
        pz = S.ps("pz", [P, 2, BANK])
        pg = S.ps("pg", [P, BANK])

        ticks = S.sem("ticks")
        const_in, filled = S.sem("const_in"), S.sem("filled")
        scaled, beta_wide, bias_made, bias_built = (S.sem(k) for k in ("scaled", "beta_wide", "bias_made", "bias_built"))
        c_in, q_in, x_in = S.sems("c_in", 2), S.sems("q_in", 2), S.sems("x_in", 2)
        x_biased = S.sem("x_biased")
        turned, cT_out, modulated = S.sem("turned"), S.sem("cT_out"), S.sem("modulated")
        biased, gated = S.sem("biased"), S.sem("gated")
        parts, stats = S.sems("parts", 2), S.sems("stats", 2)
        eps_added, rstd_done, nmean_done = S.sems("eps_added", 2), S.sems("rstd_done", 2), S.sems("nmean_done", 2)
        y_normed, y_turned, yT_out, projected = (S.sem(k) for k in ("y_normed", "y_turned", "yT_out", "projected"))
        x3_made, z_normed, gram_added = S.sem("x3_made"), S.sem("z_normed"), S.sem("gram_added")
        x3_out, gram_copied, gram_out = S.sems("x3_out", 2), S.sem("gram_copied"), S.sem("gram_out")
        block = S.block()
        CONSTS = 16 * 7

        @block.sync
        def _(sp):
            for dst, src in ((idn[:], ident), (wh[:], Wh), (wp[:], Wp), (bhr[:], row_to_all(bh, C)),
                             (bpr[:], row_to_all(bp, C)), (gcol[:], dram(gamma, 0, [(1, C), (1, 1)])),
                             (bcol[:], dram(beta, 0, [(1, C), (1, 1)]))):
                sp.dma_start(dst, src).then_inc(const_in, 16)

            def load(n):
                s = n.slot(2)
                for half in range(2):
                    p0 = half * IMG
                    sp.dma_start(cin[p0:p0 + IMG, s, :, :].rearrange("p (g c) i -> p g (c i)", c=QUAD),
                                 dram(ctx_all, n.val(EVEN * QUAD, half * ROW * B * EVEN * QUAD),
                                      [(B * EVEN * QUAD, IMG), (P * B * EVEN * QUAD, GROUPS), (1, EVEN * QUAD)]))\
                      .then_inc(c_in[s], 16)
                sp.dma_start(qin[:, s, :, :], dram(q, n.val(PIX * C), [(C, TOK), (TOK * C, EVEN), (1, C)])).then_inc(q_in[s], 16)
                load_rolled(sp, xin[:, s, :, :], IMG, x2, n, EVEN_ROWS, x_in[s])

            def step(n, first, last):
                if first == 0:
                    load(n)
                if last < -1:
                    if first >= 1:
                        hold(sp, x3_out[(n + 1).slot(2)], (n + 1).turn(2, 16), ticks)
                        hold(sp, z_normed, n.val(NCH), ticks)
                    load(n + 1)
                hold(sp, x3_made, n.val(NCH, NCH), ticks)
                sp.dma_start(dram(x3, n.val(PIX * C), [(C, TOK), (TOK * C, EVEN), (1, C)]),
                             xin[:, n.slot(2), :, :]).then_inc(x3_out[n.slot(2)], 16)

            run_steps(sp, N, U, step)
            for s in range(2):
                sp.wait_ge(x3_out[s], 16 * ((N + 1 - s) // 2))
            sp.wait_ge(gram_copied, 1)
            sp.dma_start(gram, gout[:]).then_inc(gram_out, 16)
            sp.wait_ge(gram_out, 16)

        @block.gpsimd
        def _(pool):
            pool.memset(halfneg[:], -0.5).then_inc(filled, 1)
            pool.memset(z[:], 1.0).then_inc(filled, 1)
            pool.memset(bmat[:], 1.0).then_inc(filled, 1)
            pool.wait_ge(filled, 3)
            pool.wait_ge(bias_built, 1)

            def rsqrt(n, c, which, eps):
                b = (n.off * NCH + c) % 2
                hold(pool, stats[which], n.val(NCH, c + 1), ticks)
                r = rstd[:, which, b, :]
                pool.tensor_scalar(r, mv[:, which, b, :, 1], eps, None, ALU.add).then_inc(eps_added[which], 1)
                pool.wait_ge(eps_added[which], n.val(NCH, c + 1))
                pool.tensor_tensor(r, r, halfneg[0:TOK, :], ALU.pow).then_inc(rstd_done[which], 1)

            def add_bias(n):
                s = n.slot(2)
                pool.wait_ge(x_in[s], n.turn(2, 16 * ROLLED, 16 * ROLLED))
                pool.tensor_tensor(xin[:, s, :, :], xin[:, s, :, :],
                                   brow[0:TOK, :].unsqueeze(1).to_broadcast([TOK, EVEN, C]), ALU.add).then_inc(x_biased, 1)

            def step(n, first, last):
                if first == 0:
                    rsqrt(n, 0, 0, EPS)
                    add_bias(n)
                for c in range(NCH):
                    if c + 1 < NCH:
                        rsqrt(n, c + 1, 0, EPS)
                    elif last < -1:
                        rsqrt(n + 1, 0, 0, EPS)
                    rsqrt(n, c, 1, EPS_T)
                    if c == 4 and last < -1:
                        add_bias(n + 1)

            run_steps(pool, N, U, step)

        @block.scalar
        def _(act):
            act.wait_ge(const_in, CONSTS)
            act.wait_ge(filled, 3)

            def early(n, c):
                b = (n.off * NCH + c) % 2
                act.wait_ge(turned, n.val(NCH, c + 1))
                act.activation(cT[:, b, :], pt[:, 0:CH * TOK], ACT.Copy).then_inc(cT_out, 1)

            def step(n, first, last):
                if first == 0:
                    early(n, 0)
                for c in range(NCH):
                    b = (n.off * NCH + c) % 2
                    if c + 1 < NCH:
                        early(n, c + 1)
                    elif last < -1:
                        early(n + 1, 0)
                    act.wait_ge(nmean_done[0], n.val(NCH, c + 1))
                    if first >= 1 or c >= 2:
                        act.sem_inc(ticks, 1)
                        act.wait_ge(y_turned, n.val(NCH, c - 1))
                    for t in range(CH):
                        ins = act.activation(yn[:, b, t, :], y[:, b, t, :], ACT.Identity,
                                             bias=nmean[:, 0, b, t:t + 1], scale=rstd[:, 0, b, t:t + 1])
                    ins.then_inc(y_normed, 1)
                    act.wait_ge(y_turned, n.val(NCH, c + 1))
                    act.activation(yT[:, b, :], pu[:, 0:CH * TOK], ACT.Copy).then_inc(yT_out, 1)
                    act.wait_ge(nmean_done[1], n.val(NCH, c + 1))
                    if first >= 1 or c >= 2:
                        act.sem_inc(ticks, 1)
                        act.wait_ge(gram_added, n.val(NCH, c - 1))
                    for t in range(CH):
                        ins = act.activation(z[:, b, t, 0:C], xin[:, n.slot(2), CH * c + t, :], ACT.Identity,
                                             bias=nmean[:, 1, b, t:t + 1], scale=rstd[:, 1, b, t:t + 1])
                    ins.then_inc(z_normed, 1)

            run_steps(act, N, U, step)
            act.wait_ge(gram_added, N * NCH)
            act.activation(gout[:], pg[:, 0:C + 1], ACT.Copy).then_inc(gram_copied, 1)

        @block.vector
        def _(dve):
            dve.wait_ge(const_in, CONSTS)
            dve.wait_ge(filled, 3)
            dve.tensor_scalar(bmat[:], bmat[:], bcol[:], None, ALU.mult).then_inc(beta_wide, 1)
            dve.tensor_scalar(wpg[:], wp[:], gcol[:], None, ALU.mult).then_inc(scaled, 1)
            dve.wait_ge(bias_made, 1)
            dve.tensor_tensor(brow[:], pm[:, 0, 0:C], bpr[:], ALU.add).then_inc(bias_built, 1)

            def statistics(n, c, which, src):
                b = (n.off * NCH + c) % 2
                for t in range(CH):
                    dve.bn_stats(stat[:, which, t, :], src[:, t, :]).then_inc(parts[which], 1)
                hold(dve, parts[which], n.val(NCH * CH, CH * c + CH), ticks)
                for t in range(CH):
                    ins = dve.bn_aggr(mv[:, which, b, t, :], stat[:, which, t, :])
                ins.then_inc(stats[which], 1)

            def negate(n, c, which):
                b = (n.off * NCH + c) % 2
                hold(dve, rstd_done[which], n.val(NCH, c + 1), ticks)
                dve.scalar_tensor_tensor(out=nmean[:, which, b, :], in0=mv[:, which, b, :, 0], scalar=-1.0,
                                         in1=rstd[:, which, b, :], op0=ALU.mult, op1=ALU.mult)\
                   .then_inc(nmean_done[which], 1)

            def modulate(n, c, first):
                b = (n.off * NCH + c) % 2
                if c == 0:
                    dve.wait_ge(q_in[n.slot(2)], n.turn(2, 16, 16))
                    dve.sem_inc(ticks, 1)
                if first >= 1 or c >= 2:
                    dve.wait_ge(y_normed, n.val(NCH, c - 1))
                    dve.sem_inc(ticks, 1)
                dve.wait_ge(modulated, n.val(NCH, c + 1))
                dve.tensor_tensor(y[:, b, :, :], pm[0:TOK, b, :].rearrange("p (t c) -> p t c", c=C),
                                  bhr[0:TOK, :].unsqueeze(1).to_broadcast([TOK, CH, C]), ALU.add).then_inc(biased, 1)
                dve.wait_ge(biased, n.val(NCH, c + 1))
                dve.tensor_tensor(y[:, b, :, :], y[:, b, :, :], qin[:, n.slot(2), CH * c:CH * c + CH, :], ALU.mult)\
                   .then_inc(gated, 1)
                dve.wait_ge(gated, n.val(NCH, c + 1))
                statistics(n, c, 0, y[:, b, :, :])
                negate(n, c, 0)

            def step(n, first, last):
                if first == 0:
                    modulate(n, 0, 0)
                for c in range(NCH):
                    b = (n.off * NCH + c) % 2
                    if c + 1 < NCH:
                        modulate(n, c + 1, first)
                    elif last < -1:
                        modulate(n + 1, 0, first + 1)
                    dve.wait_ge(x_biased, n.val(1, 1))
                    dve.sem_inc(ticks, 1)
                    dve.wait_ge(projected, n.val(NCH, c + 1))
                    x = xin[:, n.slot(2), CH * c:CH * c + CH, :]
                    dve.tensor_tensor(x, pz[0:TOK, b, :].rearrange("p (t c) -> p t c", c=C), x, ALU.add).then_inc(x3_made, 1)
                    dve.wait_ge(x3_made, n.val(NCH, c + 1))
                    statistics(n, c, 1, x)
                    negate(n, c, 1)

            run_steps(dve, N, U, step)

        @block.tensor
        def _(pe):
            pe.wait_ge(const_in, CONSTS)
            pe.wait_ge(beta_wide, 1)
            pe.matmul(pm[:, 0, 0:C], bmat[:], wp[:], start=True, stop=True).then_inc(bias_made, 1)
            pe.wait_ge(scaled, 1)
            pe.wait_ge(bias_built, 1)

            def early(n, c, first):
                b = (n.off * NCH + c) % 2
                if c == 0:
                    hold(pe, c_in[n.slot(2)], n.turn(2, 32, 32), ticks)
                if first >= 1 or c >= 1:
                    hold(pe, cT_out, n.val(NCH, c), ticks)
                for t in range(CH):
                    ins = pe.transpose(pt[:, t * TOK:(t + 1) * TOK], cin[:, n.slot(2), :, CH * c + t], idn[0:TOK, 0:TOK])
                ins.then_inc(turned, 1)
                if first >= 1 or c >= 2:
                    hold(pe, biased, n.val(NCH, c - 1), ticks)
                pe.wait_ge(cT_out, n.val(NCH, c + 1))
                for t in range(CH):
                    ins = pe.matmul(pm[0:TOK, b, t * C:(t + 1) * C], cT[:, b, t * TOK:(t + 1) * TOK], wh[:],
                                    start=True, stop=True)
                ins.then_inc(modulated, 1)

            def gram_of(n, c, first, last):
                b = (n.off * NCH + c) % 2
                pe.wait_ge(z_normed, n.val(NCH, c + 1))
                for t in range(CH):
                    ins = pe.matmul(pg[:, 0:C + 1], z[:, b, t, 0:C], z[:, b, t, :],
                                    start=(first == 0 and c == 0 and t == 0),
                                    stop=(last == -1 and c == NCH - 1 and t == CH - 1))
                ins.then_inc(gram_added, 1)

            def step(n, first, last):
                if first == 0:
                    early(n, 0, 0)
                for c in range(NCH):
                    b = (n.off * NCH + c) % 2
                    if c + 1 < NCH:
                        early(n, c + 1, first)
                    elif last < -1:
                        early(n + 1, 0, first + 1)
                    if c >= 1:
                        gram_of(n, c - 1, first, last)
                    elif first >= 1:
                        gram_of(n - 1, NCH - 1, first - 1, -MANY)
                    pe.wait_ge(y_normed, n.val(NCH, c + 1))
                    if first >= 1 or c >= 1:
                        pe.wait_ge(yT_out, n.val(NCH, c))
                    for t in range(CH):
                        ins = pe.transpose(pu[:, t * TOK:(t + 1) * TOK], yn[:, b, t, :], idn[0:TOK, 0:TOK])
                    ins.then_inc(y_turned, 1)
                    if first >= 1 or c >= 2:
                        hold(pe, x3_made, n.val(NCH, c - 1), ticks)
                    pe.wait_ge(yT_out, n.val(NCH, c + 1))
                    for t in range(CH):
                        ins = pe.matmul(pz[0:TOK, b, t * C:(t + 1) * C], yT[:, b, t * TOK:(t + 1) * TOK], wpg[:],
                                        start=True, stop=True)
                    ins.then_inc(projected, 1)
                if last == -1:
                    gram_of(n, NCH - 1, first, last)

            run_steps(pe, N, U, step)


def recurrent_stage(nc, B, x3, gram, W, w_t, v_t, gamma, beta, ident, out):
    TC = 16
    N = PIX // TC
    COLS_ = TC * B
    SUB = 4
    TT = TC // SUB
    ROWS = TT * B
    EPS, EPS_T = 1e-5, 1e-5
    COUNT = float(B * PIX)
    U = 4
    S = Stage(nc, "rec")
    with S.ctx:
        idn = S.sb("idn", [P, P])
        wnat = S.sb("wnat", [C, C])
        wsc = S.sb("wsc", [C, C])
        wt = S.sb("wt", [C, C])
        vt = S.sb("vt", [C, C])
        gr = S.sb("gr", [C, C + 1])
        ones = S.sb("ones", [C, 1])
        gcol, bcol = S.sb("gcol", [C, 1]), S.sb("bcol", [C, 1])
        prod = S.sb("prod", [C, C])
        wbn = S.sb("wbn", [C, C])
        cols = S.sb("cols", [C, 8])
        halfneg = S.sb("halfneg", [P, SUB])
        xin = S.sb("xin", [ROWS, 4, SUB, C])
        stat = S.sb("stat", [ROWS, SUB, 6])
        mv = S.sb("mv", [ROWS, 2, SUB, 2])
        rstd = S.sb("rstd", [ROWS, 2, SUB])
        xn = S.sb("xn", [ROWS, 2, SUB, C])
        xT = S.sb("xT", [C, 2, COLS_])
        yT = S.sb("yT", [C, 2, COLS_])
        res = S.sb("res", [ROWS, 2, SUB, C])
        y0 = S.sb("y0", [C, B])

        pin = S.ps("pin", [P, BANK])
        pout = S.ps("pout", [P, BANK])
        ph = S.ps("ph", [P, 2, BANK])
        ps = S.ps("ps", [P, BANK])

        ticks = S.sem("ticks")
        const_in, filled, setup = S.sem("const_in"), S.sem("filled"), S.sem("setup")
        setup_pe, setup_pool = S.sem("setup_pe"), S.sem("setup_pool")
        x_in = S.sems("x_in", 4)
        stats_part, stats, eps_added, rstd_done, normed = (S.sem(k) for k in ("stats_part", "stats", "eps_added", "rstd_done", "normed"))
        turned, xT_out, driven = S.sem("turned"), S.sem("xT_out"), S.sem("driven")
        added, moved = S.sem("added"), S.sem("moved")
        y_turned, res_made = S.sem("y_turned"), S.sem("res_made")
        stored = S.sems("stored", 2)
        block = S.block()
        CONSTS = 16 * 7

        @block.sync
        def _(sp):
            for dst, src in ((idn[:], ident), (wnat[:], W), (wt[:], w_t), (vt[:], v_t), (gr[:], gram),
                             (gcol[:], dram(gamma, 0, [(1, C), (1, 1)])), (bcol[:], dram(beta, 0, [(1, C), (1, 1)]))):
                sp.dma_start(dst, src).then_inc(const_in, 16)

            def move(tensor, n, tile, sub, sem):
                view = dram(tensor, n.val(TC * C, sub * TT * C), [(C, TT), (PIX * C, B), (1, C)])
                return (sp.dma_start(tile, view) if tensor is x3 else sp.dma_start(view, tile)).then_inc(sem, 16)

            def load(n):
                for sub in range(SUB):
                    move(x3, n, xin[:, n.slot(4), sub, :], sub, x_in[n.slot(4)])

            def step(n, first, last):
                if first == 0:
                    for k in range(3):
                        load(n + k)
                if last < -3:
                    if first >= 1:
                        hold(sp, res_made, n.val(), ticks)
                    load(n + 3)
                hold(sp, res_made, n.val(1, 1), ticks)
                for sub in range(SUB):
                    move(out, n, res[:, n.slot(2), sub, :], sub, stored[n.slot(2)])

            run_steps(sp, N, U, step)
            for s in range(2):
                sp.wait_ge(stored[s], 16 * SUB * (N // 2))

        @block.gpsimd
        def _(pool):
            pool.memset(halfneg[:], -0.5).then_inc(filled, 1)
            pool.memset(ones[:], 1.0).then_inc(filled, 1)
            pool.memset(y0[:], 0.0).then_inc(filled, 1)
            pool.wait_ge(filled, 3)
            pool.wait_ge(setup, 5)
            pool.tensor_tensor(cols[:, 4:5], cols[:, 3:4], halfneg[:, 0:1], ALU.pow).then_inc(setup_pool, 1)

            def norm(n):
                a = n.slot(2)
                hold(pool, stats, n.val(1, 1), ticks)
                pool.tensor_scalar(rstd[:, a, :], mv[:, a, :, 1], EPS_T, None, ALU.add).then_inc(eps_added, 1)
                pool.wait_ge(eps_added, n.val(1, 1))
                pool.tensor_tensor(rstd[:, a, :], rstd[:, a, :], halfneg[0:ROWS, :], ALU.pow).then_inc(rstd_done, 1)
                hold(pool, rstd_done, n.val(1, 1), ticks)
                for t in range(SUB):
                    ins = pool.tensor_scalar(xn[:, a, t, :], xin[:, n.slot(4), t, :], mv[:, a, t, 0:1],
                                             rstd[:, a, t:t + 1], ALU.subtract, ALU.mult)
                ins.then_inc(normed, 1)

            def step(n, first, last):
                if first == 0:
                    norm(n)
                    norm(n + 1)
                if last < -2:
                    pool.wait_ge(turned, n.val(1, 1))
                    norm(n + 2)

            run_steps(pool, N, U, step)

        @block.scalar
        def _(act):
            act.wait_ge(setup, 9)

            def step(n, first, last):
                a = n.slot(2)
                for t in range(TC):
                    cs = slice(t * B, (t + 1) * B)
                    if t == 0 and first >= 2:
                        act.wait_ge(y_turned, n.val(1, -1))
                        act.sem_inc(ticks, 1)
                    act.wait_ge(added, n.val(TC, t + 1))
                    act.activation(yT[:, a, cs], ph[:, a, cs], ACT.Sigmoid, bias=cols[:, 7:8]).then_inc(moved, 1)

            run_steps(act, N, U, step)

        @block.vector
        def _(dve):
            dve.wait_ge(const_in, CONSTS)
            done = [0]

            def then(ins):
                ins.then_inc(setup, 1)
                done[0] += 1
                dve.wait_ge(setup, done[0])

            dve.wait_ge(setup_pe, 1)
            then(dve.tensor_tensor(prod[:], ps[:, 0:C], wt[:], ALU.mult))
            dve.wait_ge(setup_pe, 3)
            then(dve.tensor_scalar(cols[:, 0:2], ps[:, C:C + 2], 1.0 / COUNT, None, ALU.mult))
            then(dve.tensor_tensor(cols[:, 2:3], cols[:, 0:1], cols[:, 0:1], ALU.mult))
            then(dve.tensor_tensor(cols[:, 3:4], cols[:, 1:2], cols[:, 2:3], ALU.subtract))
            then(dve.tensor_scalar(cols[:, 3:4], cols[:, 3:4], EPS, None, ALU.add))
            dve.wait_ge(setup_pool, 1)
            then(dve.tensor_tensor(cols[:, 5:6], cols[:, 4:5], gcol[:], ALU.mult))
            then(dve.tensor_tensor(cols[:, 6:7], cols[:, 5:6], cols[:, 0:1], ALU.mult))
            then(dve.tensor_tensor(cols[:, 7:8], bcol[:], cols[:, 6:7], ALU.subtract))
            then(dve.tensor_scalar(wsc[:], wnat[:], cols[:, 5:6], None, ALU.mult))
            dve.wait_ge(setup_pe, 4)
            then(dve.tensor_copy(wbn[:], ps[:, 128:256]))

            def layer_stats(n):
                a, s = n.slot(2), n.slot(4)
                dve.wait_ge(x_in[s], n.turn(4, 16 * SUB, 16 * SUB))
                for t in range(SUB):
                    dve.bn_stats(stat[:, t, :], xin[:, s, t, :]).then_inc(stats_part, 1)
                hold(dve, stats_part, n.val(SUB, SUB), ticks)
                for t in range(SUB):
                    ins = dve.bn_aggr(mv[:, a, t, :], stat[:, t, :])
                ins.then_inc(stats, 1)

            def drive(n):
                dve.wait_ge(turned, n.val(1, 1))
                dve.tensor_copy(xT[:, n.slot(2), :], pin[:, 0:COLS_]).then_inc(xT_out, 1)

            def finish(n, first):
                if first >= 2:
                    dve.wait_ge(stored[n.slot(2)], n.turn(2, 16 * SUB))
                    dve.sem_inc(ticks, 1)
                dve.wait_ge(y_turned, n.val(1, 1))
                dve.tensor_tensor(res[:, n.slot(2), :, :], pout[0:ROWS, :].rearrange("p (s c) -> p s c", c=C),
                                  xin[:, n.slot(4), :, :], ALU.add).then_inc(res_made, 1)

            def step(n, first, last):
                if first == 0:
                    layer_stats(n)
                    dve.wait_ge(stats, n.val(1, 1))
                    layer_stats(n + 1)
                    drive(n)
                if last < -2:
                    hold(dve, normed, n.val(1, 1), ticks)
                    dve.wait_ge(stats, n.val(1, 2))
                    layer_stats(n + 2)
                if first >= 1:
                    finish(n - 1, first - 1)
                if last < -1:
                    drive(n + 1)
                if last == -1:
                    finish(n, first)

            run_steps(dve, N, U, step)

        @block.tensor
        def _(pe):
            pe.wait_ge(const_in, CONSTS)
            pe.matmul(ps[:, 0:C], gr[:, 0:C], wt[:], start=True, stop=True).then_inc(setup_pe, 1)
            pe.wait_ge(filled, 3)
            pe.wait_ge(setup, 1)
            pe.matmul(ps[:, C:C + 1], wt[:], gr[:, C:C + 1], start=True, stop=True).then_inc(setup_pe, 1)
            pe.matmul(ps[:, C + 1:C + 2], prod[:], ones[:], start=True, stop=True).then_inc(setup_pe, 1)
            pe.wait_ge(setup, 9)
            pe.transpose(ps[:, 128:256], wsc[:], idn[:]).then_inc(setup_pe, 1)

            def turn_in(n, sub):
                if sub == 0:
                    pe.wait_ge(normed, n.val(1, 1))
                ins = pe.transpose(pin[:, sub * ROWS:(sub + 1) * ROWS], xn[:, n.slot(2), sub, :], idn[0:ROWS, 0:ROWS])
                if sub == SUB - 1:
                    ins.then_inc(turned, 1)

            def drive(n, sub):
                if sub == 0:
                    pe.wait_ge(xT_out, n.val(1, 1))
                pe.matmul(ph[:, n.slot(2), sub * ROWS:(sub + 1) * ROWS], wbn[:], xT[:, n.slot(2), sub * ROWS:(sub + 1) * ROWS],
                          start=(sub == 0), stop=False, skip_group_check=True)

            def turn_out(n, sub, first):
                if sub == 0 and first >= 1:
                    pe.wait_ge(res_made, n.val())
                ins = pe.transpose(pout[0:ROWS, sub * C:(sub + 1) * C], yT[:, n.slot(2), sub * ROWS:(sub + 1) * ROWS], idn[:])
                if sub == SUB - 1:
                    ins.then_inc(y_turned, 1)

            pe.wait_ge(setup, 10)

            def step(n, first, last):
                a = n.slot(2)
                if first == 0:
                    for sub in range(SUB):
                        turn_in(n, sub)
                    for sub in range(SUB):
                        drive(n, sub)
                for t in range(TC):
                    cs = slice(t * B, (t + 1) * B)
                    if t == 0 and first == 0:
                        pe.matmul(ph[:, a, cs], vt[:], y0[:], start=False, stop=True, skip_group_check=True).then_inc(added, 1)
                    else:
                        before = yT[:, a, (t - 1) * B:t * B] if t else yT[:, 1 - a, (TC - 1) * B:TC * B]
                        pe.wait_ge(moved, n.val(TC, t))
                        pe.matmul(ph[:, a, cs], vt[:], before, start=False, stop=True, skip_group_check=True).then_inc(added, 1)
                    if t < SUB and first >= 1:
                        turn_out(n - 1, t, first - 1)
                    if SUB <= t < 2 * SUB and last < -1:
                        turn_in(n + 1, t - SUB)
                    if TC - 5 <= t < TC - 1 and last < -1:
                        drive(n + 1, t - (TC - 5))
                if last == -1:
                    pe.wait_ge(moved, n.val(TC, TC))
                    for sub in range(SUB):
                        turn_out(n, sub, first)

            run_steps(pe, N, U, step)


def metaformer_program(nc, B, a):
    def scratch(name, *shape):
        return nc.dram_tensor(name, shape, F32).ap()

    x1 = scratch("x1", B * PIX, C)
    x2 = scratch("x2", B * PIX, C)
    x3 = scratch("x3", B * PIX, C)
    q = scratch("q", B * PIX, C)
    c0 = scratch("c0", GROUPS, P, B, ODD, QUAD)
    gates = scratch("gates", P, 4, B, EVEN)
    ctx_all = scratch("ctx_all", GROUPS, P, B, QUAD, EVEN)
    gram = scratch("gram", C, C + 1)
    attention_stage(nc, B, a["x_windows"], a["w_qkv_t"], a["w_proj_t"], a["b_proj"], a["rpb_rev"],
                    a["shift_mask"], a["ident"], x1)
    expert_stage(nc, B, x1, a["router_w"], a["router_b"], a["expert_w"], a["expert_b"], a["erank"], a["ident"], x2)
    focal_input_stage(nc, B, x2, a["Wf"], a["bf"], a["edge_mask"], a["ident"], q, c0, gates)
    convolution_stage(nc, B, c0, gates, [a["k0"], a["k1"], a["k2"]], a["gap_mask"], ctx_all)
    focal_output_stage(nc, B, ctx_all, q, x2, a["Wh"], a["bh"], a["gamma"], a["beta"], a["Wp"], a["bp"],
                       a["ident"], x3, gram)
    recurrent_stage(nc, B, x3, gram, a["ffn_W"], a["ffn_w_t"], a["ffn_v_t"], a["ffn_gamma"], a["ffn_beta"],
                    a["ident"], a["out"])


def _shape_constants(np):
    tok = np.arange(WTOK)
    row, col = tok // WS, tok % WS
    shift = np.zeros((P, 2, 4, WTOK), np.float32)
    for last_band in range(2):
        for w in range(8):
            part = (row >= WS - SHIFT) * last_band * 2 + (col >= WS - SHIFT) * (w == 7)
            p0 = (w % 2) * 64
            shift[p0:p0 + WTOK, last_band, w // 2] = np.where(part[:, None] != part[None, :], -100.0, 0.0)
    p = np.arange(P)
    pixel = p % ROW < IMG
    edge = np.stack([pixel & (p >= ROW), pixel, pixel, pixel & (p < ROW)], 1).astype(np.float32)
    return {
        "ident": np.eye(P, dtype=np.float32),
        "shift_mask": shift.reshape(P, 2, 4 * WTOK),
        "edge_mask": edge,
        "gap_mask": pixel.astype(np.float32)[:, None],
        "erank": np.tile(np.arange(EXPERTS, 0, -1).astype(np.float32), (P, 1)),
    }


def kernel(**inputs):
    import numpy as np
    import concourse.bacc as bacc
    from concourse.bass_utils import run_bass_kernel_spmd as run

    i = {k: np.asarray(v) for k, v in inputs.items()}
    x = i["x"]
    B = x.shape[0]
    rolled = np.roll(x, (-SHIFT, -SHIFT), (1, 2))
    windows = rolled.reshape(B, 8, WS, 8, WS, C).transpose(0, 1, 3, 2, 4, 5).reshape(B * 64, WTOK, C)
    arrays = {
        "x_windows": windows,
        "w_qkv_t": i["L0_conv_w_qkv"].T,
        "w_proj_t": i["L0_conv_w_proj"].T,
        "b_proj": i["L0_conv_b_proj"],
        "rpb_rev": i["L0_conv_rpb_table"][::-1].T,
        "router_w": i["L0_ffn_router_w"],
        "router_b": i["L0_ffn_router_b"],
        "expert_w": i["L0_ffn_expert_w"],
        "expert_b": i["L0_ffn_expert_b"],
        "Wf": i["L1_conv_Wf"],
        "bf": i["L1_conv_bf"],
        "Wh": i["L1_conv_Wh"],
        "bh": i["L1_conv_bh"],
        "gamma": i["L1_conv_gamma"],
        "beta": i["L1_conv_beta"],
        "Wp": i["L1_conv_Wp"],
        "bp": i["L1_conv_bp"],
        "ffn_W": i["L1_ffn_W"],
        "ffn_w_t": i["L1_ffn_W"].T,
        "ffn_v_t": i["L1_ffn_V"].T,
        "ffn_gamma": i["L1_ffn_gamma"],
        "ffn_beta": i["L1_ffn_beta"],
        **_shape_constants(np),
    }
    for k, size in enumerate(TAPS):
        taps = i[f"L1_conv_k{k}"].reshape(size, size, C)
        arrays[f"k{k}"] = taps[::-1, ::-1].transpose(2, 0, 1)
    arrays = {k: np.ascontiguousarray(v) for k, v in arrays.items()}

    nc = bacc.Bacc("TRN2", target_bir_lowering=False, num_devices=1)
    args = {k: nc.dram_tensor(k, v.shape, F32, kind="ExternalInput").ap() for k, v in arrays.items()}
    args["out"] = nc.dram_tensor("out", (B, IMG, IMG, C), F32, kind="ExternalOutput").ap()
    metaformer_program(nc, B, args)
    return run(nc, [arrays], core_ids=[0]).results[0]["out"]
```

```python
from contextlib import ExitStack

import concourse.bass as bass
from concourse import mybir

F32 = mybir.dt.float32
ALU = mybir.AluOpType
ACT = mybir.ActivationFunctionType
AX = mybir.AxisListType

P = 128
C = 128
IMG = 56
PIX = IMG * IMG
WS = 7
SHIFT = 3
WTOK = WS * WS
HEADS = 4
HD = C // HEADS
EXPERTS = 8
TAPS = (3, 5, 7)
BANK = 512


MANY = 1 << 20


class Step:

    def __init__(self, loop, unroll, off):
        self.loop, self.unroll, self.off = loop, unroll, off
        self.is_static = isinstance(loop, int)

    def __add__(self, k):
        return Step(self.loop, self.unroll, self.off + k)

    def __sub__(self, k):
        return self + -k

    def val(self, scale=1, plus=0):
        return self.loop * (self.unroll * scale) + (self.off * scale + plus)

    def slot(self, n):
        assert self.unroll % n == 0
        return self.off % n

    def turn(self, n, scale=1, plus=0):
        return self.loop * (self.unroll // n * scale) + (self.off // n * scale + plus)


def run_steps(eng, count, unroll, step, ahead=3):
    rounds = (count - 1 - ahead) // unroll
    if rounds < 3:
        for n in range(count):
            step(Step(0, unroll, n), n, n - count)
        return
    for n in range(unroll):
        step(Step(0, unroll, n), n, n - count)
    with eng.Fori(1, rounds) as it:
        for u in range(unroll):
            step(Step(it, unroll, u), MANY, -MANY)
    for n in range(rounds * unroll, count):
        step(Step(0, unroll, n), n, n - count)


def hold(eng, sem, value, ticks):
    eng.wait_ge(sem, value)
    eng.sem_inc(ticks, 1)


class Stage:

    def __init__(self, nc, name):
        self.nc, self.name, self.ctx, self.used = nc, name, ExitStack(), []

    def sb(self, name, shape):
        return self.ctx.enter_context(self.nc.sbuf_tensor(f"{self.name}_{name}", shape, F32))

    def ps(self, name, shape):
        return self.ctx.enter_context(self.nc.psum_tensor(f"{self.name}_{name}", shape, F32))

    def sem(self, name):
        self.used.append(self.ctx.enter_context(self.nc.semaphore(f"{self.name}_{name}")))
        return self.used[-1]

    def sems(self, name, n):
        return [self.sem(f"{name}{i}") for i in range(n)]

    def clear(self):
        with self.nc.Block() as block:
            @block.gpsimd
            def _(pool):
                for sem in self.used:
                    pool.sem_clear(sem)

    def block(self):
        self.ctx.callback(self.clear)
        return self.ctx.enter_context(self.nc.Block())


def dram(ap, offset, dims):
    return bass.AP(ap.tensor, offset, [list(d) for d in dims])


def row_to_all(ap, n, offset=0):
    return dram(ap, offset, [(0, P), (1, n)])


def attention_stage(nc, B, x_win, w_qkv_t, w_proj_t, b_proj, rpb_rev, shift_mask, ident, x1):
    N = B * 8
    PAIRS, W = 4, 8
    SCALE = float(HD) ** -0.5
    EPS = 1e-6
    U = 8
    S = Stage(nc, "att")
    with S.ctx:
        idn = S.sb("idn", [P, P])
        wqkv = S.sb("wqkv", [C, 3 * C])
        wproj = S.sb("wproj", [C, C])
        bproj = S.sb("bproj", [P, C])
        halfneg = S.sb("halfneg", [P, PAIRS])
        mask = S.sb("mask", [P, 2, PAIRS * WTOK])
        bias = S.sb("bias", [P, 2, HEADS, PAIRS * WTOK])
        relb = S.sb("relb", [P, HEADS, WTOK])
        xin = S.sb("xin", [P, 8, PAIRS, C])
        stat = S.sb("stat", [P, 4, PAIRS, 6])
        mv = S.sb("mv", [P, 4, PAIRS, 2])
        rstd = S.sb("rstd", [P, 4, PAIRS])
        xn = S.sb("xn", [P, 4, PAIRS, C])
        xnT = S.sb("xnT", [C, W * WTOK])
        qT = S.sb("qT", [C, W * WTOK])
        kT = S.sb("kT", [C, W * WTOK])
        vv = S.sb("vv", [P, 2, W, 2 * HD])
        sc = S.sb("sc", [P, PAIRS * HEADS, 64])
        pr = S.sb("pr", [P, PAIRS * HEADS, 64])
        mx = S.sb("mx", [P, PAIRS * HEADS])
        sm = S.sb("sm", [P, PAIRS * HEADS])
        rs = S.sb("rs", [P, PAIRS * HEADS])
        prT = S.sb("prT", [P, 2, PAIRS, P])
        oT = S.sb("oT", [C, W, 64])
        x1s = S.sb("x1s", [P, 2, PAIRS, C])

        rel_dram = nc.dram_tensor("rel_dram", (HEADS, WTOK, WTOK), F32).ap()

        psc = S.ps("psc", [P, HEADS, BANK])
        pf = S.ps("pf", [P, 2, BANK])
        pb = S.ps("pb", [P, 2, BANK])

        const_in = S.sem("const_in")
        ticks = S.sem("ticks")
        rel_in, rel_spread = S.sem("rel_in"), S.sem("rel_spread")
        zeroed_v = S.sem("zeroed_v")
        zeroed_p = S.sem("zeroed_p")
        rel_zero = S.sem("rel_zero")
        bias_built = S.sem("bias_built")
        x_in = S.sems("x_in", 8)
        stats_part = S.sem("stats_part")
        stats = S.sem("stats")
        eps_added = S.sem("eps_added")
        rstd_done = S.sem("rstd_done")
        centred = S.sem("centred")
        normed = S.sem("normed")
        bproj_added = S.sem("bproj_added")
        f0_full, f1_full = S.sem("f0_full"), S.sem("f1_full")
        xT_out, q_out, k_out, v_out = (S.sem(f"{n}_out") for n in ("xT", "q", "k", "v"))
        scored = S.sem("scored")
        biased = S.sem("biased")
        maxed = S.sem("maxed")
        shifted = S.sem("shifted")
        exped = S.sem("exped")
        summed = S.sem("summed")
        inverted = S.sem("inverted")
        probs = S.sem("probs")
        turned = S.sems("turned", 2)
        prT_out = S.sems("prT_out", 2)
        attended = S.sem("attended")
        oT_out = S.sem("oT_out")
        projected = S.sem("projected")
        x1_ready = S.sem("x1_ready")
        x1_out = S.sems("x1_out", 2)
        block = S.block()

        @block.sync
        def _(sp):
            for dst, src in ((idn[:], ident), (wqkv[:], w_qkv_t), (wproj[:], w_proj_t),
                             (bproj[:], row_to_all(b_proj, C)), (mask[:], shift_mask)):
                sp.dma_start(dst, src).then_inc(const_in, 16)
            SIDE = 2 * WS - 1
            for h in range(HEADS):
                for r1 in range(WS):
                    off = h * SIDE * SIDE + (WS - 1 - r1) * SIDE + WS - 1
                    sp.dma_start(dram(rel_dram, (h * WTOK + r1 * WS) * WTOK, [(WS, WS), (WTOK, WS), (1, WS)]),
                                 dram(rpb_rev, off, [(SIDE, WS), (-1, WS), (1, WS)])).then_inc(rel_spread, 16)
            sp.wait_ge(rel_spread, 16 * HEADS * WS)
            sp.wait_ge(rel_zero, 1)
            for base in (0, 64):
                sp.dma_start(relb[base:base + WTOK, :, :],
                             dram(rel_dram, 0, [(WTOK, WTOK), (WTOK * WTOK, HEADS), (1, WTOK)])).then_inc(rel_in, 16)

            def load(n):
                s = n.slot(8)
                for odd in range(2):
                    src = dram(x_win, n.val(W * WTOK * C, odd * WTOK * C),
                               [(C, WTOK), (2 * WTOK * C, PAIRS), (1, C)])
                    sp.dma_start(xin[odd * 64:odd * 64 + WTOK, s, :, :], src).then_inc(x_in[s], 16)

            def step(n, first, last):
                if first == 0:
                    for k in range(6):
                        load(n + k)
                if last < -6:
                    if first >= 2:
                        hold(sp, x1_ready, n.val(1, -1), ticks)
                    load(n + 6)
                hold(sp, x1_ready, n.val(1, 1), ticks)
                for pair in range(PAIRS):
                    for odd in range(2):
                        off = n.val(WS * IMG * C, (2 * pair + odd) * WS * C)
                        sp.dma_start(dram(x1, off, [(IMG * C, WS), (C, WS), (1, C)]),
                                     x1s[odd * 64:odd * 64 + WTOK, n.slot(2), pair, :]).then_inc(x1_out[n.slot(2)], 16)

            sp.wait_ge(zeroed_p, 8)
            run_steps(sp, N, U, step, 6)
            for s in range(2):
                sp.wait_ge(x1_out[s], 16 * W * ((N + 1 - s) // 2))

        @block.gpsimd
        def _(pool):
            for s in range(8):
                pool.memset(xin[:, s, :, :], 0.0).then_inc(zeroed_p, 1)
            pool.memset(halfneg[:], -0.5).then_inc(zeroed_p, 1)
            pool.memset(oT[:], 0.0).then_inc(zeroed_p, 1)
            pool.memset(pr[:], 0.0).then_inc(zeroed_p, 1)
            pool.wait_ge(zeroed_p, 11)
            pool.wait_ge(const_in, 80)

            def norm(n):
                a, s = n.slot(4), n.slot(8)
                hold(pool, stats, n.val(1, 1), ticks)
                pool.tensor_scalar(rstd[:, a, :], mv[:, a, :, 1], EPS, None, ALU.add).then_inc(eps_added, 1)
                pool.wait_ge(eps_added, n.val(1, 1))
                pool.tensor_tensor(rstd[:, a, :], rstd[:, a, :], halfneg[:], ALU.pow).then_inc(rstd_done, 1)
                pool.wait_ge(rstd_done, n.val(1, 1))
                pool.sem_inc(ticks, 1)
                for t in range(PAIRS):
                    ins = pool.tensor_scalar(xn[:, a, t, :], xin[:, s, t, :], mv[:, a, t, 0:1],
                                             rstd[:, a, t:t + 1], ALU.subtract, ALU.mult)
                ins.then_inc(normed, 1)
                pool.wait_ge(normed, n.val(1, 1))
                pool.tensor_tensor(xin[:, s, :, :], xin[:, s, :, :],
                                   bproj[:].unsqueeze(1).to_broadcast([P, PAIRS, C]), ALU.add).then_inc(bproj_added, 1)

            def step(n, first, last):
                if first == 0:
                    norm(n)
                    norm(n + 1)
                if last < -2:
                    if first >= 2:
                        pool.wait_ge(xT_out, n.val(1, -1))
                        pool.sem_inc(ticks, 1)
                    norm(n + 2)

            run_steps(pool, N, U, step)

        @block.scalar
        def _(act):
            def copy(out, in_):
                return act.activation(out, in_, ACT.Copy)

            def tokens(n):
                act.wait_ge(f0_full, n.val(2, 1))
                copy(xnT[:].rearrange("c (w t) -> c w t", t=WTOK),
                     pf[:, 0, :].rearrange("c (w t) -> c w t", t=64)[:, :, 0:WTOK]).then_inc(xT_out, 1)

            def qk(n):
                act.wait_ge(f1_full, n.val(2, 1))
                act.activation(qT[:], pf[:, 1, 0:W * WTOK], ACT.Copy, scale=SCALE).then_inc(q_out, 1)
                act.wait_ge(f0_full, n.val(2, 2))
                copy(kT[:], pf[:, 0, 0:W * WTOK]).then_inc(k_out, 1)

            def values(n):
                act.wait_ge(f1_full, n.val(2, 2))
                copy(vv[:, n.slot(2), :, :].rearrange("t w c -> t (w c)"), pf[:, 1, :]).then_inc(v_out, 1)

            def probs_by_key(n):
                for half in range(2):
                    act.wait_ge(turned[half], n.val(1, 1))
                    copy(prT[:, half, :, :].rearrange("t q i -> t (q i)"), pb[:, half, :]).then_inc(prT_out[half], 1)

            def exp(n):
                act.wait_ge(shifted, n.val(1, 1))
                act.activation(pr[:, :, 0:WTOK], sc[:, :, 0:WTOK], ACT.Exp).then_inc(exped, 1)

            def attended_out(n):
                act.wait_ge(attended, n.val(1, 1))
                copy(oT[:, :, 0:WTOK], pb[:, 0, 0:W * WTOK].rearrange("c (w t) -> c w t", t=WTOK)).then_inc(oT_out, 1)

            act.wait_ge(zeroed_p, 11)

            def step(n, first, last):
                if first == 0:
                    tokens(n)
                    qk(n)
                    values(n)
                if last < -1:
                    tokens(n + 1)
                if first >= 1:
                    probs_by_key(n - 1)
                if last < -1:
                    qk(n + 1)
                exp(n)
                if first >= 1:
                    attended_out(n - 1)
                if last < -1:
                    values(n + 1)
                if last == -1:
                    probs_by_key(n)
                    attended_out(n)

            run_steps(act, N, U, step)

        @block.vector
        def _(dve):
            dve.memset(relb[:], 0.0).then_inc(rel_zero, 1)
            dve.memset(psc[:], 0.0).then_inc(zeroed_v, 1)
            dve.memset(pf[:], 0.0).then_inc(zeroed_v, 1)
            dve.wait_ge(zeroed_p, 11)
            dve.wait_ge(const_in, 80)
            dve.wait_ge(rel_in, 32)
            for kind in range(2):
                for h in range(HEADS):
                    dve.tensor_tensor(bias[:, kind, h, :].rearrange("p (q j) -> p q j", j=WTOK),
                                      mask[:, kind, :].rearrange("p (q j) -> p q j", j=WTOK),
                                      relb[:, h, :].unsqueeze(1).to_broadcast([P, PAIRS, WTOK]),
                                      ALU.add).then_inc(bias_built, 1)

            def layer_stats(n):
                a, s = n.slot(4), n.slot(8)
                dve.wait_ge(x_in[s], n.turn(8, 32, 32))
                for t in range(PAIRS):
                    dve.bn_stats(stat[:, a, t, :], xin[:, s, t, :]).then_inc(stats_part, 1)
                hold(dve, stats_part, n.val(PAIRS, PAIRS), ticks)
                for t in range(PAIRS):
                    ins = dve.bn_aggr(mv[:, a, t, :], stat[:, a, t, :])
                ins.then_inc(stats, 1)

            def softmax_front(n, kind):
                dve.wait_ge(scored, n.val(1, 1))
                dve.tensor_tensor(sc[:].rearrange("p (q h) j -> p h q j", h=HEADS)[:, :, :, 0:WTOK],
                                  psc[:, :, 0:PAIRS * WTOK].rearrange("p h (q j) -> p h q j", j=WTOK),
                                  bias[:, kind, :, :].rearrange("p h (q j) -> p h q j", j=WTOK), ALU.add).then_inc(biased, 1)
                dve.wait_ge(biased, n.val(1, 1))
                dve.tensor_reduce(mx[:], sc[:, :, 0:WTOK], AX.X, ALU.max).then_inc(maxed, 1)
                dve.wait_ge(maxed, n.val(1, 1))
                dve.tensor_tensor(sc[:, :, 0:WTOK], sc[:, :, 0:WTOK],
                                  mx[:].unsqueeze(2).to_broadcast([P, HEADS * PAIRS, WTOK]),
                                  ALU.subtract).then_inc(shifted, 1)

            def softmax_back(n):
                dve.wait_ge(exped, n.val(1, 1))
                dve.tensor_reduce(sm[:], pr[:, :, 0:WTOK], AX.X, ALU.add).then_inc(summed, 1)
                dve.wait_ge(summed, n.val(1, 1))
                dve.reciprocal(rs[:], sm[:]).then_inc(inverted, 1)
                dve.wait_ge(inverted, n.val(1, 1))
                dve.tensor_tensor(pr[:, :, 0:WTOK], pr[:, :, 0:WTOK],
                                  rs[:].unsqueeze(2).to_broadcast([P, HEADS * PAIRS, WTOK]),
                                  ALU.mult).then_inc(probs, 1)

            def residual(n, first):
                dve.wait_ge(projected, n.val(1, 1))
                dve.wait_ge(bproj_added, n.val(1, 1))
                if first >= 2:
                    dve.wait_ge(x1_out[n.slot(2)], n.turn(2, 16 * W))
                dve.tensor_tensor(x1s[:, n.slot(2), :, :].rearrange("p q c -> p (q c)"), pb[:, 1, :],
                                  xin[:, n.slot(8), :, :].rearrange("p q c -> p (q c)"), ALU.add).then_inc(x1_ready, 1)

            dve.wait_ge(bias_built, 2 * HEADS)

            def step(n, first, last):
                kind = n.slot(8) == 7
                if first == 0:
                    for k in range(3):
                        layer_stats(n + k)
                softmax_front(n, int(kind))
                if last < -3:
                    if first >= 1:
                        dve.wait_ge(normed, n.val())
                        dve.sem_inc(ticks, 1)
                    layer_stats(n + 3)
                softmax_back(n)
                if first >= 1:
                    residual(n - 1, first - 1)
                if last == -1:
                    residual(n, first)

            run_steps(dve, N, U, step)

        @block.tensor
        def _(pe):
            pe.wait_ge(const_in, 80)
            pe.wait_ge(zeroed_v, 2)
            pe.wait_ge(zeroed_p, 11)

            def turn(n, first):
                pe.wait_ge(normed, n.val(1, 1))
                if first >= 1:
                    pe.wait_ge(k_out, n.val())
                for t in range(PAIRS):
                    ins = pe.transpose(pf[:, 0, t * P:(t + 1) * P], xn[:, n.slot(4), t, :], idn[:])
                ins.then_inc(f0_full, 1)

            def qk(n, first):
                pe.wait_ge(xT_out, n.val(1, 1))
                if first >= 1:
                    pe.wait_ge(v_out, n.val())
                pe.matmul(pf[:, 1, 0:W * WTOK], wqkv[:, 0:C], xnT[:], start=True, stop=True).then_inc(f1_full, 1)
                pe.matmul(pf[:, 0, 0:W * WTOK], wqkv[:, C:2 * C], xnT[:], start=True, stop=True).then_inc(f0_full, 1)

            def values(n):
                pe.wait_ge(q_out, n.val(1, 1))
                wv = wqkv[:, 2 * C:3 * C].rearrange("c (g o d) -> c o g d", o=2, d=HD)
                for w in range(W):
                    for odd in range(2):
                        ins = pe.matmul(pf[odd * 64:odd * 64 + WTOK, 1, w * 64:(w + 1) * 64],
                                        xnT[:, w * WTOK:(w + 1) * WTOK], wv[:, odd], start=True, stop=True)
                ins.then_inc(f1_full, 1)

            def scores(n, first):
                pe.wait_ge(k_out, n.val(1, 1))
                if first >= 1:
                    hold(pe, biased, n.val(), ticks)
                for pair in range(PAIRS):
                    for h in range(HEADS):
                        for w in (2 * pair, 2 * pair + 1):
                            p0 = (w % 2) * 64
                            ins = pe.matmul(psc[p0:p0 + WTOK, h, pair * WTOK:(pair + 1) * WTOK],
                                            qT[h * HD:(h + 1) * HD, w * WTOK:(w + 1) * WTOK],
                                            kT[h * HD:(h + 1) * HD, w * WTOK:(w + 1) * WTOK], start=True, stop=True)
                ins.then_inc(scored, 1)

            def turn_probs(n, first):
                hold(pe, probs, n.val(1, 1), ticks)
                if first >= 1:
                    pe.wait_ge(oT_out, n.val())
                for half in range(2):
                    if half == 1 and first >= 1:
                        hold(pe, x1_ready, n.val(), ticks)
                    for pair in range(PAIRS):
                        at = pair * HEADS + 2 * half
                        ins = pe.transpose(pb[:, half, pair * P:(pair + 1) * P],
                                           pr[:, at:at + 2, :].rearrange("p h j -> p (h j)"), idn[:])
                    ins.then_inc(turned[half], 1)

            def attend(n):
                hold(pe, v_out, n.val(1, 1), ticks)
                for half in range(2):
                    hold(pe, prT_out[half], n.val(1, 1), ticks)
                for w in range(W):
                    pair, i0 = w // 2, (w % 2) * 64
                    for h in range(HEADS):
                        k0, g = (h % 2) * 64, h // 2
                        ins = pe.matmul(pb[h * HD:(h + 1) * HD, 0, w * WTOK:(w + 1) * WTOK],
                                        vv[k0:k0 + WTOK, n.slot(2), w, g * HD:(g + 1) * HD],
                                        prT[k0:k0 + WTOK, g, pair, i0:i0 + WTOK], start=True, stop=True)
                ins.then_inc(attended, 1)

            def project(n):
                pe.wait_ge(oT_out, n.val(1, 1))
                for pair in range(PAIRS):
                    ins = pe.matmul(pb[:, 1, pair * C:(pair + 1) * C],
                                    oT[:, 2 * pair:2 * pair + 2, :].rearrange("c w t -> c (w t)"), wproj[:],
                                    start=True, stop=True)
                ins.then_inc(projected, 1)

            def step(n, first, last):
                if first == 0:
                    turn(n, 0)
                    qk(n, 0)
                    values(n)
                if last < -1:
                    turn(n + 1, 1)
                scores(n, first)
                if first >= 1:
                    turn_probs(n - 1, first - 1)
                if last < -1:
                    qk(n + 1, 1)
                if first >= 1:
                    attend(n - 1)
                if last < -1:
                    values(n + 1)
                if first >= 1:
                    project(n - 1)
                if last == -1:
                    turn_probs(n, first)
                    attend(n)
                    project(n)

            run_steps(pe, N, U, step)


def expert_stage(nc, B, x1, router_w, router_b, expert_w, expert_b, erank, ident, x2):
    T = 7
    GROUP = T * P
    N = B * PIX // GROUP
    EPS = 1e-5
    E = EXPERTS
    NOT_CHOSEN = -1e38
    U = 6
    S = Stage(nc, "moe")
    with S.ctx:
        idn = S.sb("idn", [P, P])
        wr = S.sb("wr", [C, E])
        br = S.sb("br", [P, E])
        we = S.sb("we", [C, E, C])
        be = S.sb("be", [E, C])
        rank = S.sb("rank", [P, E])
        halfneg = S.sb("halfneg", [P, T])
        xin = S.sb("xin", [P, 3, T, C])
        stat = S.sb("stat", [P, 2, T, 6])
        mv = S.sb("mv", [P, 2, T, 2])
        rstd = S.sb("rstd", [P, 2, T])
        xn = S.sb("xn", [P, 2, T, C])
        xnT = S.sb("xnT", [C, 2, T, P])
        logit = S.sb("logit", [P, T, E])
        rest = S.sb("rest", [P, T, E])
        hit = S.sb("hit", [P, 2, T, E])
        ranked = S.sb("ranked", [P, 2, T, E])
        one = S.sb("one", [P, 2, T, E])
        best = S.sb("best", [P, 2, T])
        top = S.sb("top", [P, 2, T])
        gap = S.sb("gap", [P, T])
        second = S.sb("second", [P, T])
        total = S.sb("total", [P, T])
        share = S.sb("share", [P, 2, T])
        part = S.sb("part", [P, 2, T, E])
        gate = S.sb("gate", [P, 2, T, E])
        gateT = S.sb("gateT", [E, T, P])
        acc = S.sb("acc", [P, 3, T, C])
        odd = S.sb("odd", [P, 2, C])

        px = S.ps("px", [P, 2, BANK])
        pr = S.ps("pr", [P, BANK])
        pe_out = S.ps("pe_out", [P, 2, 2, BANK])

        ticks = S.sem("ticks")
        const_in = S.sem("const_in")
        filled = S.sem("filled")
        x_in = S.sems("x_in", 3)
        stats_part, stats = S.sem("stats_part"), S.sem("stats")
        eps_added, rstd_done, normed = S.sem("eps_added"), S.sem("rstd_done"), S.sem("normed")
        turned, xT_out = S.sems("turned", 2), S.sems("xT_out", 2)
        logits_made = S.sem("logits_made")
        routing = S.sem("routing")
        gap_ready, second_ready = S.sem("gap_ready"), S.sem("second_ready")
        gates_ready = S.sem("gates_ready")
        gates_turned, gT_out = S.sems("gates_turned", 2), S.sems("gT_out", 2)
        bias_made, acc_begun = S.sems("bias_made", 2), S.sems("acc_begun", 2)
        expert_done = S.sem("expert_done")
        mixing, mixed = S.sem("mixing"), S.sem("mixed")
        x2_out = S.sems("x2_out", 3)
        block = S.block()
        HALVES = ((0, 4), (4, T))
        CONSTS = 16 * 6

        @block.sync
        def _(sp):
            for dst, src in ((idn[:], ident), (wr[:], router_w), (br[:], row_to_all(router_b, E)),
                             (we[:], dram(expert_w, 0, [(C, C), (C * C, E), (1, C)])),
                             (be[:], expert_b), (rank[:], erank)):
                sp.dma_start(dst, src).then_inc(const_in, 16)

            def load(n):
                sp.dma_start(xin[:, n.slot(3), :, :], dram(x1, n.val(GROUP * C), [(T * C, P), (1, T * C)]))\
                  .then_inc(x_in[n.slot(3)], 16)

            def step(n, first, last):
                if first == 0:
                    for k in range(min(3, N)):
                        load(n + k)
                elif last < -2:
                    hold(sp, acc_begun[1], n.val(), ticks)
                    load(n + 2)
                hold(sp, mixed, n.val(T, T), ticks)
                sp.dma_start(dram(x2, n.val(GROUP * C), [(T * C, P), (1, T * C)]), acc[:, n.slot(3), :, :])\
                  .then_inc(x2_out[n.slot(3)], 16)

            run_steps(sp, N, U, step)
            for s in range(3):
                sp.wait_ge(x2_out[s], 16 * ((N + 2 - s) // 3))

        @block.gpsimd
        def _(pool):
            pool.memset(halfneg[:], -0.5).then_inc(filled, 1)
            pool.wait_ge(filled, 1)

            def norm(n):
                a = n.slot(2)
                hold(pool, stats, n.val(1, 1), ticks)
                pool.tensor_scalar(rstd[:, a, :], mv[:, a, :, 1], EPS, None, ALU.add).then_inc(eps_added, 1)
                pool.wait_ge(eps_added, n.val(1, 1))
                pool.tensor_tensor(rstd[:, a, :], rstd[:, a, :], halfneg[:], ALU.pow).then_inc(rstd_done, 1)
                hold(pool, rstd_done, n.val(1, 1), ticks)
                for t in range(T):
                    ins = pool.tensor_scalar(xn[:, a, t, :], xin[:, n.slot(3), t, :], mv[:, a, t, 0:1],
                                             rstd[:, a, t:t + 1], ALU.subtract, ALU.mult)
                ins.then_inc(normed, 1)

            def step(n, first, last):
                if first == 0:
                    norm(n)
                    norm(n + 1)
                if last < -2:
                    pool.wait_ge(turned[1], n.val(1, 1))
                    norm(n + 2)

            run_steps(pool, N, U, step)

        @block.scalar
        def _(act):
            def front(n, first):
                if first >= 1:
                    act.wait_ge(mixed, n.val(T, -T))
                for b, (t0, t1) in enumerate(HALVES):
                    act.wait_ge(turned[b], n.val(1, 1))
                    act.activation(xnT[:, n.slot(2), t0:t1, :], px[:, b, 0:(t1 - t0) * P], ACT.Copy).then_inc(xT_out[b], 1)

            def gates(n):
                act.wait_ge(gap_ready, n.val(1, 1))
                act.activation(second[:], gap[:], ACT.Exp).then_inc(second_ready, 1)
                for b, (t0, t1) in enumerate(HALVES):
                    act.wait_ge(gates_turned[b], n.val(1, 1))
                    act.activation(gateT[:, t0:t1, :], px[0:E, b, 0:(t1 - t0) * P], ACT.Copy).then_inc(gT_out[b], 1)

            def step(n, first, last):
                if first == 0:
                    front(n, 0)
                    gates(n)
                if last < -1:
                    front(n + 1, first)
                    gates(n + 1)

            run_steps(act, N, U, step)

        @block.vector
        def _(dve):
            dve.wait_ge(const_in, CONSTS)

            def layer_stats(n):
                a, s = n.slot(2), n.slot(3)
                dve.wait_ge(x_in[s], n.turn(3, 16, 16))
                for t in range(T):
                    dve.bn_stats(stat[:, a, t, :], xin[:, s, t, :]).then_inc(stats_part, 1)
                hold(dve, stats_part, n.val(T, T), ticks)
                for t in range(T):
                    ins = dve.bn_aggr(mv[:, a, t, :], stat[:, a, t, :])
                ins.then_inc(stats, 1)

            OPS = 19

            def route(n):
                done = [0]

                def then(ins):
                    ins.then_inc(routing, 1)
                    done[0] += 1
                    dve.wait_ge(routing, n.val(OPS, done[0]))

                def wide(x):
                    return x.unsqueeze(2).to_broadcast([P, T, E])

                ranks = rank[:].unsqueeze(1).to_broadcast([P, T, E])
                dve.wait_ge(logits_made, n.val(1, 1))
                then(dve.tensor_tensor(logit[:], pr[:, 0:T * E].rearrange("p (t e) -> p t e", e=E),
                                       br[:].unsqueeze(1).to_broadcast([P, T, E]), ALU.add))
                for k, x in enumerate((logit, rest)):
                    then(dve.tensor_reduce(best[:, k, :], x[:], AX.X, ALU.max))
                    then(dve.tensor_tensor(hit[:, k, :, :], x[:], wide(best[:, k, :]), ALU.is_equal))
                    then(dve.tensor_tensor(ranked[:, k, :, :], hit[:, k, :, :], ranks, ALU.mult))
                    then(dve.tensor_reduce(top[:, k, :], ranked[:, k, :, :], AX.X, ALU.max))
                    then(dve.tensor_tensor(one[:, k, :, :], ranked[:, k, :, :], wide(top[:, k, :]), ALU.is_equal))
                    if k == 0:
                        then(dve.scalar_tensor_tensor(out=rest[:], in0=one[:, 0, :, :], scalar=NOT_CHOSEN,
                                                      in1=logit[:], op0=ALU.mult, op1=ALU.add))
                then(dve.tensor_tensor(gap[:], best[:, 1, :], best[:, 0, :], ALU.subtract))
                dve.sem_inc(gap_ready, 1)
                dve.wait_ge(second_ready, n.val(1, 1))
                then(dve.tensor_scalar(total[:], second[:], 1.0, None, ALU.add))
                then(dve.reciprocal(share[:, 0, :], total[:]))
                then(dve.tensor_tensor(share[:, 1, :], share[:, 0, :], second[:], ALU.mult))
                for k in range(2):
                    then(dve.tensor_tensor(part[:, k, :, :], one[:, k, :, :], wide(share[:, k, :]), ALU.mult))
                then(dve.tensor_tensor(gate[:, n.slot(2), :, :], part[:, 0, :, :], part[:, 1, :, :], ALU.add))
                assert done[0] == OPS, done
                dve.sem_inc(gates_ready, 1)

            def begin(n, first):
                if first >= 2:
                    dve.wait_ge(x2_out[n.slot(3)], n.turn(3, 16))
                for b, (t0, t1) in enumerate(HALVES):
                    dve.wait_ge(bias_made[b], n.val(1, 1))
                    dve.tensor_tensor(acc[:, n.slot(3), t0:t1, :],
                                      px[:, b, 0:(t1 - t0) * C].rearrange("p (t c) -> p t c", c=C),
                                      xin[:, n.slot(3), t0:t1, :], ALU.add).then_inc(acc_begun[b], 1)

            MIX = E

            def mix(n, t):
                e0 = MIX * t
                b = (n.off * T + t) % 2
                a, o, g = acc[:, n.slot(3), t, :], odd[:, b, :], gate[:, n.slot(2), t, :]
                dve.wait_ge(expert_done, n.val(T, t + 1))
                if t == 0:
                    dve.wait_ge(acc_begun[1], n.val(1, 1))
                for e in range(E):
                    src = pe_out[:, b, e // 4, (e % 4) * C:(e % 4 + 1) * C]
                    if e == 1:
                        dve.tensor_scalar(o, src, g[:, e:e + 1], None, ALU.mult).then_inc(mixing, 1)
                        continue
                    if e >= 2:
                        dve.wait_ge(mixing, n.val(T * MIX, e0 + e - 1))
                    into = a if e % 2 == 0 else o
                    ins = dve.scalar_tensor_tensor(out=into, in0=src, scalar=g[:, e:e + 1], in1=into,
                                                   op0=ALU.mult, op1=ALU.add).then_inc(mixing, 1)
                dve.wait_ge(mixing, n.val(T * MIX, e0 + E))
                dve.tensor_tensor(a, a, o, ALU.add).then_inc(mixed, 1)

            def step(n, first, last):
                if first == 0:
                    for k in range(min(2, N)):
                        layer_stats(n + k)
                    route(n)
                    begin(n, 0)
                if last < -2:
                    dve.wait_ge(normed, n.val(1, 1))
                    layer_stats(n + 2)
                for t in range(2):
                    mix(n, t)
                if last < -1:
                    route(n + 1)
                for t in range(2, 6):
                    mix(n, t)
                if last < -1:
                    begin(n + 1, first)
                mix(n, 6)

            run_steps(dve, N, U, step)

        @block.tensor
        def _(pe):
            pe.wait_ge(const_in, CONSTS)

            def turn(n, first):
                pe.wait_ge(normed, n.val(1, 1))
                for b, (t0, t1) in enumerate(HALVES):
                    if first >= 1:
                        pe.wait_ge(acc_begun[b], n.val())
                    for t in range(t0, t1):
                        ins = pe.transpose(px[:, b, (t - t0) * P:(t - t0 + 1) * P], xn[:, n.slot(2), t, :], idn[:])
                    ins.then_inc(turned[b], 1)

            def logits(n, first):
                pe.wait_ge(xT_out[1], n.val(1, 1))
                if first >= 1:
                    pe.wait_ge(gates_ready, n.val())
                for t in range(T):
                    ins = pe.matmul(pr[:, t * E:(t + 1) * E], xnT[:, n.slot(2), t, :], wr[:], start=True, stop=True)
                ins.then_inc(logits_made, 1)

            def turn_gates(n):
                pe.wait_ge(gates_ready, n.val(1, 1))
                for b, (t0, t1) in enumerate(HALVES):
                    for t in range(t0, t1):
                        ins = pe.transpose(px[0:E, b, (t - t0) * P:(t - t0 + 1) * P], gate[:, n.slot(2), t, :], idn[:])
                    ins.then_inc(gates_turned[b], 1)

            def gated_bias(n):
                for b, (t0, t1) in enumerate(HALVES):
                    pe.wait_ge(gT_out[b], n.val(1, 1))
                    for t in range(t0, t1):
                        ins = pe.matmul(px[:, b, (t - t0) * C:(t - t0 + 1) * C], gateT[:, t, :], be[:],
                                        start=True, stop=True)
                    ins.then_inc(bias_made[b], 1)

            def experts(n, t, first):
                b = (n.off * T + t) % 2
                if first >= 1 or t >= 2:
                    pe.wait_ge(mixed, n.val(T, t - 1))
                for half in range(2):
                    ins = pe.matmul(pe_out[:, b, half, :], xnT[:, n.slot(2), t, :],
                                    we[:, half * 4:half * 4 + 4, :].rearrange("d e c -> d (e c)"), start=True, stop=True)
                ins.then_inc(expert_done, 1)

            def step(n, first, last):
                if first == 0:
                    turn(n, 0)
                    logits(n, 0)
                    turn_gates(n)
                    gated_bias(n)
                if last < -1:
                    turn(n + 1, 1)
                for t in range(2):
                    experts(n, t, first)
                if last < -1:
                    logits(n + 1, 1)
                for t in range(2, 5):
                    experts(n, t, first)
                if last < -1:
                    turn_gates(n + 1)
                experts(n, 5, first)
                if last < -1:
                    gated_bias(n + 1)
                experts(n, 6, first)

            run_steps(pe, N, U, step)


ROW = 64
QUAD = 4
GROUPS = C // QUAD
ODD = IMG // 2 + 1
EVEN = IMG // 2
BLOCKS = (2, 3, 5)
FURTHEST = (64, 128, 256)
G_LEN = tuple(P - 1 + P * b for b in BLOCKS)
G_OFF = (0, G_LEN[0], G_LEN[0] + G_LEN[1])
G_ALL = sum(G_LEN)

ODD_ROWS = (((54, 1, 1), (0, 2, 27)), ((53, 0, 2), (1, 2, 26)))
EVEN_ROWS = (((53, 0, 2), (1, 2, 26)), ((54, 0, 1), (0, 1, 27)))
COLS = ((53, 0, 3), (0, 3, 53))
ROLLED = 8


def load_rolled(eng, dst, pitch, src, n, rows, sem):
    for half in range(2):
        for row, tile, tiles in rows[half]:
            for col, w0, ws in COLS:
                p0 = half * pitch + w0
                eng.dma_start(dst[p0:p0 + ws, tile:tile + tiles, :],
                              dram(src, n.val(PIX * C, (row * IMG + col) * C),
                                   [(C, ws), (2 * IMG * C, tiles), (1, C)])).then_inc(sem, 16)


def focal_input_stage(nc, B, x2, Wf, bf, edge_mask, ident, q, c0, gates):
    N = B
    EPS = 1e-6
    OUT = 2 * C + 4
    U = 2
    CHUNKS = [(t, min(4, ODD - t)) for t in range(0, ODD, 4)]
    NCH = len(CHUNKS)
    PAIRS = [(t, min(2, ODD - t)) for t in range(0, ODD, 2)]
    NPR = len(PAIRS)
    S = Stage(nc, "foc")
    with S.ctx:
        idn = S.sb("idn", [P, P])
        wf = S.sb("wf", [C, OUT])
        bias = S.sb("bias", [P, OUT])
        edge = S.sb("edge", [P, 4])
        cbias = S.sb("cbias", [P, 4, C])
        halfneg = S.sb("halfneg", [P, ODD])
        xin = S.sb("xin", [P, 2, ODD, C])
        stat = S.sb("stat", [P, ODD, 6])
        mv = S.sb("mv", [P, ODD, 2])
        rstd = S.sb("rstd", [P, 2, ODD])
        nmean = S.sb("nmean", [P, 2, ODD])
        xn = S.sb("xn", [P, 2, 4, C])
        xnT = S.sb("xnT", [C, 2, 4 * P])
        qs = S.sb("qs", [P, ODD, C])
        cs = S.sb("cs", [P, GROUPS, ODD, QUAD])
        gs = S.sb("gs", [P, 4, ODD])
        px = S.ps("px", [P, 2, BANK])
        py = S.ps("py", [P, 2, 2, BANK])

        ticks = S.sem("ticks")
        const_in = S.sem("const_in")
        zeroed = S.sem("zeroed")
        filled = S.sem("filled")
        cbias_built = S.sem("cbias_built")
        x_in = S.sems("x_in", 2)
        stats_part, stats, eps_added, rstd_done = (S.sem(f"{k}") for k in ("stats_part", "stats", "eps_added", "rstd_done"))
        nmean_done = S.sem("nmean_done")
        normed, turned, xT_out = S.sem("normed"), S.sem("turned"), S.sem("xT_out")
        made, ctx_read, gates_read, q_read = S.sem("made"), S.sem("ctx_read"), S.sem("gates_read"), S.sem("q_read")
        q_biased = S.sem("q_biased")
        q_out, c_out, g_out = S.sem("q_out"), S.sem("c_out"), S.sem("g_out")
        block = S.block()

        @block.sync
        def _(sp):
            for dst, src in ((idn[:], ident), (wf[:], Wf), (bias[:], row_to_all(bf, OUT)), (edge[:], edge_mask)):
                sp.dma_start(dst, src).then_inc(const_in, 16)
            sp.wait_ge(zeroed, 2)

            def step(n, first, last):
                if first == 0:
                    load_rolled(sp, xin[:, n.slot(2), :, :], ROW, x2, n, ODD_ROWS, x_in[n.slot(2)])
                if last < -1:
                    if first >= 1:
                        hold(sp, normed, n.val(NCH), ticks)
                    load_rolled(sp, xin[:, (n + 1).slot(2), :, :], ROW, x2, n + 1, ODD_ROWS, x_in[(n + 1).slot(2)])
                hold(sp, ctx_read, n.val(NPR, NPR), ticks)
                sp.dma_start(dram(c0, n.val(ODD * QUAD), [(B * ODD * QUAD, P), (P * B * ODD * QUAD, GROUPS), (1, ODD * QUAD)]),
                             cs[:].rearrange("p g j c -> p g (j c)")).then_inc(c_out, 16)
                hold(sp, gates_read, n.val(NPR, NPR), ticks)
                for half, j0 in ((0, 0), (1, 1)):
                    sp.dma_start(dram(gates, n.val(EVEN, half * ROW * 4 * B * EVEN), [(4 * B * EVEN, ROW), (B * EVEN, 4), (1, EVEN)]),
                                 gs[(1 - half) * ROW:(2 - half) * ROW, :, j0:j0 + EVEN]).then_inc(g_out, 16)
                hold(sp, q_biased, n.val(1, 1), ticks)
                for half, j0 in ((0, 1), (1, 0)):
                    row = 2 * j0 - 1 + half
                    sp.dma_start(dram(q, n.val(PIX * C, row * IMG * C), [(C, IMG), (2 * IMG * C, EVEN), (1, C)]),
                                 qs[half * ROW:half * ROW + IMG, j0:j0 + EVEN, :]).then_inc(q_out, 16)

            run_steps(sp, N, U, step)
            sp.wait_ge(c_out, 16 * N)
            sp.wait_ge(g_out, 32 * N)
            sp.wait_ge(q_out, 32 * N)

        @block.gpsimd
        def _(pool):
            for s in range(2):
                pool.memset(xin[:, s, :, :], 0.0).then_inc(zeroed, 1)
            pool.memset(halfneg[:], -0.5).then_inc(filled, 1)
            pool.wait_ge(filled, 1)
            pool.wait_ge(const_in, 64)

            def step(n, first, last):
                def scale(n):
                    a = n.slot(2)
                    hold(pool, stats, n.val(1, 1), ticks)
                    pool.tensor_scalar(rstd[:, a, :], mv[:, :, 1], EPS, None, ALU.add).then_inc(eps_added, 1)
                    pool.wait_ge(eps_added, n.val(1, 1))
                    pool.tensor_tensor(rstd[:, a, :], rstd[:, a, :], halfneg[:], ALU.pow).then_inc(rstd_done, 1)

                if first == 0:
                    scale(n)
                if last < -1:
                    scale(n + 1)
                pool.wait_ge(q_read, n.val(NPR, NPR))
                pool.tensor_tensor(qs[:], qs[:], bias[:, 0:C].unsqueeze(1).to_broadcast([P, ODD, C]), ALU.add)\
                    .then_inc(q_biased, 1)

            run_steps(pool, N, U, step)

        @block.scalar
        def _(act):
            act.wait_ge(const_in, 64)

            def normalise(n, c):
                t0, tn = CHUNKS[c]
                b = (n.off * NCH + c) % 2
                if c == 0:
                    act.wait_ge(nmean_done, n.val(1, 1))
                if not (n.is_static and n.off * NCH + c < 2):
                    act.wait_ge(turned, n.val(NCH, c - 1))
                for t in range(tn):
                    ins = act.activation(xn[:, b, t, :], xin[:, n.slot(2), t0 + t, :], ACT.Identity,
                                         bias=nmean[:, n.slot(2), t0 + t:t0 + t + 1],
                                         scale=rstd[:, n.slot(2), t0 + t:t0 + t + 1])
                ins.then_inc(normed, 1)

            def step(n, first, last):
                if first == 0:
                    normalise(n, 0)
                for c, (t0, tn) in enumerate(CHUNKS):
                    b = (n.off * NCH + c) % 2
                    act.wait_ge(turned, n.val(NCH, c + 1))
                    act.activation(xnT[:, b, 0:tn * P], px[:, b, 0:tn * P], ACT.Copy).then_inc(xT_out, 1)
                    if c + 1 < NCH:
                        normalise(n, c + 1)
                    elif last < -1:
                        normalise(n + 1, 0)
                    for k in range(2 * c, min(2 * c + 2, NPR)):
                        p0, pn = PAIRS[k]
                        y = (n.off * NPR + k) % 2
                        if k == 0 and first >= 1:
                            act.wait_ge(q_out, n.val(32))
                            act.sem_inc(ticks, 1)
                        act.wait_ge(gates_read, n.val(NPR, k + 1))
                        act.activation(qs[:, p0:p0 + pn, :], py[:, y, 0:pn, 0:C], ACT.Copy).then_inc(q_read, 1)

            run_steps(act, N, U, step)

        @block.vector
        def _(dve):
            dve.wait_ge(const_in, 64)
            for k in range(4):
                dve.tensor_scalar(cbias[:, k, :], bias[:, C:2 * C], edge[:, k:k + 1], None, ALU.mult).then_inc(cbias_built, 1)
            dve.wait_ge(cbias_built, 4)

            def layer_stats(n):
                s = n.slot(2)
                dve.wait_ge(x_in[s], n.turn(2, 16 * ROLLED, 16 * ROLLED))
                for t in range(ODD):
                    dve.bn_stats(stat[:, t, :], xin[:, s, t, :]).then_inc(stats_part, 1)
                hold(dve, stats_part, n.val(ODD, ODD), ticks)
                for t in range(ODD):
                    ins = dve.bn_aggr(mv[:, t, :], stat[:, t, :])
                ins.then_inc(stats, 1)
                dve.wait_ge(rstd_done, n.val(1, 1))
                dve.sem_inc(ticks, 1)
                dve.wait_ge(stats, n.val(1, 1))
                dve.scalar_tensor_tensor(out=nmean[:, s, :], in0=mv[:, :, 0], scalar=-1.0, in1=rstd[:, s, :],
                                         op0=ALU.mult, op1=ALU.mult).then_inc(nmean_done, 1)

            def step(n, first, last):
                if first == 0:
                    layer_stats(n)
                for k, (p0, pn) in enumerate(PAIRS):
                    y = (n.off * NPR + k) % 2
                    if k == NPR // 2 and last < -1:
                        if first >= 1:
                            dve.wait_ge(normed, n.val(NCH))
                            dve.sem_inc(ticks, 1)
                        dve.wait_ge(nmean_done, n.val(1, 1))
                        layer_stats(n + 1)
                    dve.wait_ge(made, n.val(NPR, k + 1))
                    if k == 0 and first >= 1:
                        dve.sem_inc(ticks, 1)
                        dve.wait_ge(c_out, n.val(16))
                        dve.sem_inc(ticks, 1)
                        dve.wait_ge(g_out, n.val(32))
                    version = 0 if k == 0 else (3 if k == NPR - 1 else 1)
                    dve.tensor_tensor(cs[:, :, p0:p0 + pn, :].rearrange("p g j c -> p j g c"),
                                      py[:, y, 0:pn, C:2 * C].rearrange("p j (g c) -> p j g c", c=QUAD),
                                      cbias[:, version:version + pn, :].rearrange("p j (g c) -> p j g c", c=QUAD),
                                      ALU.add).then_inc(ctx_read, 1)
                    dve.tensor_tensor(gs[:, :, p0:p0 + pn].rearrange("p l j -> p j l"), py[:, y, 0:pn, 2 * C:OUT],
                                      bias[:, 2 * C:OUT].unsqueeze(1).to_broadcast([P, pn, 4]), ALU.add).then_inc(gates_read, 1)

            run_steps(dve, N, U, step)

        @block.tensor
        def _(pe):
            pe.wait_ge(const_in, 64)

            def turn(n, c):
                t0, tn = CHUNKS[c]
                b = (n.off * NCH + c) % 2
                pe.wait_ge(normed, n.val(NCH, c + 1))
                if not (n.is_static and n.off * NCH + c < 2):
                    pe.wait_ge(xT_out, n.val(NCH, c - 1))
                for t in range(tn):
                    ins = pe.transpose(px[:, b, t * P:(t + 1) * P], xn[:, b, t, :], idn[:])
                ins.then_inc(turned, 1)

            def step(n, first, last):
                if first == 0:
                    turn(n, 0)
                for c, (t0, tn) in enumerate(CHUNKS):
                    b = (n.off * NCH + c) % 2
                    if c + 1 < NCH:
                        turn(n, c + 1)
                    elif last < -1:
                        turn(n + 1, 0)
                    pe.wait_ge(xT_out, n.val(NCH, c + 1))
                    for k in range(2 * c, min(2 * c + 2, NPR)):
                        p0, pn = PAIRS[k]
                        y = (n.off * NPR + k) % 2
                        if not (n.is_static and n.off * NPR + k < 2):
                            pe.wait_ge(gates_read, n.val(NPR, k - 1))
                            pe.sem_inc(ticks, 1)
                            pe.wait_ge(q_read, n.val(NPR, k - 1))
                        for j in range(pn):
                            t = p0 + j - t0
                            ins = pe.matmul(py[:, y, j, 0:OUT], xnT[:, b, t * P:(t + 1) * P], wf[:], start=True, stop=True)
                        ins.then_inc(made, 1)

            run_steps(pe, N, U, step)


def convolution_stage(nc, B, c0, gates, kernels, gap_mask, ctx_all):
    N = C
    HALF = B // 2
    U = 8
    PER = QUAD
    AHEAD = 4
    T_ALL = P * sum(BLOCKS)
    T_OFF = (0, P * BLOCKS[0], P * (BLOCKS[0] + BLOCKS[1]))
    S = Stage(nc, "conv")
    with S.ctx:
        gvec = S.sb("gvec", [C, G_ALL])
        ones = S.sb("ones", [P, P])
        gap = S.sb("gap", [P, 1])
        gate = S.sb("gate", [P, 4, B, EVEN])
        toep = S.sb("toep", [P, 2, PER, T_ALL])
        cin = S.sb("cin", [P, 2, B, ODD, PER])
        c1 = S.sb("c1", [P, 4, B, EVEN + 2])
        c2 = S.sb("c2", [P, 2, B, EVEN + 4])
        c3 = S.sb("c3", [P, 2, B, EVEN])
        g1 = S.sb("g1", [P, B, EVEN])
        g2 = S.sb("g2", [P, B, EVEN])
        g3 = S.sb("g3", [P, B, EVEN])
        pooled = S.sb("pooled", [P, B])
        glob = S.sb("glob", [P, B])
        out = S.sb("out", [P, 2, B, PER, EVEN])
        gvec_dram = nc.dram_tensor("gvec_dram", (C, G_ALL), F32).ap()
        group_dram = nc.dram_tensor("group_dram", (2, PER, G_ALL), F32).ap()
        rows_dram = nc.dram_tensor("rows_dram", (2, PER, P, T_ALL), F32).ap()
        pc = [S.ps(f"pc{k}", [P, 2, BANK]) for k in range(3)]
        pm = S.ps("pm", [P, BANK])

        ticks = S.sem("ticks")
        zeroed = S.sem("zeroed")
        taps_in, gvec_out = S.sem("taps_in"), S.sem("gvec_out")
        const_in = S.sem("const_in")
        rows_made = S.sems("rows_made", 2)
        group_in, toep_in, c0_in = S.sems("group_in", 2), S.sems("toep_in", 2), S.sems("c0_in", 2)
        convolved = S.sems("convolved", 3)
        activated = S.sems("activated", 3)
        gated1, gated2, gated3 = S.sem("gated1"), S.sem("gated2"), S.sem("gated3")
        pooled_part, averaged, glob_ready = S.sem("pooled_part"), S.sem("averaged"), S.sem("glob_ready")
        summed, gglob, summed_glob = S.sem("summed"), S.sem("gglob"), S.sem("summed_glob")
        combined = S.sem("combined")
        stored = S.sems("stored", 2)
        block = S.block()
        NG = N // PER

        @block.sync
        def _(sp):
            sp.wait_ge(zeroed, 1)
            for k, size in enumerate(TAPS):
                r = size // 2
                at = G_OFF[k] + P - 1 + FURTHEST[k] - r * ROW - r
                for row in range(size):
                    sp.dma_start(gvec[:, at + row * ROW:at + row * ROW + size],
                                 dram(kernels[k], row * size, [(size * size, C), (1, size)])).then_inc(taps_in, 16)
            sp.dma_start(gate[:], gates).then_inc(const_in, 16)
            sp.dma_start(gap[:], gap_mask).then_inc(const_in, 16)
            sp.wait_ge(taps_in, 16 * sum(TAPS))
            sp.dma_start(gvec_dram, gvec[:]).then_inc(gvec_out, 16)
            sp.wait_ge(gvec_out, 16)

            def load(g, n, extra):
                s = g.slot(2)
                sp.dma_start(cin[:, s, :, :, :].rearrange("p b j c -> p (b j c)"),
                             dram(c0, g.val(P * B * ODD * PER), [(B * ODD * PER, P), (1, B * ODD * PER)]))\
                  .then_inc(c0_in[s], 16)
                sp.dma_start(dram(group_dram, s * PER * G_ALL, [(G_ALL, PER), (1, G_ALL)]),
                             dram(gvec_dram, g.val(PER * G_ALL), [(G_ALL, PER), (1, G_ALL)])).then_inc(group_in[s], 16)
                hold(sp, group_in[s], g.turn(2, 16, 16), ticks)
                for k, blocks in enumerate(BLOCKS):
                    sp.dma_start(dram(rows_dram, s * PER * P * T_ALL + T_OFF[k], [(P * T_ALL, PER), (T_ALL, P), (1, P * blocks)]),
                                 dram(group_dram, s * PER * G_ALL + G_OFF[k] + P - 1,
                                      [(G_ALL, PER), (-1, P), (1, P * blocks)])).then_inc(rows_made[s], 16)
                hold(sp, rows_made[s], g.turn(2, 48, 48), ticks)
                sp.dma_start(toep[:, s, :, :], dram(rows_dram, s * PER * P * T_ALL, [(T_ALL, P), (P * T_ALL, PER), (1, T_ALL)]))\
                  .then_inc(toep_in[s], 16)

            def step(n, first, last):
                if n.off % PER != PER - 1:
                    return
                g = Step(n.loop, U // PER, n.off // PER)
                if first < PER:
                    load(g, n, 0)
                    load(g + 1, n, 1)
                if last + 1 < -2 * PER + 1:
                    hold(sp, convolved[2], n.val(1, 1), ticks)
                    load(g + 2, n, 2)
                hold(sp, combined, n.val(1, 1), ticks)
                sp.dma_start(dram(ctx_all, g.val(P * B * EVEN * PER), [(B * EVEN * PER, P), (1, B * EVEN * PER)]),
                             out[:, g.slot(2), :, :, :].rearrange("p b c i -> p (b c i)")).then_inc(stored[g.slot(2)], 16)

            run_steps(sp, N, U, step, AHEAD + PER)
            for s in range(2):
                sp.wait_ge(stored[s], 16 * (NG // 2))

        @block.gpsimd
        def _(pool):
            pool.memset(gvec[:], 0.0).then_inc(zeroed, 1)
            pool.memset(c1[:], 0.0).then_inc(zeroed, 1)
            pool.memset(c2[:], 0.0).then_inc(zeroed, 1)
            pool.memset(ones[:], 1.0).then_inc(zeroed, 1)
            pool.wait_ge(const_in, 32)

            def step(n, first, last):
                pool.wait_ge(activated[1], n.val(1, 1))
                if first >= 1:
                    pool.sem_inc(ticks, 1)
                    pool.wait_ge(combined, n.val())
                pool.tensor_tensor(g2[:], c2[:, n.slot(2), :, 2:2 + EVEN], gate[:, 1, :, :], ALU.mult).then_inc(gated2, 1)

            run_steps(pool, N, U, step, AHEAD)

        @block.scalar
        def _(act):
            act.wait_ge(zeroed, 4)
            act.wait_ge(const_in, 32)

            def gelu(k, n, first):
                dst, slots = (c1, c2, c3)[k], (4, 2, 2)[k]
                edge = (1, 2, 0)[k]
                act.wait_ge(convolved[k], n.val(1, 1))
                if first >= slots:
                    act.sem_inc(ticks, 1)
                    act.wait_ge((gated1, gated2, gated3)[k], n.val(1, 1 - slots))
                    if k < 2:
                        act.sem_inc(ticks, 1)
                        act.wait_ge(convolved[k + 1], n.val(1, 1 - slots))
                    else:
                        act.sem_inc(ticks, 1)
                        act.wait_ge(pooled_part, n.val(1, -1))
                for half in range(2):
                    ins = act.activation(dst[:, n.slot(slots), half * HALF:(half + 1) * HALF, edge:edge + EVEN],
                                         pc[k][:, half, 0:HALF * EVEN].rearrange("p (b i) -> p b i", i=EVEN),
                                         ACT.Gelu, scale=gap[:])
                ins.then_inc(activated[k], 1)

            def average(n, first):
                act.wait_ge(averaged, n.val(1, 1))
                if first >= 1:
                    act.sem_inc(ticks, 1)
                    act.wait_ge(gglob, n.val())
                act.activation(glob[:], pm[:, 0:B], ACT.Gelu, scale=1.0 / PIX).then_inc(glob_ready, 1)

            def step(n, first, last):
                if first == 0:
                    gelu(0, n, 0)
                    gelu(0, n + 1, 1)
                    gelu(1, n, 0)
                if last < -3:
                    gelu(0, n + 2, first + 2)
                if first >= 1:
                    average(n - 1, first - 1)
                if last < -2:
                    gelu(1, n + 1, first + 1)
                if last < -1:
                    gelu(2, n, first)

            run_steps(act, N + 1, U, step, AHEAD)

        @block.vector
        def _(dve):
            dve.wait_ge(const_in, 32)

            def products(n, first):
                s = n.slot(2)
                dve.wait_ge(activated[2], n.val(1, 1))
                dve.tensor_reduce(pooled[:], c3[:, s, :, :], AX.X, ALU.add).then_inc(pooled_part, 1)
                if first >= 1:
                    dve.wait_ge(combined, n.val())
                dve.tensor_tensor(g3[:], c3[:, s, :, :], gate[:, 2, :, :], ALU.mult).then_inc(gated3, 1)
                dve.wait_ge(gated3, n.val(1, 1))
                dve.sem_inc(ticks, 1)
                dve.wait_ge(gated1, n.val(1, 1))
                dve.tensor_tensor(g3[:], g3[:], g1[:], ALU.add).then_inc(summed, 1)

            def first_gate(n, first):
                dve.wait_ge(activated[0], n.val(1, 1))
                if first >= 1:
                    dve.sem_inc(ticks, 1)
                    dve.wait_ge(summed_glob, n.val())
                dve.tensor_tensor(g1[:], c1[:, n.slot(4), :, 1:1 + EVEN], gate[:, 0, :, :], ALU.mult).then_inc(gated1, 1)

            def combine(n, first):
                g = Step(n.loop, U // PER, n.off // PER)
                s = g.slot(2)
                dve.wait_ge(glob_ready, n.val(1, 1))
                dve.sem_inc(ticks, 1)
                dve.wait_ge(summed, n.val(1, 1))
                dve.tensor_tensor(g1[:], gate[:, 3, :, :], glob[:].unsqueeze(2).to_broadcast([P, B, EVEN]),
                                  ALU.mult).then_inc(gglob, 1)
                dve.wait_ge(gglob, n.val(1, 1))
                dve.tensor_tensor(g3[:], g3[:], g1[:], ALU.add).then_inc(summed_glob, 1)
                dve.wait_ge(summed_glob, n.val(1, 1))
                if first >= 2 * PER and n.off % PER == 0:
                    dve.sem_inc(ticks, 1)
                    dve.wait_ge(stored[s], g.turn(2, 16))
                dve.sem_inc(ticks, 1)
                dve.wait_ge(gated2, n.val(1, 1))
                dve.tensor_tensor(out[:, s, :, n.off % PER, :], g3[:], g2[:], ALU.add).then_inc(combined, 1)

            def step(n, first, last):
                if first >= 1:
                    combine(n - 1, first - 1)
                if last < -1:
                    first_gate(n, first)
                    products(n, first)

            run_steps(dve, N + 1, U, step, AHEAD)

        @block.tensor
        def _(pe):
            pe.wait_ge(zeroed, 4)

            def convolve(k, n, first, group_first):
                g = Step(n.loop, U // PER, n.off // PER)
                ch, s = n.off % PER, g.slot(2)
                if k == 0 and ch == 0:
                    hold(pe, c0_in[s], g.turn(2, 16, 16), ticks)
                    hold(pe, toep_in[s], g.turn(2, 16, 16), ticks)
                if k > 0:
                    hold(pe, activated[k - 1], n.val(1, 1), ticks)
                if first >= 1:
                    pe.wait_ge(activated[k], n.val())
                blocks = BLOCKS[k]
                for blk in range(blocks):
                    w = toep[:, s, ch, T_OFF[k] + blk * P:T_OFF[k] + (blk + 1) * P]
                    below = blocks - 1 - blk
                    for half in range(2):
                        b = slice(half * HALF, (half + 1) * HALF)
                        if k == 0:
                            src = cin[:, s, b, below:below + EVEN, ch]
                        else:
                            src = (c1, c2)[k - 1][:, n.slot((4, 2)[k - 1]), b, below:below + EVEN]
                        ins = pe.matmul(pc[k][:, half, 0:HALF * EVEN], w, src, start=(blk == 0), stop=(blk == blocks - 1))
                ins.then_inc(convolved[k], 1)

            def average(n, first):
                if first >= 1:
                    pe.wait_ge(glob_ready, n.val())
                    pe.sem_inc(ticks, 1)
                pe.wait_ge(pooled_part, n.val(1, 1))
                pe.matmul(pm[:, 0:B], ones[:], pooled[:], start=True, stop=True).then_inc(averaged, 1)

            def step(n, first, last):
                if first == 0:
                    convolve(0, n, 0, 0)
                    convolve(0, n + 1, 1, 0)
                    convolve(1, n, 0, 0)
                if last < -3:
                    convolve(0, n + 2, first + 2, 0)
                if first >= 1:
                    average(n - 1, first - 1)
                if last < -2:
                    convolve(1, n + 1, first + 1, 0)
                if last < -1:
                    convolve(2, n, first, 0)

            run_steps(pe, N + 1, U, step, AHEAD)


def focal_output_stage(nc, B, ctx_all, q, x2, Wh, bh, gamma, beta, Wp, bp, ident, x3, gram):
    TOK = 2 * IMG
    CH = 4
    NCH = EVEN // CH
    EPS, EPS_T = 1e-3, 1e-5
    N = B * NCH
    U = 2 * NCH
    AHEAD = 3 + NCH
    S = Stage(nc, "mod")
    with S.ctx:
        idn = S.sb("idn", [P, P])
        wh = S.sb("wh", [C, C])
        wp = S.sb("wp", [C, C])
        wpg = S.sb("wpg", [C, C])
        bhr = S.sb("bhr", [P, C])
        bpr = S.sb("bpr", [P, C])
        gcol = S.sb("gcol", [C, 1])
        bcol = S.sb("bcol", [C, 1])
        bmat = S.sb("bmat", [C, P])
        brow = S.sb("brow", [P, C])
        halfneg = S.sb("halfneg", [P, CH])
        cin = S.sb("cin", [TOK, 2, C, EVEN])
        qin = S.sb("qin", [TOK, 2, EVEN, C])
        xin = S.sb("xin", [TOK, 2, EVEN, C])
        cT = S.sb("cT", [C, 2, CH * TOK])
        y = S.sb("y", [TOK, 2, CH, C])
        yn = S.sb("yn", [TOK, 2, CH, C])
        yT = S.sb("yT", [C, 2, CH * TOK])
        z = S.sb("z", [TOK, 2, CH, C + 1])
        stat = S.sb("stat", [TOK, 2, CH, 6])
        mv = S.sb("mv", [TOK, 2, 2, CH, 2])
        rstd = S.sb("rstd", [TOK, 2, 2, CH])
        nmean = S.sb("nmean", [TOK, 2, 2, CH])
        gout = S.sb("gout", [C, C + 1])

        pt = S.ps("pt", [P, BANK])
        pm = S.ps("pm", [P, 2, BANK])
        pu = S.ps("pu", [P, BANK])
        pz = S.ps("pz", [P, 2, BANK])
        pg = S.ps("pg", [P, BANK])

        ticks = S.sem("ticks")
        const_in, filled = S.sem("const_in"), S.sem("filled")
        scaled, beta_wide, bias_made, bias_built = (S.sem(k) for k in ("scaled", "beta_wide", "bias_made", "bias_built"))
        c_in, q_in, x_in = S.sems("c_in", 2), S.sems("q_in", 2), S.sems("x_in", 2)
        x_biased = S.sem("x_biased")
        turned, cT_out, modulated = S.sem("turned"), S.sem("cT_out"), S.sem("modulated")
        biased, gated = S.sem("biased"), S.sem("gated")
        parts, stats = S.sems("parts", 2), S.sems("stats", 2)
        eps_added, rstd_done, nmean_done = S.sems("eps_added", 2), S.sems("rstd_done", 2), S.sems("nmean_done", 2)
        y_normed, y_turned, yT_out, projected = (S.sem(k) for k in ("y_normed", "y_turned", "yT_out", "projected"))
        x3_made, z_normed, gram_added = S.sem("x3_made"), S.sem("z_normed"), S.sem("gram_added")
        x3_out, gram_copied, gram_out = S.sems("x3_out", 2), S.sem("gram_copied"), S.sem("gram_out")
        block = S.block()
        CONSTS = 16 * 7

        def image(n):
            return Step(n.loop, 2, n.off // NCH), n.off % NCH

        @block.sync
        def _(sp):
            for dst, src in ((idn[:], ident), (wh[:], Wh), (wp[:], Wp), (bhr[:], row_to_all(bh, C)),
                             (bpr[:], row_to_all(bp, C)), (gcol[:], dram(gamma, 0, [(1, C), (1, 1)])),
                             (bcol[:], dram(beta, 0, [(1, C), (1, 1)]))):
                sp.dma_start(dst, src).then_inc(const_in, 16)

            def load_cq(m):
                s = m.slot(2)
                for half in range(2):
                    p0 = half * IMG
                    sp.dma_start(cin[p0:p0 + IMG, s, :, :].rearrange("p (g c) i -> p g (c i)", c=QUAD),
                                 dram(ctx_all, m.val(EVEN * QUAD, half * ROW * B * EVEN * QUAD),
                                      [(B * EVEN * QUAD, IMG), (P * B * EVEN * QUAD, GROUPS), (1, EVEN * QUAD)]))\
                      .then_inc(c_in[s], 16)
                sp.dma_start(qin[:, s, :, :], dram(q, m.val(PIX * C), [(C, TOK), (TOK * C, EVEN), (1, C)])).then_inc(q_in[s], 16)

            def load_x(m):
                load_rolled(sp, xin[:, m.slot(2), :, :], IMG, x2, m, EVEN_ROWS, x_in[m.slot(2)])

            def step(n, first, last):
                m, c = image(n)
                if first == 0:
                    for k in range(2):
                        load_cq(m + k)
                        load_x(m + k)
                if c == NCH - 1:
                    if last < -NCH - 1:
                        hold(sp, turned, n.val(1, 1), ticks)
                        hold(sp, gated, n.val(1, 1), ticks)
                        load_cq(m + 2)
                    hold(sp, x3_made, n.val(1, 1), ticks)
                    sp.dma_start(dram(x3, m.val(PIX * C), [(C, TOK), (TOK * C, EVEN), (1, C)]),
                                 xin[:, m.slot(2), :, :]).then_inc(x3_out[m.slot(2)], 16)
                    if last < -NCH - 1:
                        hold(sp, x3_out[m.slot(2)], m.turn(2, 16, 16), ticks)
                        hold(sp, z_normed, n.val(1, 1), ticks)
                        load_x(m + 2)

            run_steps(sp, N, U, step, 2 * NCH)
            for s in range(2):
                sp.wait_ge(x3_out[s], 16 * ((B + 1 - s) // 2))
            sp.wait_ge(gram_copied, 1)
            sp.dma_start(gram, gout[:]).then_inc(gram_out, 16)
            sp.wait_ge(gram_out, 16)

        @block.gpsimd
        def _(pool):
            pool.memset(halfneg[:], -0.5).then_inc(filled, 1)
            pool.memset(z[:], 1.0).then_inc(filled, 1)
            pool.memset(bmat[:], 1.0).then_inc(filled, 1)
            pool.wait_ge(filled, 3)
            pool.wait_ge(bias_built, 1)

            def rsqrt(n, which, eps, first):
                if which == 1 and first >= 2:
                    hold(pool, z_normed, n.val(1, -1), ticks)
                hold(pool, stats[which], n.val(1, 1), ticks)
                r = rstd[:, which, n.slot(2), :]
                pool.tensor_scalar(r, mv[:, which, n.slot(2), :, 1], eps, None, ALU.add).then_inc(eps_added[which], 1)
                pool.wait_ge(eps_added[which], n.val(1, 1))
                pool.tensor_tensor(r, r, halfneg[0:TOK, :], ALU.pow).then_inc(rstd_done[which], 1)

            def add_bias(n):
                m, c = image(n)
                if c == 0:
                    pool.wait_ge(x_in[m.slot(2)], m.turn(2, 16 * ROLLED, 16 * ROLLED))
                x = xin[:, m.slot(2), CH * c:CH * c + CH, :]
                pool.tensor_tensor(x, x, brow[0:TOK, :].unsqueeze(1).to_broadcast([TOK, CH, C]), ALU.add)\
                    .then_inc(x_biased, 1)

            def step(n, first, last):
                if first == 0:
                    for k in range(3):
                        rsqrt(n + k, 0, EPS, k)
                    add_bias(n)
                    rsqrt(n, 1, EPS_T, 0)
                    add_bias(n + 1)
                if last < -3:
                    rsqrt(n + 3, 0, EPS, first + 3)
                if last < -2:
                    add_bias(n + 2)
                if last < -1:
                    rsqrt(n + 1, 1, EPS_T, first + 1)

            run_steps(pool, N, U, step, AHEAD)

        @block.scalar
        def _(act):
            act.wait_ge(const_in, CONSTS)
            act.wait_ge(filled, 3)

            def context_out(n):
                act.wait_ge(turned, n.val(1, 1))
                act.activation(cT[:, n.slot(2), :], pt[:, 0:CH * TOK], ACT.Copy).then_inc(cT_out, 1)

            def y_out(n):
                act.wait_ge(y_turned, n.val(1, 1))
                act.activation(yT[:, n.slot(2), :], pu[:, 0:CH * TOK], ACT.Copy).then_inc(yT_out, 1)

            def norm_y(n, first):
                act.wait_ge(nmean_done[0], n.val(1, 1))
                if first >= 2:
                    act.sem_inc(ticks, 1)
                    act.wait_ge(y_turned, n.val(1, -1))
                b = n.slot(2)
                for t in range(CH):
                    ins = act.activation(yn[:, b, t, :], y[:, b, t, :], ACT.Identity,
                                         bias=nmean[:, 0, b, t:t + 1], scale=rstd[:, 0, b, t:t + 1])
                ins.then_inc(y_normed, 1)

            def norm_z(n, first):
                m, c = image(n)
                act.wait_ge(nmean_done[1], n.val(1, 1))
                if first >= 2:
                    act.sem_inc(ticks, 1)
                    act.wait_ge(gram_added, n.val(1, -1))
                b = n.slot(2)
                for t in range(CH):
                    ins = act.activation(z[:, b, t, 0:C], xin[:, m.slot(2), CH * c + t, :], ACT.Identity,
                                         bias=nmean[:, 1, b, t:t + 1], scale=rstd[:, 1, b, t:t + 1])
                ins.then_inc(z_normed, 1)

            def step(n, first, last):
                if first == 0:
                    for k in range(3):
                        context_out(n + k)
                        if k < 2:
                            norm_y(n + k, k)
                    y_out(n)
                if last < -3:
                    context_out(n + 3)
                if last < -1:
                    y_out(n + 1)
                if first >= 1:
                    norm_z(n - 1, first - 1)
                if last < -2:
                    norm_y(n + 2, first + 2)
                if last == -1:
                    norm_z(n, first)

            run_steps(act, N, U, step, AHEAD)
            act.wait_ge(gram_added, N)
            act.activation(gout[:], pg[:, 0:C + 1], ACT.Copy).then_inc(gram_copied, 1)

        @block.vector
        def _(dve):
            dve.wait_ge(const_in, CONSTS)
            dve.wait_ge(filled, 3)
            dve.tensor_scalar(bmat[:], bmat[:], bcol[:], None, ALU.mult).then_inc(beta_wide, 1)
            dve.tensor_scalar(wpg[:], wp[:], gcol[:], None, ALU.mult).then_inc(scaled, 1)
            dve.wait_ge(bias_made, 1)
            dve.tensor_tensor(brow[:], pm[:, 0, 0:C], bpr[:], ALU.add).then_inc(bias_built, 1)

            def statistics(n, which, src):
                for t in range(CH):
                    dve.bn_stats(stat[:, which, t, :], src[:, t, :]).then_inc(parts[which], 1)
                hold(dve, parts[which], n.val(CH, CH), ticks)
                for t in range(CH):
                    ins = dve.bn_aggr(mv[:, which, n.slot(2), t, :], stat[:, which, t, :])
                ins.then_inc(stats[which], 1)

            def negate(n, which):
                b = n.slot(2)
                hold(dve, rstd_done[which], n.val(1, 1), ticks)
                dve.scalar_tensor_tensor(out=nmean[:, which, b, :], in0=mv[:, which, b, :, 0], scalar=-1.0,
                                         in1=rstd[:, which, b, :], op0=ALU.mult, op1=ALU.mult)\
                   .then_inc(nmean_done[which], 1)

            def modulate(n, first):
                m, c = image(n)
                b = n.slot(2)
                if c == 0:
                    hold(dve, q_in[m.slot(2)], m.turn(2, 16, 16), ticks)
                if first >= 2:
                    hold(dve, y_normed, n.val(1, -1), ticks)
                dve.wait_ge(modulated, n.val(1, 1))
                dve.tensor_tensor(y[:, b, :, :], pm[0:TOK, b, :].rearrange("p (t c) -> p t c", c=C),
                                  bhr[0:TOK, :].unsqueeze(1).to_broadcast([TOK, CH, C]), ALU.add).then_inc(biased, 1)
                dve.wait_ge(biased, n.val(1, 1))
                dve.tensor_tensor(y[:, b, :, :], y[:, b, :, :], qin[:, m.slot(2), CH * c:CH * c + CH, :], ALU.mult)\
                   .then_inc(gated, 1)
                dve.wait_ge(gated, n.val(1, 1))
                statistics(n, 0, y[:, b, :, :])

            def residual(n, first):
                m, c = image(n)
                hold(dve, x_biased, n.val(1, 1), ticks)
                dve.wait_ge(projected, n.val(1, 1))
                x = xin[:, m.slot(2), CH * c:CH * c + CH, :]
                dve.tensor_tensor(x, pz[0:TOK, n.slot(2), :].rearrange("p (t c) -> p t c", c=C), x, ALU.add)\
                   .then_inc(x3_made, 1)
                dve.wait_ge(x3_made, n.val(1, 1))
                statistics(n, 1, x)

            def step(n, first, last):
                if first == 0:
                    for k in range(3):
                        if k:
                            negate(n + k - 1, 0)
                        modulate(n + k, k)
                    residual(n, 0)
                if last < -2:
                    negate(n + 2, 0)
                if last < -3:
                    modulate(n + 3, first + 3)
                negate(n, 1)
                if last < -1:
                    residual(n + 1, first + 1)

            run_steps(dve, N, U, step, AHEAD)

        @block.tensor
        def _(pe):
            pe.wait_ge(const_in, CONSTS)
            pe.wait_ge(beta_wide, 1)
            pe.matmul(pm[:, 0, 0:C], bmat[:], wp[:], start=True, stop=True).then_inc(bias_made, 1)
            pe.wait_ge(scaled, 1)
            pe.wait_ge(bias_built, 1)

            def turn_context(n, first):
                m, c = image(n)
                if c == 0:
                    hold(pe, c_in[m.slot(2)], m.turn(2, 32, 32), ticks)
                if first >= 1:
                    hold(pe, cT_out, n.val(), ticks)
                for t in range(CH):
                    ins = pe.transpose(pt[:, t * TOK:(t + 1) * TOK], cin[:, m.slot(2), :, CH * c + t], idn[0:TOK, 0:TOK])
                ins.then_inc(turned, 1)

            def modulator(n, first):
                if first >= 2:
                    hold(pe, biased, n.val(1, -1), ticks)
                pe.wait_ge(cT_out, n.val(1, 1))
                for t in range(CH):
                    ins = pe.matmul(pm[0:TOK, n.slot(2), t * C:(t + 1) * C], cT[:, n.slot(2), t * TOK:(t + 1) * TOK], wh[:],
                                    start=True, stop=True)
                ins.then_inc(modulated, 1)

            def turn_y(n, first):
                hold(pe, y_normed, n.val(1, 1), ticks)
                if first >= 1:
                    hold(pe, yT_out, n.val(), ticks)
                for t in range(CH):
                    ins = pe.transpose(pu[:, t * TOK:(t + 1) * TOK], yn[:, n.slot(2), t, :], idn[0:TOK, 0:TOK])
                ins.then_inc(y_turned, 1)

            def project(n, first):
                if first >= 2:
                    hold(pe, x3_made, n.val(1, -1), ticks)
                pe.wait_ge(yT_out, n.val(1, 1))
                for t in range(CH):
                    ins = pe.matmul(pz[0:TOK, n.slot(2), t * C:(t + 1) * C], yT[:, n.slot(2), t * TOK:(t + 1) * TOK], wpg[:],
                                    start=True, stop=True)
                ins.then_inc(projected, 1)

            def gram_of(n, first, last):
                pe.wait_ge(z_normed, n.val(1, 1))
                for t in range(CH):
                    ins = pe.matmul(pg[:, 0:C + 1], z[:, n.slot(2), t, 0:C], z[:, n.slot(2), t, :],
                                    start=(first == 0 and t == 0), stop=(last == -1 and t == CH - 1))
                ins.then_inc(gram_added, 1)

            def step(n, first, last):
                if first == 0:
                    for k in range(3):
                        turn_context(n + k, k)
                        modulator(n + k, k)
                    turn_y(n, 0)
                    project(n, 0)
                if last < -3:
                    turn_context(n + 3, first + 3)
                if last < -1:
                    turn_y(n + 1, first + 1)
                if last < -3:
                    modulator(n + 3, first + 3)
                if last < -1:
                    project(n + 1, first + 1)
                if first >= 2:
                    gram_of(n - 2, first - 2, last - 2)
                if last == -1:
                    gram_of(n - 1, first - 1, last - 1)
                    gram_of(n, first, last)

            run_steps(pe, N, U, step, AHEAD)


def recurrent_stage(nc, B, x3, gram, W, w_t, v_t, gamma, beta, ident, out):
    TC = 16
    N = PIX // TC
    COLS_ = TC * B
    SUB = 4
    TT = TC // SUB
    ROWS = TT * B
    EPS, EPS_T = 1e-5, 1e-5
    COUNT = float(B * PIX)
    U = 4
    S = Stage(nc, "rec")
    with S.ctx:
        idn = S.sb("idn", [P, P])
        wnat = S.sb("wnat", [C, C])
        wsc = S.sb("wsc", [C, C])
        wt = S.sb("wt", [C, C])
        vt = S.sb("vt", [C, C])
        gr = S.sb("gr", [C, C + 1])
        ones = S.sb("ones", [C, 1])
        gcol, bcol = S.sb("gcol", [C, 1]), S.sb("bcol", [C, 1])
        prod = S.sb("prod", [C, C])
        wbn = S.sb("wbn", [C, C])
        cols = S.sb("cols", [C, 8])
        halfneg = S.sb("halfneg", [P, SUB])
        xin = S.sb("xin", [ROWS, 4, SUB, C])
        stat = S.sb("stat", [ROWS, SUB, 6])
        mv = S.sb("mv", [ROWS, 2, SUB, 2])
        rstd = S.sb("rstd", [ROWS, 2, SUB])
        xn = S.sb("xn", [ROWS, 2, SUB, C])
        xT = S.sb("xT", [C, 2, COLS_])
        yT = S.sb("yT", [C, 2, COLS_])
        res = S.sb("res", [ROWS, 2, SUB, C])
        y0 = S.sb("y0", [C, B])

        pin = S.ps("pin", [P, BANK])
        pout = S.ps("pout", [P, BANK])
        ph = S.ps("ph", [P, 2, BANK])
        ps = S.ps("ps", [P, BANK])

        ticks = S.sem("ticks")
        const_in, filled, setup = S.sem("const_in"), S.sem("filled"), S.sem("setup")
        setup_pe, setup_pool = S.sem("setup_pe"), S.sem("setup_pool")
        x_in = S.sems("x_in", 4)
        stats_part, stats, eps_added, rstd_done, normed = (S.sem(k) for k in ("stats_part", "stats", "eps_added", "rstd_done", "normed"))
        turned, xT_out, driven = S.sem("turned"), S.sem("xT_out"), S.sem("driven")
        added, moved = S.sem("added"), S.sem("moved")
        y_turned, res_made = S.sem("y_turned"), S.sem("res_made")
        stored = S.sems("stored", 2)
        block = S.block()
        CONSTS = 16 * 7

        @block.sync
        def _(sp):
            for dst, src in ((idn[:], ident), (wnat[:], W), (wt[:], w_t), (vt[:], v_t), (gr[:], gram),
                             (gcol[:], dram(gamma, 0, [(1, C), (1, 1)])), (bcol[:], dram(beta, 0, [(1, C), (1, 1)]))):
                sp.dma_start(dst, src).then_inc(const_in, 16)

            def move(tensor, n, tile, sub, sem):
                view = dram(tensor, n.val(TC * C, sub * TT * C), [(C, TT), (PIX * C, B), (1, C)])
                return (sp.dma_start(tile, view) if tensor is x3 else sp.dma_start(view, tile)).then_inc(sem, 16)

            def load(n):
                for sub in range(SUB):
                    move(x3, n, xin[:, n.slot(4), sub, :], sub, x_in[n.slot(4)])

            def step(n, first, last):
                if first == 0:
                    for k in range(3):
                        load(n + k)
                if last < -3:
                    if first >= 1:
                        hold(sp, res_made, n.val(), ticks)
                    load(n + 3)
                hold(sp, res_made, n.val(1, 1), ticks)
                for sub in range(SUB):
                    move(out, n, res[:, n.slot(2), sub, :], sub, stored[n.slot(2)])

            run_steps(sp, N, U, step)
            for s in range(2):
                sp.wait_ge(stored[s], 16 * SUB * (N // 2))

        @block.gpsimd
        def _(pool):
            pool.memset(halfneg[:], -0.5).then_inc(filled, 1)
            pool.memset(ones[:], 1.0).then_inc(filled, 1)
            pool.memset(y0[:], 0.0).then_inc(filled, 1)
            pool.wait_ge(filled, 3)
            pool.wait_ge(setup, 5)
            pool.tensor_tensor(cols[:, 4:5], cols[:, 3:4], halfneg[:, 0:1], ALU.pow).then_inc(setup_pool, 1)

            def norm(n):
                a = n.slot(2)
                hold(pool, stats, n.val(1, 1), ticks)
                pool.tensor_scalar(rstd[:, a, :], mv[:, a, :, 1], EPS_T, None, ALU.add).then_inc(eps_added, 1)
                pool.wait_ge(eps_added, n.val(1, 1))
                pool.tensor_tensor(rstd[:, a, :], rstd[:, a, :], halfneg[0:ROWS, :], ALU.pow).then_inc(rstd_done, 1)
                hold(pool, rstd_done, n.val(1, 1), ticks)
                for t in range(SUB):
                    ins = pool.tensor_scalar(xn[:, a, t, :], xin[:, n.slot(4), t, :], mv[:, a, t, 0:1],
                                             rstd[:, a, t:t + 1], ALU.subtract, ALU.mult)
                ins.then_inc(normed, 1)

            def step(n, first, last):
                if first == 0:
                    norm(n)
                    norm(n + 1)
                if last < -2:
                    pool.wait_ge(turned, n.val(1, 1))
                    norm(n + 2)

            run_steps(pool, N, U, step)

        @block.scalar
        def _(act):
            act.wait_ge(setup, 9)

            def step(n, first, last):
                a = n.slot(2)
                for t in range(TC):
                    cs = slice(t * B, (t + 1) * B)
                    if t == 0 and first >= 2:
                        act.wait_ge(y_turned, n.val(1, -1))
                        act.sem_inc(ticks, 1)
                    act.wait_ge(added, n.val(TC, t + 1))
                    act.activation(yT[:, a, cs], ph[:, a, cs], ACT.Sigmoid, bias=cols[:, 7:8]).then_inc(moved, 1)

            run_steps(act, N, U, step)

        @block.vector
        def _(dve):
            dve.wait_ge(const_in, CONSTS)
            done = [0]

            def then(ins):
                ins.then_inc(setup, 1)
                done[0] += 1
                dve.wait_ge(setup, done[0])

            dve.wait_ge(setup_pe, 1)
            then(dve.tensor_tensor(prod[:], ps[:, 0:C], wt[:], ALU.mult))
            dve.wait_ge(setup_pe, 3)
            then(dve.tensor_scalar(cols[:, 0:2], ps[:, C:C + 2], 1.0 / COUNT, None, ALU.mult))
            then(dve.tensor_tensor(cols[:, 2:3], cols[:, 0:1], cols[:, 0:1], ALU.mult))
            then(dve.tensor_tensor(cols[:, 3:4], cols[:, 1:2], cols[:, 2:3], ALU.subtract))
            then(dve.tensor_scalar(cols[:, 3:4], cols[:, 3:4], EPS, None, ALU.add))
            dve.wait_ge(setup_pool, 1)
            then(dve.tensor_tensor(cols[:, 5:6], cols[:, 4:5], gcol[:], ALU.mult))
            then(dve.tensor_tensor(cols[:, 6:7], cols[:, 5:6], cols[:, 0:1], ALU.mult))
            then(dve.tensor_tensor(cols[:, 7:8], bcol[:], cols[:, 6:7], ALU.subtract))
            then(dve.tensor_scalar(wsc[:], wnat[:], cols[:, 5:6], None, ALU.mult))
            dve.wait_ge(setup_pe, 4)
            then(dve.tensor_copy(wbn[:], ps[:, 128:256]))

            def layer_stats(n):
                a, s = n.slot(2), n.slot(4)
                dve.wait_ge(x_in[s], n.turn(4, 16 * SUB, 16 * SUB))
                for t in range(SUB):
                    dve.bn_stats(stat[:, t, :], xin[:, s, t, :]).then_inc(stats_part, 1)
                hold(dve, stats_part, n.val(SUB, SUB), ticks)
                for t in range(SUB):
                    ins = dve.bn_aggr(mv[:, a, t, :], stat[:, t, :])
                ins.then_inc(stats, 1)

            def drive(n):
                dve.wait_ge(turned, n.val(1, 1))
                dve.tensor_copy(xT[:, n.slot(2), :], pin[:, 0:COLS_]).then_inc(xT_out, 1)

            def finish(n, first):
                if first >= 2:
                    dve.wait_ge(stored[n.slot(2)], n.turn(2, 16 * SUB))
                    dve.sem_inc(ticks, 1)
                dve.wait_ge(y_turned, n.val(1, 1))
                dve.tensor_tensor(res[:, n.slot(2), :, :], pout[0:ROWS, :].rearrange("p (s c) -> p s c", c=C),
                                  xin[:, n.slot(4), :, :], ALU.add).then_inc(res_made, 1)

            def step(n, first, last):
                if first == 0:
                    layer_stats(n)
                    dve.wait_ge(stats, n.val(1, 1))
                    layer_stats(n + 1)
                    drive(n)
                if last < -2:
                    hold(dve, normed, n.val(1, 1), ticks)
                    dve.wait_ge(stats, n.val(1, 2))
                    layer_stats(n + 2)
                if first >= 1:
                    finish(n - 1, first - 1)
                if last < -1:
                    drive(n + 1)
                if last == -1:
                    finish(n, first)

            run_steps(dve, N, U, step)

        @block.tensor
        def _(pe):
            pe.wait_ge(const_in, CONSTS)
            pe.matmul(ps[:, 0:C], gr[:, 0:C], wt[:], start=True, stop=True).then_inc(setup_pe, 1)
            pe.wait_ge(filled, 3)
            pe.wait_ge(setup, 1)
            pe.matmul(ps[:, C:C + 1], wt[:], gr[:, C:C + 1], start=True, stop=True).then_inc(setup_pe, 1)
            pe.matmul(ps[:, C + 1:C + 2], prod[:], ones[:], start=True, stop=True).then_inc(setup_pe, 1)
            pe.wait_ge(setup, 9)
            pe.transpose(ps[:, 128:256], wsc[:], idn[:]).then_inc(setup_pe, 1)

            def turn_in(n, sub):
                if sub == 0:
                    pe.wait_ge(normed, n.val(1, 1))
                ins = pe.transpose(pin[:, sub * ROWS:(sub + 1) * ROWS], xn[:, n.slot(2), sub, :], idn[0:ROWS, 0:ROWS])
                if sub == SUB - 1:
                    ins.then_inc(turned, 1)

            def drive(n, sub):
                if sub == 0:
                    pe.wait_ge(xT_out, n.val(1, 1))
                pe.matmul(ph[:, n.slot(2), sub * ROWS:(sub + 1) * ROWS], wbn[:], xT[:, n.slot(2), sub * ROWS:(sub + 1) * ROWS],
                          start=(sub == 0), stop=False, skip_group_check=True)

            def turn_out(n, sub, first):
                if sub == 0 and first >= 1:
                    pe.wait_ge(res_made, n.val())
                ins = pe.transpose(pout[0:ROWS, sub * C:(sub + 1) * C], yT[:, n.slot(2), sub * ROWS:(sub + 1) * ROWS], idn[:])
                if sub == SUB - 1:
                    ins.then_inc(y_turned, 1)

            pe.wait_ge(setup, 10)

            def add(n, cs, before):
                for r in range(0, C, 32):
                    ins = pe.matmul(ph[r:r + 32, n.slot(2), cs], vt[:, r:r + 32], before, start=False, stop=True,
                                    skip_group_check=True)
                ins.then_inc(added, 1)

            def step(n, first, last):
                a = n.slot(2)
                if first == 0:
                    for sub in range(SUB):
                        turn_in(n, sub)
                    for sub in range(SUB):
                        drive(n, sub)
                for t in range(TC):
                    cs = slice(t * B, (t + 1) * B)
                    if t == 0 and first == 0:
                        add(n, cs, y0[:])
                    else:
                        before = yT[:, a, (t - 1) * B:t * B] if t else yT[:, 1 - a, (TC - 1) * B:TC * B]
                        pe.wait_ge(moved, n.val(TC, t))
                        add(n, cs, before)
                    if t < SUB and first >= 1:
                        turn_out(n - 1, t, first - 1)
                    if SUB <= t < 2 * SUB and last < -1:
                        turn_in(n + 1, t - SUB)
                    if TC - 5 <= t < TC - 1 and last < -1:
                        drive(n + 1, t - (TC - 5))
                if last == -1:
                    pe.wait_ge(moved, n.val(TC, TC))
                    for sub in range(SUB):
                        turn_out(n, sub, first)

            run_steps(pe, N, U, step)


def metaformer_program(nc, B, a):
    def scratch(name, *shape):
        return nc.dram_tensor(name, shape, F32).ap()

    x1 = scratch("x1", B * PIX, C)
    x2 = scratch("x2", B * PIX, C)
    x3 = scratch("x3", B * PIX, C)
    q = scratch("q", B * PIX, C)
    c0 = scratch("c0", GROUPS, P, B, ODD, QUAD)
    gates = scratch("gates", P, 4, B, EVEN)
    ctx_all = scratch("ctx_all", GROUPS, P, B, QUAD, EVEN)
    gram = scratch("gram", C, C + 1)
    attention_stage(nc, B, a["x_windows"], a["w_qkv_t"], a["w_proj_t"], a["b_proj"], a["rpb_rev"],
                    a["shift_mask"], a["ident"], x1)
    expert_stage(nc, B, x1, a["router_w"], a["router_b"], a["expert_w"], a["expert_b"], a["erank"], a["ident"], x2)
    focal_input_stage(nc, B, x2, a["Wf"], a["bf"], a["edge_mask"], a["ident"], q, c0, gates)
    convolution_stage(nc, B, c0, gates, [a["k0"], a["k1"], a["k2"]], a["gap_mask"], ctx_all)
    focal_output_stage(nc, B, ctx_all, q, x2, a["Wh"], a["bh"], a["gamma"], a["beta"], a["Wp"], a["bp"],
                       a["ident"], x3, gram)
    recurrent_stage(nc, B, x3, gram, a["ffn_W"], a["ffn_w_t"], a["ffn_v_t"], a["ffn_gamma"], a["ffn_beta"],
                    a["ident"], a["out"])


def _shape_constants(np):
    tok = np.arange(WTOK)
    row, col = tok // WS, tok % WS
    shift = np.zeros((P, 2, 4, WTOK), np.float32)
    for last_band in range(2):
        for w in range(8):
            part = (row >= WS - SHIFT) * last_band * 2 + (col >= WS - SHIFT) * (w == 7)
            p0 = (w % 2) * 64
            shift[p0:p0 + WTOK, last_band, w // 2] = np.where(part[:, None] != part[None, :], -100.0, 0.0)
    p = np.arange(P)
    pixel = p % ROW < IMG
    edge = np.stack([pixel & (p >= ROW), pixel, pixel, pixel & (p < ROW)], 1).astype(np.float32)
    return {
        "ident": np.eye(P, dtype=np.float32),
        "shift_mask": shift.reshape(P, 2, 4 * WTOK),
        "edge_mask": edge,
        "gap_mask": pixel.astype(np.float32)[:, None],
        "erank": np.tile(np.arange(EXPERTS, 0, -1).astype(np.float32), (P, 1)),
    }


def kernel(**inputs):
    import numpy as np
    import concourse.bacc as bacc
    from concourse.bass_utils import run_bass_kernel_spmd as run

    i = {k: np.asarray(v) for k, v in inputs.items()}
    x = i["x"]
    B = x.shape[0]
    rolled = np.roll(x, (-SHIFT, -SHIFT), (1, 2))
    windows = rolled.reshape(B, 8, WS, 8, WS, C).transpose(0, 1, 3, 2, 4, 5).reshape(B * 64, WTOK, C)
    arrays = {
        "x_windows": windows,
        "w_qkv_t": i["L0_conv_w_qkv"].T,
        "w_proj_t": i["L0_conv_w_proj"].T,
        "b_proj": i["L0_conv_b_proj"],
        "rpb_rev": i["L0_conv_rpb_table"][::-1].T,
        "router_w": i["L0_ffn_router_w"],
        "router_b": i["L0_ffn_router_b"],
        "expert_w": i["L0_ffn_expert_w"],
        "expert_b": i["L0_ffn_expert_b"],
        "Wf": i["L1_conv_Wf"],
        "bf": i["L1_conv_bf"],
        "Wh": i["L1_conv_Wh"],
        "bh": i["L1_conv_bh"],
        "gamma": i["L1_conv_gamma"],
        "beta": i["L1_conv_beta"],
        "Wp": i["L1_conv_Wp"],
        "bp": i["L1_conv_bp"],
        "ffn_W": i["L1_ffn_W"],
        "ffn_w_t": i["L1_ffn_W"].T,
        "ffn_v_t": i["L1_ffn_V"].T,
        "ffn_gamma": i["L1_ffn_gamma"],
        "ffn_beta": i["L1_ffn_beta"],
        **_shape_constants(np),
    }
    for k, size in enumerate(TAPS):
        taps = i[f"L1_conv_k{k}"].reshape(size, size, C)
        arrays[f"k{k}"] = taps[::-1, ::-1].transpose(2, 0, 1)
    arrays = {k: np.ascontiguousarray(v) for k, v in arrays.items()}

    nc = bacc.Bacc("TRN2", target_bir_lowering=False, num_devices=1)
    args = {k: nc.dram_tensor(k, v.shape, F32, kind="ExternalInput").ap() for k, v in arrays.items()}
    args["out"] = nc.dram_tensor("out", (B, IMG, IMG, C), F32, kind="ExternalOutput").ap()
    metaformer_program(nc, B, args)
    return run(nc, [arrays], core_ids=[0]).results[0]["out"]
```

```python
from contextlib import ExitStack

import concourse.bass as bass
from concourse import mybir

F32 = mybir.dt.float32
ALU = mybir.AluOpType
ACT = mybir.ActivationFunctionType
AX = mybir.AxisListType

P = 128
C = 128
IMG = 56
PIX = IMG * IMG
WS = 7
SHIFT = 3
WTOK = WS * WS
HEADS = 4
HD = C // HEADS
EXPERTS = 8
TAPS = (3, 5, 7)
BANK = 512


MANY = 1 << 20


class Step:

    def __init__(self, loop, unroll, off):
        self.loop, self.unroll, self.off = loop, unroll, off
        self.is_static = isinstance(loop, int)

    def __add__(self, k):
        return Step(self.loop, self.unroll, self.off + k)

    def __sub__(self, k):
        return self + -k

    def val(self, scale=1, plus=0):
        return self.loop * (self.unroll * scale) + (self.off * scale + plus)

    def slot(self, n):
        assert self.unroll % n == 0
        return self.off % n

    def turn(self, n, scale=1, plus=0):
        return self.loop * (self.unroll // n * scale) + (self.off // n * scale + plus)


def run_steps(eng, count, unroll, step, ahead=3):
    rounds = (count - 1 - ahead) // unroll
    if rounds < 3:
        for n in range(count):
            step(Step(0, unroll, n), n, n - count)
        return
    for n in range(unroll):
        step(Step(0, unroll, n), n, n - count)
    with eng.Fori(1, rounds) as it:
        for u in range(unroll):
            step(Step(it, unroll, u), MANY, -MANY)
    for n in range(rounds * unroll, count):
        step(Step(0, unroll, n), n, n - count)


def hold(eng, sem, value, ticks):
    eng.wait_ge(sem, value)
    eng.sem_inc(ticks, 1)


class Stage:

    def __init__(self, nc, name):
        self.nc, self.name, self.ctx, self.used = nc, name, ExitStack(), []

    def sb(self, name, shape):
        return self.ctx.enter_context(self.nc.sbuf_tensor(f"{self.name}_{name}", shape, F32))

    def ps(self, name, shape):
        return self.ctx.enter_context(self.nc.psum_tensor(f"{self.name}_{name}", shape, F32))

    def sem(self, name):
        self.used.append(self.ctx.enter_context(self.nc.semaphore(f"{self.name}_{name}")))
        return self.used[-1]

    def sems(self, name, n):
        return [self.sem(f"{name}{i}") for i in range(n)]

    def clear(self):
        with self.nc.Block() as block:
            @block.gpsimd
            def _(pool):
                for sem in self.used:
                    pool.sem_clear(sem)

    def block(self):
        self.ctx.callback(self.clear)
        return self.ctx.enter_context(self.nc.Block())


def dram(ap, offset, dims):
    return bass.AP(ap.tensor, offset, [list(d) for d in dims])


def row_to_all(ap, n, offset=0):
    return dram(ap, offset, [(0, P), (1, n)])


def attention_stage(nc, B, x_win, w_qkv_t, w_proj_t, b_proj, rpb_rev, shift_mask, ident, x1):
    N = B * 8
    PAIRS, W = 4, 8
    SCALE = float(HD) ** -0.5
    EPS = 1e-6
    U = 8
    S = Stage(nc, "att")
    with S.ctx:
        idn = S.sb("idn", [P, P])
        wqkv = S.sb("wqkv", [C, 3 * C])
        wproj = S.sb("wproj", [C, C])
        bproj = S.sb("bproj", [P, C])
        halfneg = S.sb("halfneg", [P, PAIRS])
        mask = S.sb("mask", [P, 2, PAIRS * WTOK])
        bias = S.sb("bias", [P, 2, HEADS, PAIRS * WTOK])
        relb = S.sb("relb", [P, HEADS, WTOK])
        xin = S.sb("xin", [P, 8, PAIRS, C])
        stat = S.sb("stat", [P, 4, PAIRS, 6])
        mv = S.sb("mv", [P, 4, PAIRS, 2])
        rstd = S.sb("rstd", [P, 4, PAIRS])
        xn = S.sb("xn", [P, 4, PAIRS, C])
        xnT = S.sb("xnT", [C, W * WTOK])
        qT = S.sb("qT", [C, W * WTOK])
        kT = S.sb("kT", [C, W * WTOK])
        vv = S.sb("vv", [P, 2, W, 2 * HD])
        sc = S.sb("sc", [P, PAIRS * HEADS, 64])
        pr = S.sb("pr", [P, PAIRS * HEADS, 64])
        mx = S.sb("mx", [P, PAIRS * HEADS])
        sm = S.sb("sm", [P, PAIRS * HEADS])
        rs = S.sb("rs", [P, PAIRS * HEADS])
        prT = S.sb("prT", [P, 2, PAIRS, P])
        oT = S.sb("oT", [C, W, 64])
        x1s = S.sb("x1s", [P, 2, PAIRS, C])

        rel_dram = nc.dram_tensor("rel_dram", (HEADS, WTOK, WTOK), F32).ap()

        psc = S.ps("psc", [P, HEADS, BANK])
        pf = S.ps("pf", [P, 2, BANK])
        pb = S.ps("pb", [P, 2, BANK])

        const_in = S.sem("const_in")
        ticks = S.sem("ticks")
        rel_in, rel_spread = S.sem("rel_in"), S.sem("rel_spread")
        zeroed_v = S.sem("zeroed_v")
        zeroed_p = S.sem("zeroed_p")
        rel_zero = S.sem("rel_zero")
        bias_built = S.sem("bias_built")
        x_in = S.sems("x_in", 8)
        stats_part = S.sem("stats_part")
        stats = S.sem("stats")
        eps_added = S.sem("eps_added")
        rstd_done = S.sem("rstd_done")
        centred = S.sem("centred")
        normed = S.sem("normed")
        bproj_added = S.sem("bproj_added")
        f0_full, f1_full = S.sem("f0_full"), S.sem("f1_full")
        xT_out, q_out, k_out, v_out = (S.sem(f"{n}_out") for n in ("xT", "q", "k", "v"))
        scored = S.sem("scored")
        biased = S.sem("biased")
        maxed = S.sem("maxed")
        shifted = S.sem("shifted")
        exped = S.sem("exped")
        summed = S.sem("summed")
        inverted = S.sem("inverted")
        probs = S.sem("probs")
        turned = S.sems("turned", 2)
        prT_out = S.sems("prT_out", 2)
        attended = S.sem("attended")
        oT_out = S.sem("oT_out")
        projected = S.sem("projected")
        x1_ready = S.sem("x1_ready")
        x1_out = S.sems("x1_out", 2)
        block = S.block()

        @block.sync
        def _(sp):
            for dst, src in ((idn[:], ident), (wqkv[:], w_qkv_t), (wproj[:], w_proj_t),
                             (bproj[:], row_to_all(b_proj, C)), (mask[:], shift_mask)):
                sp.dma_start(dst, src).then_inc(const_in, 16)
            SIDE = 2 * WS - 1
            for h in range(HEADS):
                for r1 in range(WS):
                    off = h * SIDE * SIDE + (WS - 1 - r1) * SIDE + WS - 1
                    sp.dma_start(dram(rel_dram, (h * WTOK + r1 * WS) * WTOK, [(WS, WS), (WTOK, WS), (1, WS)]),
                                 dram(rpb_rev, off, [(SIDE, WS), (-1, WS), (1, WS)])).then_inc(rel_spread, 16)
            sp.wait_ge(rel_spread, 16 * HEADS * WS)
            sp.wait_ge(rel_zero, 1)
            for base in (0, 64):
                sp.dma_start(relb[base:base + WTOK, :, :],
                             dram(rel_dram, 0, [(WTOK, WTOK), (WTOK * WTOK, HEADS), (1, WTOK)])).then_inc(rel_in, 16)

            def load(n):
                s = n.slot(8)
                for odd in range(2):
                    src = dram(x_win, n.val(W * WTOK * C, odd * WTOK * C),
                               [(C, WTOK), (2 * WTOK * C, PAIRS), (1, C)])
                    sp.dma_start(xin[odd * 64:odd * 64 + WTOK, s, :, :], src).then_inc(x_in[s], 16)

            def step(n, first, last):
                if first == 0:
                    for k in range(6):
                        load(n + k)
                if last < -6:
                    if first >= 2:
                        hold(sp, x1_ready, n.val(1, -1), ticks)
                    load(n + 6)
                hold(sp, x1_ready, n.val(1, 1), ticks)
                for pair in range(PAIRS):
                    for odd in range(2):
                        off = n.val(WS * IMG * C, (2 * pair + odd) * WS * C)
                        sp.dma_start(dram(x1, off, [(IMG * C, WS), (C, WS), (1, C)]),
                                     x1s[odd * 64:odd * 64 + WTOK, n.slot(2), pair, :]).then_inc(x1_out[n.slot(2)], 16)

            sp.wait_ge(zeroed_p, 8)
            run_steps(sp, N, U, step, 6)
            for s in range(2):
                sp.wait_ge(x1_out[s], 16 * W * ((N + 1 - s) // 2))

        @block.gpsimd
        def _(pool):
            for s in range(8):
                pool.memset(xin[:, s, :, :], 0.0).then_inc(zeroed_p, 1)
            pool.memset(halfneg[:], -0.5).then_inc(zeroed_p, 1)
            pool.memset(oT[:], 0.0).then_inc(zeroed_p, 1)
            pool.memset(pr[:], 0.0).then_inc(zeroed_p, 1)
            pool.wait_ge(zeroed_p, 11)
            pool.wait_ge(const_in, 80)

            def norm(n):
                a, s = n.slot(4), n.slot(8)
                hold(pool, stats, n.val(1, 1), ticks)
                pool.tensor_scalar(rstd[:, a, :], mv[:, a, :, 1], EPS, None, ALU.add).then_inc(eps_added, 1)
                pool.wait_ge(eps_added, n.val(1, 1))
                pool.tensor_tensor(rstd[:, a, :], rstd[:, a, :], halfneg[:], ALU.pow).then_inc(rstd_done, 1)
                pool.wait_ge(rstd_done, n.val(1, 1))
                pool.sem_inc(ticks, 1)
                for t in range(PAIRS):
                    ins = pool.tensor_scalar(xn[:, a, t, :], xin[:, s, t, :], mv[:, a, t, 0:1],
                                             rstd[:, a, t:t + 1], ALU.subtract, ALU.mult)
                ins.then_inc(normed, 1)
                pool.wait_ge(normed, n.val(1, 1))
                pool.tensor_tensor(xin[:, s, :, :], xin[:, s, :, :],
                                   bproj[:].unsqueeze(1).to_broadcast([P, PAIRS, C]), ALU.add).then_inc(bproj_added, 1)

            def step(n, first, last):
                if first == 0:
                    norm(n)
                    norm(n + 1)
                if last < -2:
                    if first >= 2:
                        pool.wait_ge(xT_out, n.val(1, -1))
                        pool.sem_inc(ticks, 1)
                    norm(n + 2)

            run_steps(pool, N, U, step)

        @block.scalar
        def _(act):
            def copy(out, in_):
                return act.activation(out, in_, ACT.Copy)

            def tokens(n):
                act.wait_ge(f0_full, n.val(2, 1))
                copy(xnT[:].rearrange("c (w t) -> c w t", t=WTOK),
                     pf[:, 0, :].rearrange("c (w t) -> c w t", t=64)[:, :, 0:WTOK]).then_inc(xT_out, 1)

            def qk(n):
                act.wait_ge(f1_full, n.val(2, 1))
                act.activation(qT[:], pf[:, 1, 0:W * WTOK], ACT.Copy, scale=SCALE).then_inc(q_out, 1)
                act.wait_ge(f0_full, n.val(2, 2))
                copy(kT[:], pf[:, 0, 0:W * WTOK]).then_inc(k_out, 1)

            def values(n):
                act.wait_ge(f1_full, n.val(2, 2))
                copy(vv[:, n.slot(2), :, :].rearrange("t w c -> t (w c)"), pf[:, 1, :]).then_inc(v_out, 1)

            def probs_by_key(n):
                for half in range(2):
                    act.wait_ge(turned[half], n.val(1, 1))
                    copy(prT[:, half, :, :].rearrange("t q i -> t (q i)"), pb[:, half, :]).then_inc(prT_out[half], 1)

            def exp(n):
                act.wait_ge(shifted, n.val(1, 1))
                act.activation(pr[:, :, 0:WTOK], sc[:, :, 0:WTOK], ACT.Exp).then_inc(exped, 1)

            def attended_out(n):
                act.wait_ge(attended, n.val(1, 1))
                copy(oT[:, :, 0:WTOK], pb[:, 0, 0:W * WTOK].rearrange("c (w t) -> c w t", t=WTOK)).then_inc(oT_out, 1)

            act.wait_ge(zeroed_p, 11)

            def step(n, first, last):
                if first == 0:
                    tokens(n)
                    qk(n)
                    values(n)
                if last < -1:
                    tokens(n + 1)
                if first >= 1:
                    probs_by_key(n - 1)
                if last < -1:
                    qk(n + 1)
                exp(n)
                if first >= 1:
                    attended_out(n - 1)
                if last < -1:
                    values(n + 1)
                if last == -1:
                    probs_by_key(n)
                    attended_out(n)

            run_steps(act, N, U, step)

        @block.vector
        def _(dve):
            dve.memset(relb[:], 0.0).then_inc(rel_zero, 1)
            dve.memset(psc[:], 0.0).then_inc(zeroed_v, 1)
            dve.memset(pf[:], 0.0).then_inc(zeroed_v, 1)
            dve.wait_ge(zeroed_p, 11)
            dve.wait_ge(const_in, 80)
            dve.wait_ge(rel_in, 32)
            for kind in range(2):
                for h in range(HEADS):
                    dve.tensor_tensor(bias[:, kind, h, :].rearrange("p (q j) -> p q j", j=WTOK),
                                      mask[:, kind, :].rearrange("p (q j) -> p q j", j=WTOK),
                                      relb[:, h, :].unsqueeze(1).to_broadcast([P, PAIRS, WTOK]),
                                      ALU.add).then_inc(bias_built, 1)

            def layer_stats(n):
                a, s = n.slot(4), n.slot(8)
                dve.wait_ge(x_in[s], n.turn(8, 32, 32))
                for t in range(PAIRS):
                    dve.bn_stats(stat[:, a, t, :], xin[:, s, t, :]).then_inc(stats_part, 1)
                hold(dve, stats_part, n.val(PAIRS, PAIRS), ticks)
                for t in range(PAIRS):
                    ins = dve.bn_aggr(mv[:, a, t, :], stat[:, a, t, :])
                ins.then_inc(stats, 1)

            def softmax_front(n, kind):
                dve.wait_ge(scored, n.val(1, 1))
                dve.tensor_tensor(sc[:].rearrange("p (q h) j -> p h q j", h=HEADS)[:, :, :, 0:WTOK],
                                  psc[:, :, 0:PAIRS * WTOK].rearrange("p h (q j) -> p h q j", j=WTOK),
                                  bias[:, kind, :, :].rearrange("p h (q j) -> p h q j", j=WTOK), ALU.add).then_inc(biased, 1)
                dve.wait_ge(biased, n.val(1, 1))
                dve.tensor_reduce(mx[:], sc[:, :, 0:WTOK], AX.X, ALU.max).then_inc(maxed, 1)
                dve.wait_ge(maxed, n.val(1, 1))
                dve.tensor_tensor(sc[:, :, 0:WTOK], sc[:, :, 0:WTOK],
                                  mx[:].unsqueeze(2).to_broadcast([P, HEADS * PAIRS, WTOK]),
                                  ALU.subtract).then_inc(shifted, 1)

            def softmax_back(n):
                dve.wait_ge(exped, n.val(1, 1))
                dve.tensor_reduce(sm[:], pr[:, :, 0:WTOK], AX.X, ALU.add).then_inc(summed, 1)
                dve.wait_ge(summed, n.val(1, 1))
                dve.reciprocal(rs[:], sm[:]).then_inc(inverted, 1)
                dve.wait_ge(inverted, n.val(1, 1))
                dve.tensor_tensor(pr[:, :, 0:WTOK], pr[:, :, 0:WTOK],
                                  rs[:].unsqueeze(2).to_broadcast([P, HEADS * PAIRS, WTOK]),
                                  ALU.mult).then_inc(probs, 1)

            def residual(n, first):
                dve.wait_ge(projected, n.val(1, 1))
                dve.wait_ge(bproj_added, n.val(1, 1))
                if first >= 2:
                    dve.wait_ge(x1_out[n.slot(2)], n.turn(2, 16 * W))
                dve.tensor_tensor(x1s[:, n.slot(2), :, :].rearrange("p q c -> p (q c)"), pb[:, 1, :],
                                  xin[:, n.slot(8), :, :].rearrange("p q c -> p (q c)"), ALU.add).then_inc(x1_ready, 1)

            dve.wait_ge(bias_built, 2 * HEADS)

            def step(n, first, last):
                kind = n.slot(8) == 7
                if first == 0:
                    for k in range(3):
                        layer_stats(n + k)
                softmax_front(n, int(kind))
                if last < -3:
                    if first >= 1:
                        dve.wait_ge(normed, n.val())
                        dve.sem_inc(ticks, 1)
                    layer_stats(n + 3)
                softmax_back(n)
                if first >= 1:
                    residual(n - 1, first - 1)
                if last == -1:
                    residual(n, first)

            run_steps(dve, N, U, step)

        @block.tensor
        def _(pe):
            pe.wait_ge(const_in, 80)
            pe.wait_ge(zeroed_v, 2)
            pe.wait_ge(zeroed_p, 11)

            def turn(n, first):
                pe.wait_ge(normed, n.val(1, 1))
                if first >= 1:
                    pe.wait_ge(k_out, n.val())
                for t in range(PAIRS):
                    ins = pe.transpose(pf[:, 0, t * P:(t + 1) * P], xn[:, n.slot(4), t, :], idn[:])
                ins.then_inc(f0_full, 1)

            def qk(n, first):
                pe.wait_ge(xT_out, n.val(1, 1))
                if first >= 1:
                    pe.wait_ge(v_out, n.val())
                pe.matmul(pf[:, 1, 0:W * WTOK], wqkv[:, 0:C], xnT[:], start=True, stop=True).then_inc(f1_full, 1)
                pe.matmul(pf[:, 0, 0:W * WTOK], wqkv[:, C:2 * C], xnT[:], start=True, stop=True).then_inc(f0_full, 1)

            def values(n):
                pe.wait_ge(q_out, n.val(1, 1))
                wv = wqkv[:, 2 * C:3 * C].rearrange("c (g o d) -> c o g d", o=2, d=HD)
                for w in range(W):
                    for odd in range(2):
                        ins = pe.matmul(pf[odd * 64:odd * 64 + WTOK, 1, w * 64:(w + 1) * 64],
                                        xnT[:, w * WTOK:(w + 1) * WTOK], wv[:, odd], start=True, stop=True)
                ins.then_inc(f1_full, 1)

            def scores(n, first):
                pe.wait_ge(k_out, n.val(1, 1))
                if first >= 1:
                    hold(pe, biased, n.val(), ticks)
                for pair in range(PAIRS):
                    for h in range(HEADS):
                        for w in (2 * pair, 2 * pair + 1):
                            p0 = (w % 2) * 64
                            ins = pe.matmul(psc[p0:p0 + WTOK, h, pair * WTOK:(pair + 1) * WTOK],
                                            qT[h * HD:(h + 1) * HD, w * WTOK:(w + 1) * WTOK],
                                            kT[h * HD:(h + 1) * HD, w * WTOK:(w + 1) * WTOK], start=True, stop=True)
                ins.then_inc(scored, 1)

            def turn_probs(n, first):
                hold(pe, probs, n.val(1, 1), ticks)
                if first >= 1:
                    pe.wait_ge(oT_out, n.val())
                for half in range(2):
                    if half == 1 and first >= 1:
                        hold(pe, x1_ready, n.val(), ticks)
                    for pair in range(PAIRS):
                        at = pair * HEADS + 2 * half
                        ins = pe.transpose(pb[:, half, pair * P:(pair + 1) * P],
                                           pr[:, at:at + 2, :].rearrange("p h j -> p (h j)"), idn[:])
                    ins.then_inc(turned[half], 1)

            def attend(n):
                hold(pe, v_out, n.val(1, 1), ticks)
                for half in range(2):
                    hold(pe, prT_out[half], n.val(1, 1), ticks)
                for w in range(W):
                    pair, i0 = w // 2, (w % 2) * 64
                    for h in range(HEADS):
                        k0, g = (h % 2) * 64, h // 2
                        ins = pe.matmul(pb[h * HD:(h + 1) * HD, 0, w * WTOK:(w + 1) * WTOK],
                                        vv[k0:k0 + WTOK, n.slot(2), w, g * HD:(g + 1) * HD],
                                        prT[k0:k0 + WTOK, g, pair, i0:i0 + WTOK], start=True, stop=True)
                ins.then_inc(attended, 1)

            def project(n):
                pe.wait_ge(oT_out, n.val(1, 1))
                for pair in range(PAIRS):
                    ins = pe.matmul(pb[:, 1, pair * C:(pair + 1) * C],
                                    oT[:, 2 * pair:2 * pair + 2, :].rearrange("c w t -> c (w t)"), wproj[:],
                                    start=True, stop=True)
                ins.then_inc(projected, 1)

            def step(n, first, last):
                if first == 0:
                    turn(n, 0)
                    qk(n, 0)
                    values(n)
                if last < -1:
                    turn(n + 1, 1)
                scores(n, first)
                if first >= 1:
                    turn_probs(n - 1, first - 1)
                if last < -1:
                    qk(n + 1, 1)
                if first >= 1:
                    attend(n - 1)
                if last < -1:
                    values(n + 1)
                if first >= 1:
                    project(n - 1)
                if last == -1:
                    turn_probs(n, first)
                    attend(n)
                    project(n)

            run_steps(pe, N, U, step)


def expert_stage(nc, B, x1, router_w, router_b, expert_w, expert_b, erank, ident, x2):
    T = 7
    GROUP = T * P
    N = B * PIX // GROUP
    EPS = 1e-5
    E = EXPERTS
    NOT_CHOSEN = -1e38
    ROUTE_OPS = 19
    GAP_READY = 13
    TP = 5
    U = 6
    S = Stage(nc, "moe")
    with S.ctx:
        idn = S.sb("idn", [P, P])
        wr = S.sb("wr", [C, E])
        br = S.sb("br", [P, E])
        we = S.sb("we", [C, E, C])
        be = S.sb("be", [E, C])
        rank = S.sb("rank", [P, E])
        halfneg = S.sb("halfneg", [P, T])
        xin = S.sb("xin", [P, 3, T, C])
        stat = S.sb("stat", [P, 2, T, 6])
        mv = S.sb("mv", [P, 2, T, 2])
        rstd = S.sb("rstd", [P, 2, T])
        nmean = S.sb("nmean", [P, 2, T])
        xn = S.sb("xn", [P, 2, T, C])
        xnT = S.sb("xnT", [C, 2, T, P])
        logit = S.sb("logit", [P, T, E])
        rest = S.sb("rest", [P, T, E])
        hit = S.sb("hit", [P, 2, T, E])
        ranked = S.sb("ranked", [P, 2, T, E])
        one = S.sb("one", [P, 2, T, E])
        best = S.sb("best", [P, 2, T])
        top = S.sb("top", [P, 2, T])
        gap = S.sb("gap", [P, T])
        second = S.sb("second", [P, T])
        total = S.sb("total", [P, T])
        share = S.sb("share", [P, 2, T])
        part = S.sb("part", [P, 2, T, E])
        gate = S.sb("gate", [P, 2, T, E])
        gateT = S.sb("gateT", [E, T, P])
        acc = S.sb("acc", [P, 3, T, C])
        odd = S.sb("odd", [P, 2, C])
        scaled = S.sb("scaled", [P, 2, 4, C])
        paired = S.sb("paired", [P, 2, 2, C])
        others = S.sb("others", [P, 2, C])

        px = S.ps("px", [P, 2, BANK])
        pr = S.ps("pr", [P, BANK])
        pe_out = S.ps("pe_out", [P, 2, 2, BANK])

        ticks = S.sem("ticks")
        const_in = S.sem("const_in")
        filled = S.sem("filled")
        x_in = S.sems("x_in", 3)
        stats_part, stats = S.sem("stats_part"), S.sem("stats")
        eps_added, rstd_done, normed = S.sem("eps_added"), S.sem("rstd_done"), S.sem("normed")
        nmean_done, normed_act = S.sem("nmean_done"), S.sem("normed_act")
        turned, xT_out = S.sems("turned", 2), S.sems("xT_out", 2)
        logits_made = S.sem("logits_made")
        routing = S.sem("routing")
        second_ready = S.sem("second_ready")
        gates_turned, gT_out = S.sems("gates_turned", 2), S.sems("gT_out", 2)
        bias_made, acc_begun = S.sems("bias_made", 2), S.sems("acc_begun", 2)
        expert_done = S.sem("expert_done")
        mixing, joined, mixed = S.sem("mixing"), S.sem("joined"), S.sem("mixed")
        scaled_ready, paired_ready, others_ready = S.sem("scaled_ready"), S.sem("paired_ready"), S.sem("others_ready")
        x2_out = S.sems("x2_out", 3)
        block = S.block()
        HALVES = ((0, 4), (4, T))
        CONSTS = 16 * 6

        @block.sync
        def _(sp):
            for dst, src in ((idn[:], ident), (wr[:], router_w), (br[:], row_to_all(router_b, E)),
                             (we[:], dram(expert_w, 0, [(C, C), (C * C, E), (1, C)])),
                             (be[:], expert_b), (rank[:], erank)):
                sp.dma_start(dst, src).then_inc(const_in, 16)

            def load(n):
                sp.dma_start(xin[:, n.slot(3), :, :], dram(x1, n.val(GROUP * C), [(T * C, P), (1, T * C)]))\
                  .then_inc(x_in[n.slot(3)], 16)

            def step(n, first, last):
                if first == 0:
                    for k in range(min(3, N)):
                        load(n + k)
                if last < -3:
                    hold(sp, acc_begun[1], n.val(1, 1), ticks)
                    load(n + 3)
                hold(sp, mixed, n.val(T, T), ticks)
                sp.dma_start(dram(x2, n.val(GROUP * C), [(T * C, P), (1, T * C)]), acc[:, n.slot(3), :, :])\
                  .then_inc(x2_out[n.slot(3)], 16)

            run_steps(sp, N, U, step, 4)
            for s in range(3):
                sp.wait_ge(x2_out[s], 16 * ((N + 2 - s) // 3))

        @block.gpsimd
        def _(pool):
            pool.memset(halfneg[:], -0.5).then_inc(filled, 1)
            pool.wait_ge(filled, 1)

            def scale(n, first):
                a = n.slot(2)
                if first >= 2:
                    hold(pool, normed_act, n.val(1, -1), ticks)
                hold(pool, stats, n.val(1, 1), ticks)
                pool.tensor_scalar(rstd[:, a, :], mv[:, a, :, 1], EPS, None, ALU.add).then_inc(eps_added, 1)
                pool.wait_ge(eps_added, n.val(1, 1))
                pool.tensor_tensor(rstd[:, a, :], rstd[:, a, :], halfneg[:], ALU.pow).then_inc(rstd_done, 1)

            def norm(n, t):
                a = n.slot(2)
                if t == 0:
                    hold(pool, rstd_done, n.val(1, 1), ticks)
                pool.tensor_scalar(xn[:, a, t, :], xin[:, n.slot(3), t, :], mv[:, a, t, 0:1],
                                   rstd[:, a, t:t + 1], ALU.subtract, ALU.mult).then_inc(normed, 1)

            def pair(n, t, first):
                b = (n.off * T + t) % 2
                hold(pool, scaled_ready, n.val(T, t + 1), ticks)
                pool.tensor_tensor(paired[:, b, :, :], scaled[:, b, 0:2, :], scaled[:, b, 2:4, :], ALU.add)\
                    .then_inc(paired_ready, 1)

            def join(n, t, first):
                b = (n.off * T + t) % 2
                if first >= 1 or t >= 2:
                    hold(pool, mixed, n.val(T, t - 1), ticks)
                pool.wait_ge(paired_ready, n.val(T, t + 1))
                pool.tensor_tensor(others[:, b, :], paired[:, b, 0, :], paired[:, b, 1, :], ALU.add)\
                    .then_inc(others_ready, 1)

            def step(n, first, last):
                if first == 0:
                    for k in range(2):
                        scale(n + k, k)
                        for t in range(TP):
                            norm(n + k, t)
                for t in range(T):
                    pair(n, t, first)
                    if 1 <= t <= TP and last < -2:
                        norm(n + 2, t - 1)
                    join(n, t, first)
                    if t == 0 and last < -2:
                        scale(n + 2, first + 2)
                        hold(pool, turned[1], n.val(1, 1), ticks)

            run_steps(pool, N, U, step, 4)

        @block.scalar
        def _(act):
            def front(n, first):
                if first >= 1:
                    act.wait_ge(mixed, n.val(T, -T))
                for b, (t0, t1) in enumerate(HALVES):
                    act.wait_ge(turned[b], n.val(1, 1))
                    act.activation(xnT[:, n.slot(2), t0:t1, :], px[:, b, 0:(t1 - t0) * P], ACT.Copy).then_inc(xT_out[b], 1)

            def norm(n):
                a = n.slot(2)
                hold(act, nmean_done, n.val(1, 1), ticks)
                for t in range(TP, T):
                    ins = act.activation(xn[:, a, t, :], xin[:, n.slot(3), t, :], ACT.Identity,
                                         bias=nmean[:, a, t:t + 1], scale=rstd[:, a, t:t + 1])
                ins.then_inc(normed_act, 1)

            def second_weight(n):
                act.wait_ge(routing, n.val(ROUTE_OPS, GAP_READY))
                act.activation(second[:], gap[:], ACT.Exp).then_inc(second_ready, 1)

            def gates(n):
                for b, (t0, t1) in enumerate(HALVES):
                    act.wait_ge(gates_turned[b], n.val(1, 1))
                    act.activation(gateT[:, t0:t1, :], px[0:E, b, 0:(t1 - t0) * P], ACT.Copy).then_inc(gT_out[b], 1)

            def pick(n, t, first):
                b = (n.off * T + t) % 2
                if first >= 1 or t >= 2:
                    act.wait_ge(paired_ready, n.val(T, t - 1))
                    act.sem_inc(ticks, 1)
                act.wait_ge(expert_done, n.val(T, t + 1))
                for e in range(4):
                    g = gate[:, n.slot(2), t, 4 + e:5 + e]
                    ins = act.activation(scaled[:, b, e, :], pe_out[:, b, 1, e * C:(e + 1) * C], ACT.Identity, scale=g)
                ins.then_inc(scaled_ready, 1)

            def step(n, first, last):
                if first == 0:
                    norm(n)
                    norm(n + 1)
                    front(n, 0)
                    second_weight(n)
                    gates(n)
                for t in range(T):
                    pick(n, t, first)
                    if last < -1:
                        if t == 0:
                            front(n + 1, first)
                        if t == 3:
                            second_weight(n + 1)
                        if t == 5:
                            gates(n + 1)
                    if t == 4 and last < -2:
                        norm(n + 2)

            run_steps(act, N, U, step, 4)

        @block.vector
        def _(dve):
            dve.wait_ge(const_in, CONSTS)

            def layer_stats(n, t0, t1):
                a, s = n.slot(2), n.slot(3)
                if t0 == 0:
                    hold(dve, x_in[s], n.turn(3, 16, 16), ticks)
                for t in range(t0, t1):
                    dve.bn_stats(stat[:, a, t, :], xin[:, s, t, :]).then_inc(stats_part, 1)

            def negate(n):
                a = n.slot(2)
                hold(dve, rstd_done, n.val(1, 1), ticks)
                dve.scalar_tensor_tensor(out=nmean[:, a, TP:T], in0=mv[:, a, TP:T, 0], scalar=-1.0, in1=rstd[:, a, TP:T],
                                         op0=ALU.mult, op1=ALU.mult).then_inc(nmean_done, 1)

            def layer_stats_end(n):
                a = n.slot(2)
                hold(dve, stats_part, n.val(T, T), ticks)
                for t in range(T):
                    ins = dve.bn_aggr(mv[:, a, t, :], stat[:, a, t, :])
                ins.then_inc(stats, 1)

            ranks = rank[:].unsqueeze(1).to_broadcast([P, T, E])

            def wide(x):
                return x.unsqueeze(2).to_broadcast([P, T, E])

            def route(n, k):
                if k == 0:
                    dve.wait_ge(logits_made, n.val(1, 1))
                    ins = dve.tensor_tensor(logit[:], pr[:, 0:T * E].rearrange("p (t e) -> p t e", e=E),
                                            br[:].unsqueeze(1).to_broadcast([P, T, E]), ALU.add)
                    ins.then_inc(routing, 1)
                    return
                if k == 13:
                    hold(dve, second_ready, n.val(1, 1), ticks)
                dve.wait_ge(routing, n.val(ROUTE_OPS, k))
                i = 0 if k <= 6 else 1
                x, at = (logit, rest)[i], (1, 7)[i]
                if k == at:
                    ins = dve.tensor_reduce(best[:, i, :], x[:], AX.X, ALU.max)
                elif k == at + 1:
                    ins = dve.tensor_tensor(hit[:, i, :, :], x[:], wide(best[:, i, :]), ALU.is_equal)
                elif k == at + 2:
                    ins = dve.tensor_tensor(ranked[:, i, :, :], hit[:, i, :, :], ranks, ALU.mult)
                elif k == at + 3:
                    ins = dve.tensor_reduce(top[:, i, :], ranked[:, i, :, :], AX.X, ALU.max)
                elif k == at + 4:
                    ins = dve.tensor_tensor(one[:, i, :, :], ranked[:, i, :, :], wide(top[:, i, :]), ALU.is_equal)
                elif k == 6:
                    ins = dve.scalar_tensor_tensor(out=rest[:], in0=one[:, 0, :, :], scalar=NOT_CHOSEN,
                                                   in1=logit[:], op0=ALU.mult, op1=ALU.add)
                elif k == 12:
                    ins = dve.tensor_tensor(gap[:], best[:, 1, :], best[:, 0, :], ALU.subtract)
                elif k == 13:
                    ins = dve.tensor_scalar(total[:], second[:], 1.0, None, ALU.add)
                elif k == 14:
                    ins = dve.reciprocal(share[:, 0, :], total[:])
                elif k == 15:
                    ins = dve.tensor_tensor(share[:, 1, :], share[:, 0, :], second[:], ALU.mult)
                elif k in (16, 17):
                    ins = dve.tensor_tensor(part[:, k - 16, :, :], one[:, k - 16, :, :], wide(share[:, k - 16, :]), ALU.mult)
                else:
                    ins = dve.tensor_tensor(gate[:, n.slot(2), :, :], part[:, 0, :, :], part[:, 1, :, :], ALU.add)
                ins.then_inc(routing, 1)

            def route_between(n, t, place, more):
                k = 6 * (t - 1) + place - 4
                if more and 0 <= k < ROUTE_OPS:
                    route(n + 1, k)

            def begin(n, first):
                if first >= 2:
                    dve.wait_ge(x2_out[n.slot(3)], n.turn(3, 16))
                for b, (t0, t1) in enumerate(HALVES):
                    dve.wait_ge(bias_made[b], n.val(1, 1))
                    dve.tensor_tensor(acc[:, n.slot(3), t0:t1, :],
                                      px[:, b, 0:(t1 - t0) * C].rearrange("p (t c) -> p t c", c=C),
                                      xin[:, n.slot(3), t0:t1, :], ALU.add).then_inc(acc_begun[b], 1)

            MIX = 4

            def gated(n, t, e, into, start=False):
                g = gate[:, n.slot(2), t, e:e + 1]
                src = pe_out[:, (n.off * T + t) % 2, 0, e * C:(e + 1) * C]
                if start:
                    dve.tensor_scalar(into, src, g, None, ALU.mult).then_inc(mixing, 1)
                else:
                    dve.scalar_tensor_tensor(out=into, in0=src, scalar=g, in1=into, op0=ALU.mult, op1=ALU.add)\
                       .then_inc(mixing, 1)

            def mix(n, t, first, more):
                b = (n.off * T + t) % 2
                if first >= 1 or t >= 2:
                    hold(dve, joined, n.val(T, t - 1), ticks)
                dve.wait_ge(expert_done, n.val(T, t + 1))
                gated(n, t, 1, odd[:, b, :], start=True)
                route_between(n, t, 0, more)
                if t == 0:
                    hold(dve, acc_begun[1], n.val(1, 1), ticks)
                gated(n, t, 0, acc[:, n.slot(3), t, :])
                route_between(n, t, 1, more)
                if first >= 1 or t >= 1:
                    add_odd(n, t - 1)
                route_between(n, t, 2, more)
                hold(dve, mixing, n.val(T * MIX, MIX * t + 1), ticks)
                gated(n, t, 3, odd[:, b, :])
                route_between(n, t, 3, more)
                if first >= 1 or t >= 1:
                    add_others(n, t - 1)
                route_between(n, t, 4, more)
                hold(dve, mixing, n.val(T * MIX, MIX * t + 2), ticks)
                gated(n, t, 2, acc[:, n.slot(3), t, :])
                route_between(n, t, 5, more)

            def tile_of(n, t):
                m, u = (n, t) if t >= 0 else (n - 1, T - 1)
                return acc[:, m.slot(3), u, :], (n.off * T + t) % 2

            def add_odd(n, t):
                a, b = tile_of(n, t)
                hold(dve, mixing, n.val(T * MIX, MIX * (t + 1)), ticks)
                dve.tensor_tensor(a, a, odd[:, b, :], ALU.add).then_inc(joined, 1)

            def add_others(n, t):
                a, b = tile_of(n, t)
                hold(dve, joined, n.val(T, t + 1), ticks)
                dve.wait_ge(others_ready, n.val(T, t + 1))
                dve.tensor_tensor(a, a, others[:, b, :], ALU.add).then_inc(mixed, 1)

            def step(n, first, last):
                if first == 0:
                    for k in range(3):
                        if k >= 1:
                            negate(n + k - 1)
                        if k == 2:
                            hold(dve, normed, n.val(TP, TP), ticks)
                        layer_stats(n + k, 0, T)
                        layer_stats_end(n + k)
                    for k in range(ROUTE_OPS):
                        route(n, k)
                    begin(n, 0)
                more = last < -1
                for t in range(T):
                    mix(n, t, first, more)
                    if last < -2 and t == 2:
                        negate(n + 2)
                    if last < -3 and t == 5:
                        hold(dve, normed, n.val(TP, 2 * TP), ticks)
                        layer_stats(n + 3, 0, 4)
                    if last < -3 and t == 6:
                        layer_stats(n + 3, 4, T)
                if more:
                    begin(n + 1, first + 1)
                else:
                    add_odd(n, T - 1)
                    add_others(n, T - 1)
                if last < -3:
                    layer_stats_end(n + 3)

            run_steps(dve, N, U, step, 4)

        @block.tensor
        def _(pe):
            pe.wait_ge(const_in, CONSTS)

            def turn(n, first):
                hold(pe, normed_act, n.val(1, 1), ticks)
                pe.wait_ge(normed, n.val(TP, TP))
                for b, (t0, t1) in enumerate(HALVES):
                    if first >= 1:
                        pe.wait_ge(acc_begun[b], n.val())
                    for t in range(t0, t1):
                        ins = pe.transpose(px[:, b, (t - t0) * P:(t - t0 + 1) * P], xn[:, n.slot(2), t, :], idn[:])
                    ins.then_inc(turned[b], 1)

            def logits(n, first):
                pe.wait_ge(xT_out[1], n.val(1, 1))
                if first >= 1:
                    pe.wait_ge(routing, n.val(ROUTE_OPS))
                for t in range(T):
                    ins = pe.matmul(pr[:, t * E:(t + 1) * E], xnT[:, n.slot(2), t, :], wr[:], start=True, stop=True)
                ins.then_inc(logits_made, 1)

            def turn_gates(n):
                pe.wait_ge(routing, n.val(ROUTE_OPS, ROUTE_OPS))
                for b, (t0, t1) in enumerate(HALVES):
                    for t in range(t0, t1):
                        ins = pe.transpose(px[0:E, b, (t - t0) * P:(t - t0 + 1) * P], gate[:, n.slot(2), t, :], idn[:])
                    ins.then_inc(gates_turned[b], 1)

            def gated_bias(n):
                for b, (t0, t1) in enumerate(HALVES):
                    pe.wait_ge(gT_out[b], n.val(1, 1))
                    for t in range(t0, t1):
                        ins = pe.matmul(px[:, b, (t - t0) * C:(t - t0 + 1) * C], gateT[:, t, :], be[:],
                                        start=True, stop=True)
                    ins.then_inc(bias_made[b], 1)

            def experts(n, t, first):
                b = (n.off * T + t) % 2
                if first >= 1 or t >= 2:
                    hold(pe, mixing, n.val(T * 4, 4 * (t - 1)), ticks)
                    hold(pe, scaled_ready, n.val(T, t - 1), ticks)
                for half in range(2):
                    ins = pe.matmul(pe_out[:, b, half, :], xnT[:, n.slot(2), t, :],
                                    we[:, half * 4:half * 4 + 4, :].rearrange("d e c -> d (e c)"), start=True, stop=True)
                ins.then_inc(expert_done, 1)

            def step(n, first, last):
                if first == 0:
                    turn(n, 0)
                    logits(n, 0)
                    turn_gates(n)
                    gated_bias(n)
                for t in range(T):
                    experts(n, t, first)
                    if last < -1:
                        if t == 0:
                            turn(n + 1, 1)
                        if t == 1:
                            logits(n + 1, 1)
                        if t == 5:
                            turn_gates(n + 1)
                        if t == 6:
                            gated_bias(n + 1)

            run_steps(pe, N, U, step, 4)


ROW = 64
QUAD = 4
GROUPS = C // QUAD
ODD = IMG // 2 + 1
EVEN = IMG // 2
BLOCKS = (2, 3, 5)
FURTHEST = (64, 128, 256)
G_LEN = tuple(P - 1 + P * b for b in BLOCKS)
G_OFF = (0, G_LEN[0], G_LEN[0] + G_LEN[1])
G_ALL = sum(G_LEN)

ODD_ROWS = (((54, 1, 1), (0, 2, 27)), ((53, 0, 2), (1, 2, 26)))
EVEN_ROWS = (((53, 0, 2), (1, 2, 26)), ((54, 0, 1), (0, 1, 27)))
COLS = ((53, 0, 3), (0, 3, 53))
ROLLED = 8


def load_rolled(eng, dst, pitch, src, n, rows, sem):
    for half in range(2):
        for row, tile, tiles in rows[half]:
            for col, w0, ws in COLS:
                p0 = half * pitch + w0
                eng.dma_start(dst[p0:p0 + ws, tile:tile + tiles, :],
                              dram(src, n.val(PIX * C, (row * IMG + col) * C),
                                   [(C, ws), (2 * IMG * C, tiles), (1, C)])).then_inc(sem, 16)


def focal_input_stage(nc, B, x2, Wf, bf, edge_mask, ident, q, c0, gates):
    EPS = 1e-6
    OUT = 2 * C + 4
    CH = 4
    CHUNKS = [(t, min(CH, ODD - t)) for t in range(0, ODD, CH)]
    NCH = len(CHUNKS)
    assert CHUNKS[-1][1] == 1
    N = B * NCH
    U = 2 * NCH
    AHEAD = 4 + NCH
    S = Stage(nc, "foc")
    with S.ctx:
        idn = S.sb("idn", [P, P])
        wf = S.sb("wf", [C, OUT])
        bias = S.sb("bias", [P, OUT])
        edge = S.sb("edge", [P, 4])
        cbias = S.sb("cbias", [P, 4, C])
        halfneg = S.sb("halfneg", [P, CH])
        xin = S.sb("xin", [P, 2, ODD, C])
        stat = S.sb("stat", [P, CH, 6])
        mv = S.sb("mv", [P, 4, CH, 2])
        rstd = S.sb("rstd", [P, 4, CH])
        nmean = S.sb("nmean", [P, 4, CH])
        xn = S.sb("xn", [P, 2, 4, C])
        xnT = S.sb("xnT", [C, 2, 4 * P])
        qs = S.sb("qs", [P, 2, ODD, C])
        cs = S.sb("cs", [P, 2, GROUPS, ODD, QUAD])
        gs = S.sb("gs", [P, 2, 4, ODD])
        px = S.ps("px", [P, 2, BANK])
        py = S.ps("py", [P, 2, 2, BANK])

        ticks = S.sem("ticks")
        const_in = S.sem("const_in")
        zeroed = S.sem("zeroed")
        filled = S.sem("filled")
        cbias_built = S.sem("cbias_built")
        x_in = S.sems("x_in", 2)
        stats_part, stats, eps_added, rstd_done = (S.sem(f"{k}") for k in ("stats_part", "stats", "eps_added", "rstd_done"))
        nmean_done = S.sem("nmean_done")
        normed, turned, xT_out = S.sem("normed"), S.sem("turned"), S.sem("xT_out")
        made, ctx_read, gates_read, q_read = S.sem("made"), S.sem("ctx_read"), S.sem("gates_read"), S.sem("q_read")
        q_biased = S.sem("q_biased")
        q_out, c_out, g_out = S.sems("q_out", 2), S.sems("c_out", 2), S.sems("g_out", 2)
        block = S.block()

        def image(n):
            return Step(n.loop, 2, n.off // NCH), n.off % NCH

        def pairs(n):
            t0, tn = CHUNKS[n.off % NCH]
            if tn == 1:
                return [(0, t0, 1, 2, n.val(2, 2))]
            return [(y, t0 + 2 * y, 2, 1, n.val(2, y + 1)) for y in range(2)]

        @block.sync
        def _(sp):
            for dst, src in ((idn[:], ident), (wf[:], Wf), (bias[:], row_to_all(bf, OUT)), (edge[:], edge_mask)):
                sp.dma_start(dst, src).then_inc(const_in, 16)
            sp.wait_ge(zeroed, 2)

            def step(n, first, last):
                m, c = image(n)
                s = m.slot(2)
                if first == 0:
                    for k in range(2):
                        load_rolled(sp, xin[:, k, :, :], ROW, x2, m + k, ODD_ROWS, x_in[k])
                if c < NCH - 1:
                    return
                if last < -NCH - 1:
                    hold(sp, normed, n.val(1, 1), ticks)
                    load_rolled(sp, xin[:, s, :, :], ROW, x2, m + 2, ODD_ROWS, x_in[s])
                hold(sp, ctx_read, n.val(2, 2), ticks)
                sp.dma_start(dram(c0, m.val(ODD * QUAD), [(B * ODD * QUAD, P), (P * B * ODD * QUAD, GROUPS), (1, ODD * QUAD)]),
                             cs[:, s, :, :, :].rearrange("p g j c -> p g (j c)")).then_inc(c_out[s], 16)
                hold(sp, gates_read, n.val(2, 2), ticks)
                for half, j0 in ((0, 0), (1, 1)):
                    sp.dma_start(dram(gates, m.val(EVEN, half * ROW * 4 * B * EVEN), [(4 * B * EVEN, ROW), (B * EVEN, 4), (1, EVEN)]),
                                 gs[(1 - half) * ROW:(2 - half) * ROW, s, :, j0:j0 + EVEN]).then_inc(g_out[s], 16)
                hold(sp, q_biased, n.val(1, 1), ticks)
                for half, j0 in ((0, 1), (1, 0)):
                    row = 2 * j0 - 1 + half
                    sp.dma_start(dram(q, m.val(PIX * C, row * IMG * C), [(C, IMG), (2 * IMG * C, EVEN), (1, C)]),
                                 qs[half * ROW:half * ROW + IMG, s, j0:j0 + EVEN, :]).then_inc(q_out[s], 16)

            run_steps(sp, N, U, step, 2 * NCH)
            for s in range(2):
                images = (B + 1 - s) // 2
                sp.wait_ge(c_out[s], 16 * images)
                sp.wait_ge(g_out[s], 32 * images)
                sp.wait_ge(q_out[s], 32 * images)

        @block.gpsimd
        def _(pool):
            for s in range(2):
                pool.memset(xin[:, s, :, :], 0.0).then_inc(zeroed, 1)
            pool.memset(halfneg[:], -0.5).then_inc(filled, 1)
            pool.wait_ge(filled, 1)
            pool.wait_ge(const_in, 64)

            def scale(n, first):
                a, tn = n.slot(4), CHUNKS[n.off % NCH][1]
                if first >= 4:
                    hold(pool, normed, n.val(1, -3), ticks)
                hold(pool, stats, n.val(1, 1), ticks)
                pool.tensor_scalar(rstd[:, a, 0:tn], mv[:, a, 0:tn, 1], EPS, None, ALU.add).then_inc(eps_added, 1)
                pool.wait_ge(eps_added, n.val(1, 1))
                pool.tensor_tensor(rstd[:, a, 0:tn], rstd[:, a, 0:tn], halfneg[:, 0:tn], ALU.pow).then_inc(rstd_done, 1)

            def add_bias(n):
                m, c = image(n)
                t0, tn = CHUNKS[c]
                hold(pool, q_read, n.val(2, 2), ticks)
                x = qs[:, m.slot(2), t0:t0 + tn, :]
                pool.tensor_tensor(x, x, bias[:, 0:C].unsqueeze(1).to_broadcast([P, tn, C]), ALU.add).then_inc(q_biased, 1)

            def step(n, first, last):
                if first == 0:
                    for k in range(4):
                        scale(n + k, k)
                if last < -4:
                    scale(n + 4, first + 4)
                add_bias(n)

            run_steps(pool, N, U, step, AHEAD)

        @block.scalar
        def _(act):
            act.wait_ge(const_in, 64)

            def normalise(n, first):
                m, c = image(n)
                t0, tn = CHUNKS[c]
                act.wait_ge(nmean_done, n.val(1, 1))
                if first >= 2:
                    act.sem_inc(ticks, 1)
                    act.wait_ge(turned, n.val(1, -1))
                for t in range(tn):
                    ins = act.activation(xn[:, n.slot(2), t, :], xin[:, m.slot(2), t0 + t, :], ACT.Identity,
                                         bias=nmean[:, n.slot(4), t:t + 1], scale=rstd[:, n.slot(4), t:t + 1])
                ins.then_inc(normed, 1)

            def turned_out(n, first):
                tn = CHUNKS[n.off % NCH][1]
                act.wait_ge(turned, n.val(1, 1))
                if first >= 2:
                    act.sem_inc(ticks, 1)
                    act.wait_ge(made, n.val(2, -2))
                act.activation(xnT[:, n.slot(2), 0:tn * P], px[:, n.slot(2), 0:tn * P], ACT.Copy).then_inc(xT_out, 1)

            def step(n, first, last):
                if first == 0:
                    normalise(n, 0)
                    normalise(n + 1, 1)
                    turned_out(n, 0)
                if last < -2:
                    normalise(n + 2, first + 2)
                if last < -1:
                    turned_out(n + 1, first + 1)
                m, c = image(n)
                if c == 0 and first >= 2 * NCH:
                    act.wait_ge(q_out[m.slot(2)], m.turn(2, 32))
                    act.sem_inc(ticks, 1)
                for y, t, tn, up, value in pairs(n):
                    act.wait_ge(gates_read, value)
                    act.activation(qs[:, m.slot(2), t:t + tn, :], py[:, y, 0:tn, 0:C], ACT.Copy).then_inc(q_read, up)

            run_steps(act, N, U, step, AHEAD)

        @block.vector
        def _(dve):
            dve.wait_ge(const_in, 64)
            for k in range(4):
                dve.tensor_scalar(cbias[:, k, :], bias[:, C:2 * C], edge[:, k:k + 1], None, ALU.mult).then_inc(cbias_built, 1)
            dve.wait_ge(cbias_built, 4)

            def layer_stats(n):
                m, c = image(n)
                t0, tn = CHUNKS[c]
                if c == 0:
                    hold(dve, x_in[m.slot(2)], m.turn(2, 16 * ROLLED, 16 * ROLLED), ticks)
                for t in range(tn):
                    ins = dve.bn_stats(stat[:, t, :], xin[:, m.slot(2), t0 + t, :])
                ins.then_inc(stats_part, 1)
                hold(dve, stats_part, n.val(1, 1), ticks)
                for t in range(tn):
                    ins = dve.bn_aggr(mv[:, n.slot(4), t, :], stat[:, t, :])
                ins.then_inc(stats, 1)

            def negate(n):
                a, tn = n.slot(4), CHUNKS[n.off % NCH][1]
                hold(dve, rstd_done, n.val(1, 1), ticks)
                dve.scalar_tensor_tensor(out=nmean[:, a, 0:tn], in0=mv[:, a, 0:tn, 0], scalar=-1.0, in1=rstd[:, a, 0:tn],
                                         op0=ALU.mult, op1=ALU.mult).then_inc(nmean_done, 1)

            def step(n, first, last):
                if first == 0:
                    for k in range(4):
                        if k >= 1:
                            negate(n + k - 1)
                        layer_stats(n + k)
                if last < -3:
                    negate(n + 3)
                if last < -4:
                    layer_stats(n + 4)
                m, c = image(n)
                s = m.slot(2)
                if c == 0 and first >= 2 * NCH:
                    hold(dve, c_out[s], m.turn(2, 16), ticks)
                    hold(dve, g_out[s], m.turn(2, 32), ticks)
                for y, t, tn, up, value in pairs(n):
                    dve.wait_ge(made, value)
                    version = 0 if t == 0 else (3 if tn == 1 else 1)
                    dve.tensor_tensor(cs[:, s, :, t:t + tn, :].rearrange("p g j c -> p j g c"),
                                      py[:, y, 0:tn, C:2 * C].rearrange("p j (g c) -> p j g c", c=QUAD),
                                      cbias[:, version:version + tn, :].rearrange("p j (g c) -> p j g c", c=QUAD),
                                      ALU.add).then_inc(ctx_read, up)
                    dve.tensor_tensor(gs[:, s, :, t:t + tn].rearrange("p l j -> p j l"), py[:, y, 0:tn, 2 * C:OUT],
                                      bias[:, 2 * C:OUT].unsqueeze(1).to_broadcast([P, tn, 4]), ALU.add)\
                       .then_inc(gates_read, up)

            run_steps(dve, N, U, step, AHEAD)

        @block.tensor
        def _(pe):
            pe.wait_ge(const_in, 64)

            def turn(n, first):
                tn = CHUNKS[n.off % NCH][1]
                hold(pe, normed, n.val(1, 1), ticks)
                if first >= 2:
                    hold(pe, xT_out, n.val(1, -1), ticks)
                for t in range(tn):
                    ins = pe.transpose(px[:, n.slot(2), t * P:(t + 1) * P], xn[:, n.slot(2), t, :], idn[:])
                ins.then_inc(turned, 1)

            def step(n, first, last):
                if first == 0:
                    turn(n, 0)
                if last < -1:
                    turn(n + 1, first + 1)
                pe.wait_ge(xT_out, n.val(1, 1))
                t0, _ = CHUNKS[n.off % NCH]
                for y, t, tn, up, value in pairs(n):
                    if first >= 1:
                        hold(pe, gates_read, n.val(2, y - 1), ticks)
                        hold(pe, q_read, n.val(2, y - 1), ticks)
                    for j in range(tn):
                        at = (t + j - t0) * P
                        ins = pe.matmul(py[:, y, j, 0:OUT], xnT[:, n.slot(2), at:at + P], wf[:], start=True, stop=True)
                    ins.then_inc(made, up)

            run_steps(pe, N, U, step, AHEAD)


def convolution_stage(nc, B, c0, gates, kernels, gap_mask, ctx_all):
    N = C
    HALF = B // 2
    U = 8
    PER = QUAD
    AHEAD = 4
    T_ALL = P * sum(BLOCKS)
    T_OFF = (0, P * BLOCKS[0], P * (BLOCKS[0] + BLOCKS[1]))
    S = Stage(nc, "conv")
    with S.ctx:
        gvec = S.sb("gvec", [C, G_ALL])
        ones = S.sb("ones", [P, P])
        gap = S.sb("gap", [P, 1])
        gate = S.sb("gate", [P, 4, B, EVEN])
        toep = S.sb("toep", [P, 2, PER, T_ALL])
        cin = S.sb("cin", [P, 2, B, ODD, PER])
        c1 = S.sb("c1", [P, 4, B, EVEN + 2])
        c2 = S.sb("c2", [P, 2, B, EVEN + 4])
        c3 = S.sb("c3", [P, 2, B, EVEN])
        g1 = S.sb("g1", [P, B, EVEN])
        g2 = S.sb("g2", [P, B, EVEN])
        g3 = S.sb("g3", [P, B, EVEN])
        pooled = S.sb("pooled", [P, B])
        glob = S.sb("glob", [P, B])
        out = S.sb("out", [P, 2, B, PER, EVEN])
        gvec_dram = nc.dram_tensor("gvec_dram", (C, G_ALL), F32).ap()
        group_dram = nc.dram_tensor("group_dram", (2, PER, G_ALL), F32).ap()
        rows_dram = nc.dram_tensor("rows_dram", (2, PER, P, T_ALL), F32).ap()
        pc = [S.ps(f"pc{k}", [P, 2, BANK]) for k in range(3)]
        pm = S.ps("pm", [P, BANK])

        ticks = S.sem("ticks")
        zeroed = S.sem("zeroed")
        taps_in, gvec_out = S.sem("taps_in"), S.sem("gvec_out")
        const_in = S.sem("const_in")
        rows_made = S.sems("rows_made", 2)
        group_in, toep_in, c0_in = S.sems("group_in", 2), S.sems("toep_in", 2), S.sems("c0_in", 2)
        convolved = S.sems("convolved", 3)
        activated = S.sems("activated", 3)
        gated1, gated2, gated3 = S.sem("gated1"), S.sem("gated2"), S.sem("gated3")
        pooled_part, averaged, glob_ready = S.sem("pooled_part"), S.sem("averaged"), S.sem("glob_ready")
        summed, gglob, summed_glob = S.sem("summed"), S.sem("gglob"), S.sem("summed_glob")
        combined = S.sem("combined")
        stored = S.sems("stored", 2)
        block = S.block()
        NG = N // PER

        @block.sync
        def _(sp):
            sp.wait_ge(zeroed, 1)
            for k, size in enumerate(TAPS):
                r = size // 2
                at = G_OFF[k] + P - 1 + FURTHEST[k] - r * ROW - r
                for row in range(size):
                    sp.dma_start(gvec[:, at + row * ROW:at + row * ROW + size],
                                 dram(kernels[k], row * size, [(size * size, C), (1, size)])).then_inc(taps_in, 16)
            sp.dma_start(gate[:], gates).then_inc(const_in, 16)
            sp.dma_start(gap[:], gap_mask).then_inc(const_in, 16)
            sp.wait_ge(taps_in, 16 * sum(TAPS))
            sp.dma_start(gvec_dram, gvec[:]).then_inc(gvec_out, 16)
            sp.wait_ge(gvec_out, 16)

            def load(g, n, extra):
                s = g.slot(2)
                sp.dma_start(cin[:, s, :, :, :].rearrange("p b j c -> p (b j c)"),
                             dram(c0, g.val(P * B * ODD * PER), [(B * ODD * PER, P), (1, B * ODD * PER)]))\
                  .then_inc(c0_in[s], 16)
                sp.dma_start(dram(group_dram, s * PER * G_ALL, [(G_ALL, PER), (1, G_ALL)]),
                             dram(gvec_dram, g.val(PER * G_ALL), [(G_ALL, PER), (1, G_ALL)])).then_inc(group_in[s], 16)
                hold(sp, group_in[s], g.turn(2, 16, 16), ticks)
                for k, blocks in enumerate(BLOCKS):
                    sp.dma_start(dram(rows_dram, s * PER * P * T_ALL + T_OFF[k], [(P * T_ALL, PER), (T_ALL, P), (1, P * blocks)]),
                                 dram(group_dram, s * PER * G_ALL + G_OFF[k] + P - 1,
                                      [(G_ALL, PER), (-1, P), (1, P * blocks)])).then_inc(rows_made[s], 16)
                hold(sp, rows_made[s], g.turn(2, 48, 48), ticks)
                sp.dma_start(toep[:, s, :, :], dram(rows_dram, s * PER * P * T_ALL, [(T_ALL, P), (P * T_ALL, PER), (1, T_ALL)]))\
                  .then_inc(toep_in[s], 16)

            def step(n, first, last):
                if n.off % PER != PER - 1:
                    return
                g = Step(n.loop, U // PER, n.off // PER)
                if first < PER:
                    load(g, n, 0)
                    load(g + 1, n, 1)
                if last + 1 < -2 * PER + 1:
                    hold(sp, convolved[2], n.val(1, 1), ticks)
                    load(g + 2, n, 2)
                hold(sp, combined, n.val(1, 1), ticks)
                sp.dma_start(dram(ctx_all, g.val(P * B * EVEN * PER), [(B * EVEN * PER, P), (1, B * EVEN * PER)]),
                             out[:, g.slot(2), :, :, :].rearrange("p b c i -> p (b c i)")).then_inc(stored[g.slot(2)], 16)

            run_steps(sp, N, U, step, AHEAD + PER)
            for s in range(2):
                sp.wait_ge(stored[s], 16 * (NG // 2))

        @block.gpsimd
        def _(pool):
            pool.memset(gvec[:], 0.0).then_inc(zeroed, 1)
            pool.memset(c1[:], 0.0).then_inc(zeroed, 1)
            pool.memset(c2[:], 0.0).then_inc(zeroed, 1)
            pool.memset(ones[:], 1.0).then_inc(zeroed, 1)
            pool.wait_ge(const_in, 32)

            def step(n, first, last):
                pool.wait_ge(activated[1], n.val(1, 1))
                if first >= 1:
                    pool.sem_inc(ticks, 1)
                    pool.wait_ge(combined, n.val())
                pool.tensor_tensor(g2[:], c2[:, n.slot(2), :, 2:2 + EVEN], gate[:, 1, :, :], ALU.mult).then_inc(gated2, 1)

            run_steps(pool, N, U, step, AHEAD)

        @block.scalar
        def _(act):
            act.wait_ge(zeroed, 4)
            act.wait_ge(const_in, 32)

            def gelu(k, n, first):
                dst, slots = (c1, c2, c3)[k], (4, 2, 2)[k]
                edge = (1, 2, 0)[k]
                act.wait_ge(convolved[k], n.val(1, 1))
                if first >= slots:
                    act.sem_inc(ticks, 1)
                    act.wait_ge((gated1, gated2, gated3)[k], n.val(1, 1 - slots))
                    if k < 2:
                        act.sem_inc(ticks, 1)
                        act.wait_ge(convolved[k + 1], n.val(1, 1 - slots))
                    else:
                        act.sem_inc(ticks, 1)
                        act.wait_ge(pooled_part, n.val(1, -1))
                for half in range(2):
                    ins = act.activation(dst[:, n.slot(slots), half * HALF:(half + 1) * HALF, edge:edge + EVEN],
                                         pc[k][:, half, 0:HALF * EVEN].rearrange("p (b i) -> p b i", i=EVEN),
                                         ACT.Gelu, scale=gap[:])
                ins.then_inc(activated[k], 1)

            def average(n, first):
                act.wait_ge(averaged, n.val(1, 1))
                if first >= 1:
                    act.sem_inc(ticks, 1)
                    act.wait_ge(gglob, n.val())
                act.activation(glob[:], pm[:, 0:B], ACT.Gelu, scale=1.0 / PIX).then_inc(glob_ready, 1)

            def step(n, first, last):
                if first == 0:
                    gelu(0, n, 0)
                    gelu(0, n + 1, 1)
                    gelu(1, n, 0)
                if last < -3:
                    gelu(0, n + 2, first + 2)
                if first >= 1:
                    average(n - 1, first - 1)
                if last < -2:
                    gelu(1, n + 1, first + 1)
                if last < -1:
                    gelu(2, n, first)

            run_steps(act, N + 1, U, step, AHEAD)

        @block.vector
        def _(dve):
            dve.wait_ge(const_in, 32)

            def products(n, first):
                s = n.slot(2)
                dve.wait_ge(activated[2], n.val(1, 1))
                dve.tensor_reduce(pooled[:], c3[:, s, :, :], AX.X, ALU.add).then_inc(pooled_part, 1)
                if first >= 1:
                    dve.wait_ge(combined, n.val())
                dve.tensor_tensor(g3[:], c3[:, s, :, :], gate[:, 2, :, :], ALU.mult).then_inc(gated3, 1)
                dve.wait_ge(gated3, n.val(1, 1))
                dve.sem_inc(ticks, 1)
                dve.wait_ge(gated1, n.val(1, 1))
                dve.tensor_tensor(g3[:], g3[:], g1[:], ALU.add).then_inc(summed, 1)

            def first_gate(n, first):
                dve.wait_ge(activated[0], n.val(1, 1))
                if first >= 1:
                    dve.sem_inc(ticks, 1)
                    dve.wait_ge(summed_glob, n.val())
                dve.tensor_tensor(g1[:], c1[:, n.slot(4), :, 1:1 + EVEN], gate[:, 0, :, :], ALU.mult).then_inc(gated1, 1)

            def combine(n, first):
                g = Step(n.loop, U // PER, n.off // PER)
                s = g.slot(2)
                dve.wait_ge(glob_ready, n.val(1, 1))
                dve.sem_inc(ticks, 1)
                dve.wait_ge(summed, n.val(1, 1))
                dve.tensor_tensor(g1[:], gate[:, 3, :, :], glob[:].unsqueeze(2).to_broadcast([P, B, EVEN]),
                                  ALU.mult).then_inc(gglob, 1)
                dve.wait_ge(gglob, n.val(1, 1))
                dve.tensor_tensor(g3[:], g3[:], g1[:], ALU.add).then_inc(summed_glob, 1)
                dve.wait_ge(summed_glob, n.val(1, 1))
                if first >= 2 * PER and n.off % PER == 0:
                    dve.sem_inc(ticks, 1)
                    dve.wait_ge(stored[s], g.turn(2, 16))
                dve.sem_inc(ticks, 1)
                dve.wait_ge(gated2, n.val(1, 1))
                dve.tensor_tensor(out[:, s, :, n.off % PER, :], g3[:], g2[:], ALU.add).then_inc(combined, 1)

            def step(n, first, last):
                if first >= 1:
                    combine(n - 1, first - 1)
                if last < -1:
                    first_gate(n, first)
                    products(n, first)

            run_steps(dve, N + 1, U, step, AHEAD)

        @block.tensor
        def _(pe):
            pe.wait_ge(zeroed, 4)

            def convolve(k, n, first, group_first):
                g = Step(n.loop, U // PER, n.off // PER)
                ch, s = n.off % PER, g.slot(2)
                if k == 0 and ch == 0:
                    hold(pe, c0_in[s], g.turn(2, 16, 16), ticks)
                    hold(pe, toep_in[s], g.turn(2, 16, 16), ticks)
                if k > 0:
                    hold(pe, activated[k - 1], n.val(1, 1), ticks)
                if first >= 1:
                    pe.wait_ge(activated[k], n.val())
                blocks = BLOCKS[k]
                order = [blocks // 2] + [i for i in range(blocks) if i != blocks // 2]
                for blk in order:
                    w = toep[:, s, ch, T_OFF[k] + blk * P:T_OFF[k] + (blk + 1) * P]
                    below = blocks - 1 - blk
                    away = below - blocks // 2 if k else 0
                    i0, i1 = max(0, -away), EVEN - max(0, away)
                    for half in range(2):
                        b = slice(half * HALF, (half + 1) * HALF)
                        if k == 0:
                            src = cin[:, s, b, below:below + EVEN, ch]
                        else:
                            src = (c1, c2)[k - 1][:, n.slot((4, 2)[k - 1]), b, below + i0:below + i1]
                        ins = pe.matmul(pc[k][:, half, 0:HALF * EVEN].rearrange("p (b i) -> p b i", i=EVEN)[:, :, i0:i1],
                                        w, src, start=(blk == order[0]), stop=(blk == order[-1]), skip_group_check=True)
                ins.then_inc(convolved[k], 1)

            def average(n, first):
                if first >= 1:
                    pe.wait_ge(glob_ready, n.val())
                    pe.sem_inc(ticks, 1)
                pe.wait_ge(pooled_part, n.val(1, 1))
                pe.matmul(pm[:, 0:B], ones[:], pooled[:], start=True, stop=True).then_inc(averaged, 1)

            def step(n, first, last):
                if first == 0:
                    convolve(0, n, 0, 0)
                    convolve(0, n + 1, 1, 0)
                    convolve(1, n, 0, 0)
                if last < -3:
                    convolve(0, n + 2, first + 2, 0)
                if first >= 1:
                    average(n - 1, first - 1)
                if last < -2:
                    convolve(1, n + 1, first + 1, 0)
                if last < -1:
                    convolve(2, n, first, 0)

            run_steps(pe, N + 1, U, step, AHEAD)


def focal_output_stage(nc, B, ctx_all, q, x2, Wh, bh, gamma, beta, Wp, bp, ident, x3, gram):
    TOK = 2 * IMG
    CH = 4
    NCH = EVEN // CH
    EPS, EPS_T = 1e-3, 1e-5
    N = B * NCH
    U = 2 * NCH
    AHEAD = 3 + NCH
    S = Stage(nc, "mod")
    with S.ctx:
        idn = S.sb("idn", [P, P])
        wh = S.sb("wh", [C, C])
        wp = S.sb("wp", [C, C])
        wpg = S.sb("wpg", [C, C])
        bhr = S.sb("bhr", [P, C])
        bpr = S.sb("bpr", [P, C])
        gcol = S.sb("gcol", [C, 1])
        bcol = S.sb("bcol", [C, 1])
        bmat = S.sb("bmat", [C, P])
        brow = S.sb("brow", [P, C])
        halfneg = S.sb("halfneg", [P, CH])
        cin = S.sb("cin", [TOK, 2, C, EVEN])
        qin = S.sb("qin", [TOK, 2, EVEN, C])
        xin = S.sb("xin", [TOK, 2, EVEN, C])
        cT = S.sb("cT", [C, 2, CH * TOK])
        y = S.sb("y", [TOK, 2, CH, C])
        yn = S.sb("yn", [TOK, 2, CH, C])
        yT = S.sb("yT", [C, 2, CH * TOK])
        z = S.sb("z", [TOK, 2, CH, C + 1])
        stat = S.sb("stat", [TOK, 2, CH, 6])
        mv = S.sb("mv", [TOK, 2, 2, CH, 2])
        rstd = S.sb("rstd", [TOK, 2, 2, CH])
        nmean = S.sb("nmean", [TOK, 2, 2, CH])
        gout = S.sb("gout", [C, C + 1])

        pt = S.ps("pt", [P, BANK])
        pm = S.ps("pm", [P, 2, BANK])
        pu = S.ps("pu", [P, BANK])
        pz = S.ps("pz", [P, 2, BANK])
        pg = S.ps("pg", [P, BANK])

        ticks = S.sem("ticks")
        const_in, filled = S.sem("const_in"), S.sem("filled")
        scaled, beta_wide, bias_made, bias_built = (S.sem(k) for k in ("scaled", "beta_wide", "bias_made", "bias_built"))
        c_in, q_in, x_in = S.sems("c_in", 2), S.sems("q_in", 2), S.sems("x_in", 2)
        x_biased = S.sem("x_biased")
        turned, cT_out, modulated = S.sem("turned"), S.sem("cT_out"), S.sem("modulated")
        biased, gated = S.sem("biased"), S.sem("gated")
        parts, stats = S.sems("parts", 2), S.sems("stats", 2)
        eps_added, rstd_done, nmean_done = S.sems("eps_added", 2), S.sems("rstd_done", 2), S.sems("nmean_done", 2)
        y_normed, y_turned, yT_out, projected = (S.sem(k) for k in ("y_normed", "y_turned", "yT_out", "projected"))
        x3_made, z_normed, gram_added = S.sem("x3_made"), S.sem("z_normed"), S.sem("gram_added")
        x3_out, gram_copied, gram_out = S.sems("x3_out", 2), S.sem("gram_copied"), S.sem("gram_out")
        block = S.block()
        CONSTS = 16 * 7

        def image(n):
            return Step(n.loop, 2, n.off // NCH), n.off % NCH

        @block.sync
        def _(sp):
            for dst, src in ((idn[:], ident), (wh[:], Wh), (wp[:], Wp), (bhr[:], row_to_all(bh, C)),
                             (bpr[:], row_to_all(bp, C)), (gcol[:], dram(gamma, 0, [(1, C), (1, 1)])),
                             (bcol[:], dram(beta, 0, [(1, C), (1, 1)]))):
                sp.dma_start(dst, src).then_inc(const_in, 16)

            def load_cq(m):
                s = m.slot(2)
                for half in range(2):
                    p0 = half * IMG
                    sp.dma_start(cin[p0:p0 + IMG, s, :, :].rearrange("p (g c) i -> p g (c i)", c=QUAD),
                                 dram(ctx_all, m.val(EVEN * QUAD, half * ROW * B * EVEN * QUAD),
                                      [(B * EVEN * QUAD, IMG), (P * B * EVEN * QUAD, GROUPS), (1, EVEN * QUAD)]))\
                      .then_inc(c_in[s], 16)
                sp.dma_start(qin[:, s, :, :], dram(q, m.val(PIX * C), [(C, TOK), (TOK * C, EVEN), (1, C)])).then_inc(q_in[s], 16)

            def load_x(m):
                load_rolled(sp, xin[:, m.slot(2), :, :], IMG, x2, m, EVEN_ROWS, x_in[m.slot(2)])

            def step(n, first, last):
                m, c = image(n)
                if first == 0:
                    for k in range(2):
                        load_cq(m + k)
                        load_x(m + k)
                if c == NCH - 1:
                    if last < -NCH - 1:
                        hold(sp, turned, n.val(1, 1), ticks)
                        hold(sp, gated, n.val(1, 1), ticks)
                        load_cq(m + 2)
                    hold(sp, x3_made, n.val(1, 1), ticks)
                    sp.dma_start(dram(x3, m.val(PIX * C), [(C, TOK), (TOK * C, EVEN), (1, C)]),
                                 xin[:, m.slot(2), :, :]).then_inc(x3_out[m.slot(2)], 16)
                    if last < -NCH - 1:
                        hold(sp, x3_out[m.slot(2)], m.turn(2, 16, 16), ticks)
                        hold(sp, z_normed, n.val(1, 1), ticks)
                        load_x(m + 2)

            run_steps(sp, N, U, step, 2 * NCH)
            for s in range(2):
                sp.wait_ge(x3_out[s], 16 * ((B + 1 - s) // 2))
            sp.wait_ge(gram_copied, 1)
            sp.dma_start(gram, gout[:]).then_inc(gram_out, 16)
            sp.wait_ge(gram_out, 16)

        @block.gpsimd
        def _(pool):
            pool.memset(halfneg[:], -0.5).then_inc(filled, 1)
            pool.memset(z[:], 1.0).then_inc(filled, 1)
            pool.memset(bmat[:], 1.0).then_inc(filled, 1)
            pool.wait_ge(filled, 3)
            pool.wait_ge(bias_built, 1)

            def rsqrt(n, which, eps, first):
                if which == 1 and first >= 2:
                    hold(pool, z_normed, n.val(1, -1), ticks)
                hold(pool, stats[which], n.val(1, 1), ticks)
                r = rstd[:, which, n.slot(2), :]
                pool.tensor_scalar(r, mv[:, which, n.slot(2), :, 1], eps, None, ALU.add).then_inc(eps_added[which], 1)
                pool.wait_ge(eps_added[which], n.val(1, 1))
                pool.tensor_tensor(r, r, halfneg[0:TOK, :], ALU.pow).then_inc(rstd_done[which], 1)

            def add_bias(n):
                m, c = image(n)
                if c == 0:
                    pool.wait_ge(x_in[m.slot(2)], m.turn(2, 16 * ROLLED, 16 * ROLLED))
                x = xin[:, m.slot(2), CH * c:CH * c + CH, :]
                pool.tensor_tensor(x, x, brow[0:TOK, :].unsqueeze(1).to_broadcast([TOK, CH, C]), ALU.add)\
                    .then_inc(x_biased, 1)

            def step(n, first, last):
                if first == 0:
                    for k in range(3):
                        rsqrt(n + k, 0, EPS, k)
                    add_bias(n)
                    rsqrt(n, 1, EPS_T, 0)
                    add_bias(n + 1)
                if last < -3:
                    rsqrt(n + 3, 0, EPS, first + 3)
                if last < -1:
                    rsqrt(n + 1, 1, EPS_T, first + 1)
                if last < -2:
                    add_bias(n + 2)

            run_steps(pool, N, U, step, AHEAD)

        @block.scalar
        def _(act):
            act.wait_ge(const_in, CONSTS)
            act.wait_ge(filled, 3)

            def context_out(n):
                act.wait_ge(turned, n.val(1, 1))
                act.activation(cT[:, n.slot(2), :], pt[:, 0:CH * TOK], ACT.Copy).then_inc(cT_out, 1)

            def y_out(n):
                act.wait_ge(y_turned, n.val(1, 1))
                act.activation(yT[:, n.slot(2), :], pu[:, 0:CH * TOK], ACT.Copy).then_inc(yT_out, 1)

            def norm_y(n, first):
                act.wait_ge(nmean_done[0], n.val(1, 1))
                if first >= 2:
                    act.sem_inc(ticks, 1)
                    act.wait_ge(y_turned, n.val(1, -1))
                b = n.slot(2)
                for t in range(CH):
                    ins = act.activation(yn[:, b, t, :], y[:, b, t, :], ACT.Identity,
                                         bias=nmean[:, 0, b, t:t + 1], scale=rstd[:, 0, b, t:t + 1])
                ins.then_inc(y_normed, 1)

            def norm_z(n, first):
                m, c = image(n)
                act.wait_ge(nmean_done[1], n.val(1, 1))
                if first >= 2:
                    act.sem_inc(ticks, 1)
                    act.wait_ge(gram_added, n.val(1, -1))
                b = n.slot(2)
                for t in range(CH):
                    ins = act.activation(z[:, b, t, 0:C], xin[:, m.slot(2), CH * c + t, :], ACT.Identity,
                                         bias=nmean[:, 1, b, t:t + 1], scale=rstd[:, 1, b, t:t + 1])
                ins.then_inc(z_normed, 1)

            def step(n, first, last):
                if first == 0:
                    for k in range(3):
                        context_out(n + k)
                        if k < 2:
                            norm_y(n + k, k)
                    y_out(n)
                if last < -3:
                    context_out(n + 3)
                if last < -1:
                    y_out(n + 1)
                if first >= 1:
                    norm_z(n - 1, first - 1)
                if last < -2:
                    norm_y(n + 2, first + 2)
                if last == -1:
                    norm_z(n, first)

            run_steps(act, N, U, step, AHEAD)
            act.wait_ge(gram_added, N)
            act.activation(gout[:], pg[:, 0:C + 1], ACT.Copy).then_inc(gram_copied, 1)

        @block.vector
        def _(dve):
            dve.wait_ge(const_in, CONSTS)
            dve.wait_ge(filled, 3)
            dve.tensor_scalar(bmat[:], bmat[:], bcol[:], None, ALU.mult).then_inc(beta_wide, 1)
            dve.tensor_scalar(wpg[:], wp[:], gcol[:], None, ALU.mult).then_inc(scaled, 1)
            dve.wait_ge(bias_made, 1)
            dve.tensor_tensor(brow[:], pm[:, 0, 0:C], bpr[:], ALU.add).then_inc(bias_built, 1)

            def statistics(n, which, src):
                for t in range(CH):
                    ins = dve.bn_stats(stat[:, which, t, :], src[:, t, :])
                ins.then_inc(parts[which], 1)

            def statistics_end(n, which):
                hold(dve, parts[which], n.val(1, 1), ticks)
                for t in range(CH):
                    ins = dve.bn_aggr(mv[:, which, n.slot(2), t, :], stat[:, which, t, :])
                ins.then_inc(stats[which], 1)

            def negate(n, which):
                b = n.slot(2)
                hold(dve, rstd_done[which], n.val(1, 1), ticks)
                dve.scalar_tensor_tensor(out=nmean[:, which, b, :], in0=mv[:, which, b, :, 0], scalar=-1.0,
                                         in1=rstd[:, which, b, :], op0=ALU.mult, op1=ALU.mult)\
                   .then_inc(nmean_done[which], 1)

            def add_bh(n, first):
                b = n.slot(2)
                if first >= 2:
                    hold(dve, y_normed, n.val(1, -1), ticks)
                dve.wait_ge(modulated, n.val(1, 1))
                dve.tensor_tensor(y[:, b, :, :], pm[0:TOK, b, :].rearrange("p (t c) -> p t c", c=C),
                                  bhr[0:TOK, :].unsqueeze(1).to_broadcast([TOK, CH, C]), ALU.add).then_inc(biased, 1)

            def multiply_q(n):
                m, c = image(n)
                b = n.slot(2)
                if c == 0:
                    hold(dve, q_in[m.slot(2)], m.turn(2, 16, 16), ticks)
                dve.wait_ge(biased, n.val(1, 1))
                dve.tensor_tensor(y[:, b, :, :], y[:, b, :, :], qin[:, m.slot(2), CH * c:CH * c + CH, :], ALU.mult)\
                   .then_inc(gated, 1)

            def y_statistics(n):
                dve.wait_ge(gated, n.val(1, 1))
                statistics(n, 0, y[:, n.slot(2), :, :])

            def x_chunk(n):
                m, c = image(n)
                return xin[:, m.slot(2), CH * c:CH * c + CH, :]

            def residual(n):
                hold(dve, x_biased, n.val(1, 1), ticks)
                dve.wait_ge(projected, n.val(1, 1))
                x = x_chunk(n)
                dve.tensor_tensor(x, pz[0:TOK, n.slot(2), :].rearrange("p (t c) -> p t c", c=C), x, ALU.add)\
                   .then_inc(x3_made, 1)

            def x_statistics(n):
                dve.wait_ge(x3_made, n.val(1, 1))
                statistics(n, 1, x_chunk(n))

            def step(n, first, last):
                if first == 0:
                    for k in range(3):
                        if k:
                            negate(n + k - 1, 0)
                        add_bh(n + k, k)
                        multiply_q(n + k)
                        y_statistics(n + k)
                        statistics_end(n + k, 0)
                    residual(n)
                    x_statistics(n)
                    statistics_end(n, 1)
                new, old = last < -3, last < -1
                if new:
                    add_bh(n + 3, first + 3)
                    multiply_q(n + 3)
                if last < -2:
                    negate(n + 2, 0)
                negate(n, 1)
                if new:
                    y_statistics(n + 3)
                if old:
                    residual(n + 1)
                if new:
                    statistics_end(n + 3, 0)
                if old:
                    x_statistics(n + 1)
                    statistics_end(n + 1, 1)

            run_steps(dve, N, U, step, AHEAD)

        @block.tensor
        def _(pe):
            pe.wait_ge(const_in, CONSTS)
            pe.wait_ge(beta_wide, 1)
            pe.matmul(pm[:, 0, 0:C], bmat[:], wp[:], start=True, stop=True).then_inc(bias_made, 1)
            pe.wait_ge(scaled, 1)
            pe.wait_ge(bias_built, 1)

            def turn_context(n, first):
                m, c = image(n)
                if c == 0:
                    hold(pe, c_in[m.slot(2)], m.turn(2, 32, 32), ticks)
                if first >= 1:
                    hold(pe, cT_out, n.val(), ticks)
                for t in range(CH):
                    ins = pe.transpose(pt[:, t * TOK:(t + 1) * TOK], cin[:, m.slot(2), :, CH * c + t], idn[0:TOK, 0:TOK])
                ins.then_inc(turned, 1)

            def modulator(n, first):
                if first >= 2:
                    hold(pe, biased, n.val(1, -1), ticks)
                pe.wait_ge(cT_out, n.val(1, 1))
                for t in range(CH):
                    ins = pe.matmul(pm[0:TOK, n.slot(2), t * C:(t + 1) * C], cT[:, n.slot(2), t * TOK:(t + 1) * TOK], wh[:],
                                    start=True, stop=True)
                ins.then_inc(modulated, 1)

            def turn_y(n, first):
                hold(pe, y_normed, n.val(1, 1), ticks)
                if first >= 1:
                    hold(pe, yT_out, n.val(), ticks)
                for t in range(CH):
                    ins = pe.transpose(pu[:, t * TOK:(t + 1) * TOK], yn[:, n.slot(2), t, :], idn[0:TOK, 0:TOK])
                ins.then_inc(y_turned, 1)

            def project(n, first):
                if first >= 2:
                    hold(pe, x3_made, n.val(1, -1), ticks)
                pe.wait_ge(yT_out, n.val(1, 1))
                for t in range(CH):
                    ins = pe.matmul(pz[0:TOK, n.slot(2), t * C:(t + 1) * C], yT[:, n.slot(2), t * TOK:(t + 1) * TOK], wpg[:],
                                    start=True, stop=True)
                ins.then_inc(projected, 1)

            def gram_of(n, first, last):
                pe.wait_ge(z_normed, n.val(1, 1))
                for t in range(CH):
                    ins = pe.matmul(pg[:, 0:C + 1], z[:, n.slot(2), t, 0:C], z[:, n.slot(2), t, :],
                                    start=(first == 0 and t == 0), stop=(last == -1 and t == CH - 1))
                ins.then_inc(gram_added, 1)

            def step(n, first, last):
                if first == 0:
                    for k in range(3):
                        turn_context(n + k, k)
                        modulator(n + k, k)
                    turn_y(n, 0)
                    project(n, 0)
                if last < -3:
                    turn_context(n + 3, first + 3)
                if last < -1:
                    turn_y(n + 1, first + 1)
                if last < -3:
                    modulator(n + 3, first + 3)
                if last < -1:
                    project(n + 1, first + 1)
                if first >= 2:
                    gram_of(n - 2, first - 2, last - 2)
                if last == -1:
                    gram_of(n - 1, first - 1, last - 1)
                    gram_of(n, first, last)

            run_steps(pe, N, U, step, AHEAD)


def recurrent_stage(nc, B, x3, gram, W, w_t, v_t, gamma, beta, ident, out):
    TC = 16
    N = PIX // TC
    COLS_ = TC * B
    SUB = 4
    TT = TC // SUB
    ROWS = TT * B
    EPS, EPS_T = 1e-5, 1e-5
    COUNT = float(B * PIX)
    U = 4
    S = Stage(nc, "rec")
    with S.ctx:
        idn = S.sb("idn", [P, P])
        wnat = S.sb("wnat", [C, C])
        wsc = S.sb("wsc", [C, C])
        wt = S.sb("wt", [C, C])
        vt = S.sb("vt", [C, C])
        gr = S.sb("gr", [C, C + 1])
        ones = S.sb("ones", [C, 1])
        gcol, bcol = S.sb("gcol", [C, 1]), S.sb("bcol", [C, 1])
        prod = S.sb("prod", [C, C])
        wbn = S.sb("wbn", [C, C])
        cols = S.sb("cols", [C, 8])
        halfneg = S.sb("halfneg", [P, SUB])
        xin = S.sb("xin", [ROWS, 4, SUB, C])
        stat = S.sb("stat", [ROWS, SUB, 6])
        mv = S.sb("mv", [ROWS, 2, SUB, 2])
        rstd = S.sb("rstd", [ROWS, 2, SUB])
        xn = S.sb("xn", [ROWS, 2, SUB, C])
        xT = S.sb("xT", [C, 2, COLS_])
        yT = S.sb("yT", [C, 2, COLS_])
        res = S.sb("res", [ROWS, 2, SUB, C])
        y0 = S.sb("y0", [C, B])

        pin = S.ps("pin", [P, BANK])
        pout = S.ps("pout", [P, BANK])
        ph = S.ps("ph", [P, 2, BANK])
        ps = S.ps("ps", [P, BANK])

        ticks = S.sem("ticks")
        const_in, filled, setup = S.sem("const_in"), S.sem("filled"), S.sem("setup")
        setup_pe, setup_pool = S.sem("setup_pe"), S.sem("setup_pool")
        x_in = S.sems("x_in", 4)
        stats_part, stats, eps_added, rstd_done, normed = (S.sem(k) for k in ("stats_part", "stats", "eps_added", "rstd_done", "normed"))
        turned, xT_out = S.sem("turned"), S.sem("xT_out")
        driven, shifted = S.sem("driven"), S.sem("shifted")
        added, moved = S.sem("added"), S.sem("moved")
        y_turned, res_made = S.sem("y_turned"), S.sem("res_made")
        stored = S.sems("stored", 2)
        block = S.block()
        CONSTS = 16 * 7

        @block.sync
        def _(sp):
            for dst, src in ((idn[:], ident), (wnat[:], W), (wt[:], w_t), (vt[:], v_t), (gr[:], gram),
                             (gcol[:], dram(gamma, 0, [(1, C), (1, 1)])), (bcol[:], dram(beta, 0, [(1, C), (1, 1)]))):
                sp.dma_start(dst, src).then_inc(const_in, 16)

            def move(tensor, n, tile, sub, sem):
                view = dram(tensor, n.val(TC * C, sub * TT * C), [(C, TT), (PIX * C, B), (1, C)])
                return (sp.dma_start(tile, view) if tensor is x3 else sp.dma_start(view, tile)).then_inc(sem, 16)

            def load(n):
                for sub in range(SUB):
                    move(x3, n, xin[:, n.slot(4), sub, :], sub, x_in[n.slot(4)])

            def step(n, first, last):
                if first == 0:
                    for k in range(3):
                        load(n + k)
                if last < -3:
                    if first >= 1:
                        hold(sp, res_made, n.val(), ticks)
                    load(n + 3)
                hold(sp, res_made, n.val(1, 1), ticks)
                for sub in range(SUB):
                    move(out, n, res[:, n.slot(2), sub, :], sub, stored[n.slot(2)])

            run_steps(sp, N, U, step)
            for s in range(2):
                sp.wait_ge(stored[s], 16 * SUB * (N // 2))

        @block.gpsimd
        def _(pool):
            pool.memset(halfneg[:], -0.5).then_inc(filled, 1)
            pool.memset(ones[:], 1.0).then_inc(filled, 1)
            pool.memset(y0[:], 0.0).then_inc(filled, 1)
            pool.wait_ge(filled, 3)
            pool.wait_ge(setup, 5)
            pool.tensor_tensor(cols[:, 4:5], cols[:, 3:4], halfneg[:, 0:1], ALU.pow).then_inc(setup_pool, 1)

            def norm(n):
                a = n.slot(2)
                hold(pool, stats, n.val(1, 1), ticks)
                pool.tensor_scalar(rstd[:, a, :], mv[:, a, :, 1], EPS_T, None, ALU.add).then_inc(eps_added, 1)
                pool.wait_ge(eps_added, n.val(1, 1))
                pool.tensor_tensor(rstd[:, a, :], rstd[:, a, :], halfneg[0:ROWS, :], ALU.pow).then_inc(rstd_done, 1)
                hold(pool, rstd_done, n.val(1, 1), ticks)
                for t in range(SUB):
                    ins = pool.tensor_scalar(xn[:, a, t, :], xin[:, n.slot(4), t, :], mv[:, a, t, 0:1],
                                             rstd[:, a, t:t + 1], ALU.subtract, ALU.mult)
                ins.then_inc(normed, 1)

            def step(n, first, last):
                if first == 0:
                    norm(n)
                    norm(n + 1)
                if last < -2:
                    pool.wait_ge(turned, n.val(1, 1))
                    norm(n + 2)

            run_steps(pool, N, U, step)

        @block.scalar
        def _(act):

            def step(n, first, last):
                a = n.slot(2)
                for t in range(TC):
                    cs = slice(t * B, (t + 1) * B)
                    if t == 0 and first >= 2:
                        act.wait_ge(y_turned, n.val(1, -1))
                        act.sem_inc(ticks, 1)
                    act.wait_ge(added, n.val(TC, t + 1))
                    act.activation(yT[:, a, cs], ph[:, a, cs], ACT.Sigmoid).then_inc(moved, 1)

            run_steps(act, N, U, step)

        @block.vector
        def _(dve):
            dve.wait_ge(const_in, CONSTS)
            done = [0]

            def then(ins):
                ins.then_inc(setup, 1)
                done[0] += 1
                dve.wait_ge(setup, done[0])

            dve.wait_ge(setup_pe, 1)
            then(dve.tensor_tensor(prod[:], ps[:, 0:C], wt[:], ALU.mult))
            dve.wait_ge(setup_pe, 3)
            then(dve.tensor_scalar(cols[:, 0:2], ps[:, C:C + 2], 1.0 / COUNT, None, ALU.mult))
            then(dve.tensor_tensor(cols[:, 2:3], cols[:, 0:1], cols[:, 0:1], ALU.mult))
            then(dve.tensor_tensor(cols[:, 3:4], cols[:, 1:2], cols[:, 2:3], ALU.subtract))
            then(dve.tensor_scalar(cols[:, 3:4], cols[:, 3:4], EPS, None, ALU.add))
            dve.wait_ge(setup_pool, 1)
            then(dve.tensor_tensor(cols[:, 5:6], cols[:, 4:5], gcol[:], ALU.mult))
            then(dve.tensor_tensor(cols[:, 6:7], cols[:, 5:6], cols[:, 0:1], ALU.mult))
            then(dve.tensor_tensor(cols[:, 7:8], bcol[:], cols[:, 6:7], ALU.subtract))
            then(dve.tensor_scalar(wsc[:], wnat[:], cols[:, 5:6], None, ALU.mult))
            dve.wait_ge(setup_pe, 4)
            then(dve.tensor_copy(wbn[:], ps[:, 128:256]))

            def layer_stats(n):
                a, s = n.slot(2), n.slot(4)
                dve.wait_ge(x_in[s], n.turn(4, 16 * SUB, 16 * SUB))
                for t in range(SUB):
                    dve.bn_stats(stat[:, t, :], xin[:, s, t, :]).then_inc(stats_part, 1)
                hold(dve, stats_part, n.val(SUB, SUB), ticks)
                for t in range(SUB):
                    ins = dve.bn_aggr(mv[:, a, t, :], stat[:, t, :])
                ins.then_inc(stats, 1)

            def drive(n):
                dve.wait_ge(turned, n.val(1, 1))
                dve.tensor_copy(xT[:, n.slot(2), :], pin[:, 0:COLS_]).then_inc(xT_out, 1)

            def shift(n):
                dve.wait_ge(driven, n.val(1, 1))
                a = n.slot(2)
                dve.tensor_scalar(ph[:, a, 0:COLS_], ph[:, a, 0:COLS_], cols[:, 7:8], None, ALU.add).then_inc(shifted, 1)

            def finish(n, first):
                if first >= 2:
                    dve.wait_ge(stored[n.slot(2)], n.turn(2, 16 * SUB))
                    dve.sem_inc(ticks, 1)
                dve.wait_ge(y_turned, n.val(1, 1))
                dve.tensor_tensor(res[:, n.slot(2), :, :], pout[0:ROWS, :].rearrange("p (s c) -> p s c", c=C),
                                  xin[:, n.slot(4), :, :], ALU.add).then_inc(res_made, 1)

            def step(n, first, last):
                if first == 0:
                    layer_stats(n)
                    dve.wait_ge(stats, n.val(1, 1))
                    layer_stats(n + 1)
                    drive(n)
                    shift(n)
                if last < -2:
                    hold(dve, normed, n.val(1, 1), ticks)
                    dve.wait_ge(stats, n.val(1, 2))
                    layer_stats(n + 2)
                if first >= 1:
                    finish(n - 1, first - 1)
                if last < -1:
                    drive(n + 1)
                    shift(n + 1)
                if last == -1:
                    finish(n, first)

            run_steps(dve, N, U, step)

        @block.tensor
        def _(pe):
            pe.wait_ge(const_in, CONSTS)
            pe.matmul(ps[:, 0:C], gr[:, 0:C], wt[:], start=True, stop=True).then_inc(setup_pe, 1)
            pe.wait_ge(filled, 3)
            pe.wait_ge(setup, 1)
            pe.matmul(ps[:, C:C + 1], wt[:], gr[:, C:C + 1], start=True, stop=True).then_inc(setup_pe, 1)
            pe.matmul(ps[:, C + 1:C + 2], prod[:], ones[:], start=True, stop=True).then_inc(setup_pe, 1)
            pe.wait_ge(setup, 9)
            pe.transpose(ps[:, 128:256], wsc[:], idn[:]).then_inc(setup_pe, 1)

            def turn_in(n, sub):
                if sub == 0:
                    pe.wait_ge(normed, n.val(1, 1))
                ins = pe.transpose(pin[:, sub * ROWS:(sub + 1) * ROWS], xn[:, n.slot(2), sub, :], idn[0:ROWS, 0:ROWS])
                if sub == SUB - 1:
                    ins.then_inc(turned, 1)

            def drive(n, sub):
                if sub == 0:
                    pe.wait_ge(xT_out, n.val(1, 1))
                ins = pe.matmul(ph[:, n.slot(2), sub * ROWS:(sub + 1) * ROWS], wbn[:],
                                xT[:, n.slot(2), sub * ROWS:(sub + 1) * ROWS], start=(sub == 0), stop=False,
                                skip_group_check=True)
                if sub == SUB - 1:
                    ins.then_inc(driven, 1)

            def turn_out(n, sub, first):
                if sub == 0 and first >= 1:
                    pe.wait_ge(res_made, n.val())
                ins = pe.transpose(pout[0:ROWS, sub * C:(sub + 1) * C], yT[:, n.slot(2), sub * ROWS:(sub + 1) * ROWS], idn[:])
                if sub == SUB - 1:
                    ins.then_inc(y_turned, 1)

            pe.wait_ge(setup, 10)

            def add(n, cs, before):
                for r in range(0, C, 32):
                    ins = pe.matmul(ph[r:r + 32, n.slot(2), cs], vt[:, r:r + 32], before, start=False, stop=True,
                                    skip_group_check=True)
                ins.then_inc(added, 1)

            def step(n, first, last):
                a = n.slot(2)
                if first == 0:
                    for sub in range(SUB):
                        turn_in(n, sub)
                    for sub in range(SUB):
                        drive(n, sub)
                hold(pe, shifted, n.val(1, 1), ticks)
                for t in range(TC):
                    cs = slice(t * B, (t + 1) * B)
                    if t == 0 and first == 0:
                        add(n, cs, y0[:])
                    else:
                        before = yT[:, a, (t - 1) * B:t * B] if t else yT[:, 1 - a, (TC - 1) * B:TC * B]
                        pe.wait_ge(moved, n.val(TC, t))
                        add(n, cs, before)
                    if t < SUB and first >= 1:
                        turn_out(n - 1, t, first - 1)
                    if SUB <= t < 2 * SUB and last < -1:
                        turn_in(n + 1, t - SUB)
                    if TC - 7 <= t < TC - 3 and last < -1:
                        drive(n + 1, t - (TC - 7))
                if last == -1:
                    pe.wait_ge(moved, n.val(TC, TC))
                    for sub in range(SUB):
                        turn_out(n, sub, first)

            run_steps(pe, N, U, step)


def metaformer_program(nc, B, a):
    def scratch(name, *shape):
        return nc.dram_tensor(name, shape, F32).ap()

    x1 = scratch("x1", B * PIX, C)
    x2 = scratch("x2", B * PIX, C)
    x3 = scratch("x3", B * PIX, C)
    q = scratch("q", B * PIX, C)
    c0 = scratch("c0", GROUPS, P, B, ODD, QUAD)
    gates = scratch("gates", P, 4, B, EVEN)
    ctx_all = scratch("ctx_all", GROUPS, P, B, QUAD, EVEN)
    gram = scratch("gram", C, C + 1)
    attention_stage(nc, B, a["x_windows"], a["w_qkv_t"], a["w_proj_t"], a["b_proj"], a["rpb_rev"],
                    a["shift_mask"], a["ident"], x1)
    expert_stage(nc, B, x1, a["router_w"], a["router_b"], a["expert_w"], a["expert_b"], a["erank"], a["ident"], x2)
    focal_input_stage(nc, B, x2, a["Wf"], a["bf"], a["edge_mask"], a["ident"], q, c0, gates)
    convolution_stage(nc, B, c0, gates, [a["k0"], a["k1"], a["k2"]], a["gap_mask"], ctx_all)
    focal_output_stage(nc, B, ctx_all, q, x2, a["Wh"], a["bh"], a["gamma"], a["beta"], a["Wp"], a["bp"],
                       a["ident"], x3, gram)
    recurrent_stage(nc, B, x3, gram, a["ffn_W"], a["ffn_w_t"], a["ffn_v_t"], a["ffn_gamma"], a["ffn_beta"],
                    a["ident"], a["out"])


def _shape_constants(np):
    tok = np.arange(WTOK)
    row, col = tok // WS, tok % WS
    shift = np.zeros((P, 2, 4, WTOK), np.float32)
    for last_band in range(2):
        for w in range(8):
            part = (row >= WS - SHIFT) * last_band * 2 + (col >= WS - SHIFT) * (w == 7)
            p0 = (w % 2) * 64
            shift[p0:p0 + WTOK, last_band, w // 2] = np.where(part[:, None] != part[None, :], -100.0, 0.0)
    p = np.arange(P)
    pixel = p % ROW < IMG
    edge = np.stack([pixel & (p >= ROW), pixel, pixel, pixel & (p < ROW)], 1).astype(np.float32)
    return {
        "ident": np.eye(P, dtype=np.float32),
        "shift_mask": shift.reshape(P, 2, 4 * WTOK),
        "edge_mask": edge,
        "gap_mask": pixel.astype(np.float32)[:, None],
        "erank": np.tile(np.arange(EXPERTS, 0, -1).astype(np.float32), (P, 1)),
    }


def kernel(**inputs):
    import numpy as np
    import concourse.bacc as bacc
    from concourse.bass_utils import run_bass_kernel_spmd as run

    i = {k: np.asarray(v) for k, v in inputs.items()}
    x = i["x"]
    B = x.shape[0]
    rolled = np.roll(x, (-SHIFT, -SHIFT), (1, 2))
    windows = rolled.reshape(B, 8, WS, 8, WS, C).transpose(0, 1, 3, 2, 4, 5).reshape(B * 64, WTOK, C)
    arrays = {
        "x_windows": windows,
        "w_qkv_t": i["L0_conv_w_qkv"].T,
        "w_proj_t": i["L0_conv_w_proj"].T,
        "b_proj": i["L0_conv_b_proj"],
        "rpb_rev": i["L0_conv_rpb_table"][::-1].T,
        "router_w": i["L0_ffn_router_w"],
        "router_b": i["L0_ffn_router_b"],
        "expert_w": i["L0_ffn_expert_w"],
        "expert_b": i["L0_ffn_expert_b"],
        "Wf": i["L1_conv_Wf"],
        "bf": i["L1_conv_bf"],
        "Wh": i["L1_conv_Wh"],
        "bh": i["L1_conv_bh"],
        "gamma": i["L1_conv_gamma"],
        "beta": i["L1_conv_beta"],
        "Wp": i["L1_conv_Wp"],
        "bp": i["L1_conv_bp"],
        "ffn_W": i["L1_ffn_W"],
        "ffn_w_t": i["L1_ffn_W"].T,
        "ffn_v_t": i["L1_ffn_V"].T,
        "ffn_gamma": i["L1_ffn_gamma"],
        "ffn_beta": i["L1_ffn_beta"],
        **_shape_constants(np),
    }
    for k, size in enumerate(TAPS):
        taps = i[f"L1_conv_k{k}"].reshape(size, size, C)
        arrays[f"k{k}"] = taps[::-1, ::-1].transpose(2, 0, 1)
    arrays = {k: np.ascontiguousarray(v) for k, v in arrays.items()}

    nc = bacc.Bacc("TRN2", target_bir_lowering=False, num_devices=1)
    args = {k: nc.dram_tensor(k, v.shape, F32, kind="ExternalInput").ap() for k, v in arrays.items()}
    args["out"] = nc.dram_tensor("out", (B, IMG, IMG, C), F32, kind="ExternalOutput").ap()
    metaformer_program(nc, B, args)
    return run(nc, [arrays], core_ids=[0]).results[0]["out"]
```
